# Optimizing a Trainium2 kernel written in Bass

```python
import numpy as np
import jax
import jax.numpy as jnp

def _softmax(x, axis=-1):
    return jax.nn.softmax(x, axis=axis)

def _gelu(x):
    return jax.nn.gelu(x, approximate=True)

def _silu(x):
    return jax.nn.silu(x)

def _sigmoid(x):
    return jax.nn.sigmoid(x)

def _layernorm(x, axis=-1, eps=1e-05):
    m = jnp.mean(x, axis=axis, keepdims=True)
    v = jnp.var(x, axis=axis, keepdims=True)
    return (x - m) / jnp.sqrt(v + eps)

def _scatter_add(tgt, idx, src, axis=0):
    return tgt.at[idx].add(src)

def _segment_sum(src, seg, n):
    return jax.ops.segment_sum(src, seg, n)
kernel_name = 'mk_cond_seq_d4_seqx_r4_8f9d6b'

def setup_inputs(seed: int=0):
    np.random.seed(seed)
    _w = jnp.asarray

    def _rec_inputs():
        import jax
        import jax.numpy as jnp
        _rk = jax.random.key(seed)
        x = -0.0003482 + 1 * jax.random.normal(jax.random.fold_in(_rk, 1), (4, 512, 288), jnp.float32)
        _lenS = 512 - jax.random.randint(jax.random.fold_in(_rk, 7), (4,), 0, max(1, 512 // 4) + 1, jnp.int32)
        _lenS2 = 512 - jax.random.randint(jax.random.fold_in(_rk, 8), (4,), 0, max(1, 512 // 4) + 1, jnp.int32)
        cond_1152 = 0.00257642 + 1.0011 * jax.random.normal(jax.random.fold_in(_rk, 11), (4, 288), jnp.float32)
        return (x, cond_1152)
    x, cond_1152 = _rec_inputs()

    def _L0_cond_setup():
        import jax, jax.numpy as jnp
        import numpy as np
        from jax.scipy.linalg import expm
        N, D, COND_DIM = (288, 64, 288)
        B, T = (16, 256)

        def _rotation(cond, W, b):
            v = jax.nn.silu(cond) @ W.T + b
            iu, ju = jnp.triu_indices(D, k=1)
            A = jnp.zeros((cond.shape[0], D, D), dtype=v.dtype)
            A = A.at[:, iu, ju].set(v).at[:, ju, iu].set(-v)
            return expm(A)
        key = jax.random.key(seed)
        k1, k2, k3, k4, k5 = jax.random.split(key, 5)
        x = jax.random.normal(k1, (B, T, N), dtype=jnp.float32)
        cond = jax.random.normal(k2, (B, COND_DIM), dtype=jnp.float32)
        P = jax.random.normal(k3, (N, D), dtype=jnp.float32)
        n_skew = D * (D - 1) // 2
        bound = 1.0 / np.sqrt(COND_DIM)
        W = jax.random.uniform(k4, (n_skew, COND_DIM), minval=-bound, maxval=bound, dtype=jnp.float32)
        b = jax.random.uniform(k5, (n_skew,), minval=-bound, maxval=bound, dtype=jnp.float32)
        return {'x': x, 'cond': cond, 'P': P, 'W': W, 'b': b}
    _L0_cond_all = _L0_cond_setup()
    _L0_cond_in = {k: v for k, v in _L0_cond_all.items() if k in ('P', 'W', 'b')}
    del _L0_cond_all

    def _L1_cond_setup():
        import jax, jax.numpy as jnp
        import numpy as np
        B, L, C = (8, 256, 288)
        H = 16
        D = C // H
        FF = int(C * 4.0)
        EPS = 1e-06

        def _layernorm(x):
            mu = jnp.mean(x, axis=-1, keepdims=True)
            var = jnp.mean(jnp.square(x - mu), axis=-1, keepdims=True)
            return (x - mu) * jax.lax.rsqrt(var + EPS)

        def _modulate(x, shift, scale):
            return x * (1.0 + scale) + shift

        def _attention(h, W_qkv, b_qkv, W_proj, b_proj):
            b, l, c = h.shape
            qkv = h @ W_qkv + b_qkv
            qkv = qkv.reshape(b, l, 3, H, D)
            q, k, v = (qkv[:, :, 0], qkv[:, :, 1], qkv[:, :, 2])
            scale = D ** (-0.5)
            scores = jnp.einsum('blhd,bmhd->bhlm', q * scale, k)
            attn = jax.nn.softmax(scores, axis=-1)
            o = jnp.einsum('bhlm,bmhd->blhd', attn, v).reshape(b, l, c)
            return o @ W_proj + b_proj
        key = jax.random.key(seed)
        ks = jax.random.split(key, 12)
        s = 0.02
        return {'x': jax.random.normal(ks[0], (B, L, C), jnp.float32), 'c': jax.random.normal(ks[1], (B, 1, C), jnp.float32), 'W_qkv': jax.random.normal(ks[2], (C, 3 * C), jnp.float32) * s, 'b_qkv': jnp.zeros((3 * C,), jnp.float32), 'W_proj': jax.random.normal(ks[3], (C, C), jnp.float32) * s, 'b_proj': jnp.zeros((C,), jnp.float32), 'W_fc1': jax.random.normal(ks[4], (C, FF), jnp.float32) * s, 'b_fc1': jnp.zeros((FF,), jnp.float32), 'W_fc2': jax.random.normal(ks[5], (FF, C), jnp.float32) * s, 'b_fc2': jnp.zeros((C,), jnp.float32), 'W_ada': jax.random.normal(ks[6], (C, 6 * C), jnp.float32) * s, 'b_ada': jnp.zeros((6 * C,), jnp.float32)}
    _L1_cond_all = _L1_cond_setup()
    _L1_cond_in = {k: v for k, v in _L1_cond_all.items() if k in ('W_qkv', 'b_qkv', 'W_proj', 'b_proj', 'W_fc1', 'b_fc1', 'W_fc2', 'b_fc2', 'W_ada', 'b_ada')}
    del _L1_cond_all

    def _L2_cond_setup():
        import jax, jax.numpy as jnp
        import numpy as np
        NUM_HEADS = 16
        NUM_EXPERTS = 4
        TOP_K = 2
        LN_EPS = 1e-06

        def _ln(h):
            mu = jnp.mean(h, axis=-1, keepdims=True)
            var = jnp.var(h, axis=-1, keepdims=True)
            return (h - mu) * jax.lax.rsqrt(var + LN_EPS)

        def _modulate(h, shift, scale):
            return h * (1.0 + scale[:, None, :]) + shift[:, None, :]
        key = jax.random.key(seed)
        ks = jax.random.split(key, 12)
        B, N, C = (8, 256, 288)
        H = 4 * C
        E = NUM_EXPERTS
        s = 0.02
        return {'x': jax.random.normal(ks[0], (B, N, C), jnp.float32), 'c': jax.random.normal(ks[1], (B, C), jnp.float32), 'w_adaln': jax.random.normal(ks[2], (C, 6 * C), jnp.float32) * s, 'b_adaln': jnp.zeros((6 * C,), jnp.float32), 'w_qkv': jax.random.normal(ks[3], (C, 3 * C), jnp.float32) * s, 'b_qkv': jnp.zeros((3 * C,), jnp.float32), 'w_proj': jax.random.normal(ks[4], (C, C), jnp.float32) * s, 'b_proj': jnp.zeros((C,), jnp.float32), 'w_gate': jax.random.normal(ks[5], (C, E), jnp.float32) * s, 'w1': jax.random.normal(ks[6], (E, C, H), jnp.float32) * s, 'b1': jnp.zeros((E, H), jnp.float32), 'w2': jax.random.normal(ks[7], (E, H, C), jnp.float32) * s, 'b2': jnp.zeros((E, C), jnp.float32)}
    _L2_cond_all = _L2_cond_setup()
    _L2_cond_in = {k: v for k, v in _L2_cond_all.items() if k in ('w_adaln', 'b_adaln', 'w_qkv', 'b_qkv', 'w_proj', 'b_proj', 'w_gate', 'w1', 'b1', 'w2', 'b2')}
    del _L2_cond_all

    def _L3_cond_setup():
        import math
        import jax, jax.numpy as jnp
        import numpy as np
        B, T, D = (8, 256, 288)
        H = 16
        E = 4
        EPS = 1e-06

        def _layer_norm(x):
            mu = jnp.mean(x, axis=-1, keepdims=True)
            var = jnp.mean(jnp.square(x - mu), axis=-1, keepdims=True)
            return (x - mu) * jax.lax.rsqrt(var + EPS)

        def _modulate(x, shift, scale):
            return x * (1.0 + scale) + shift

        def _attention(y, qkv_w, qkv_b, out_w, out_b):
            b, t, d = y.shape
            hd = d // H
            qkv = y @ qkv_w + qkv_b
            q, k, v = jnp.split(qkv, 3, axis=-1)
            q = q.reshape(b, t, H, hd).transpose(0, 2, 1, 3)
            k = k.reshape(b, t, H, hd).transpose(0, 2, 1, 3)
            v = v.reshape(b, t, H, hd).transpose(0, 2, 1, 3)
            scores = jnp.einsum('bhqd,bhkd->bhqk', q, k) / math.sqrt(hd)
            attn = jax.nn.softmax(scores, axis=-1)
            out = jnp.einsum('bhqk,bhkd->bhqd', attn, v)
            out = out.transpose(0, 2, 1, 3).reshape(b, t, d)
            return out @ out_w + out_b
        key = jax.random.key(seed)
        ks = jax.random.split(key, 12)
        std = 0.02
        return {'x': jax.random.normal(ks[0], (B, T, D), dtype=jnp.float32), 'c': jax.random.normal(ks[1], (B, D), dtype=jnp.float32), 'qkv_w': jax.random.normal(ks[2], (D, 3 * D), dtype=jnp.float32) * std, 'qkv_b': jnp.zeros((3 * D,), dtype=jnp.float32), 'out_w': jax.random.normal(ks[3], (D, D), dtype=jnp.float32) * std, 'out_b': jnp.zeros((D,), dtype=jnp.float32), 'w1': jax.random.normal(ks[4], (D, E * D), dtype=jnp.float32) * std, 'b1': jnp.zeros((E * D,), dtype=jnp.float32), 'w2': jax.random.normal(ks[5], (E * D, D), dtype=jnp.float32) * std, 'b2': jnp.zeros((D,), dtype=jnp.float32), 'ada_w': jax.random.normal(ks[6], (D, 6 * D), dtype=jnp.float32) * std, 'ada_b': jnp.zeros((6 * D,), dtype=jnp.float32)}
    _L3_cond_all = _L3_cond_setup()
    _L3_cond_in = {k: v for k, v in _L3_cond_all.items() if k in ('qkv_w', 'qkv_b', 'out_w', 'out_b', 'w1', 'b1', 'w2', 'b2', 'ada_w', 'ada_b')}
    del _L3_cond_all
    return {'x': x, 'cond_1152': cond_1152, 'L0_cond_P': _L0_cond_in['P'], 'L0_cond_W': _L0_cond_in['W'], 'L0_cond_b': _L0_cond_in['b'], 'L1_cond_W_qkv': _L1_cond_in['W_qkv'], 'L1_cond_b_qkv': _L1_cond_in['b_qkv'], 'L1_cond_W_proj': _L1_cond_in['W_proj'], 'L1_cond_b_proj': _L1_cond_in['b_proj'], 'L1_cond_W_fc1': _L1_cond_in['W_fc1'], 'L1_cond_b_fc1': _L1_cond_in['b_fc1'], 'L1_cond_W_fc2': _L1_cond_in['W_fc2'], 'L1_cond_b_fc2': _L1_cond_in['b_fc2'], 'L1_cond_W_ada': _L1_cond_in['W_ada'], 'L1_cond_b_ada': _L1_cond_in['b_ada'], 'L2_cond_w_adaln': _L2_cond_in['w_adaln'], 'L2_cond_b_adaln': _L2_cond_in['b_adaln'], 'L2_cond_w_qkv': _L2_cond_in['w_qkv'], 'L2_cond_b_qkv': _L2_cond_in['b_qkv'], 'L2_cond_w_proj': _L2_cond_in['w_proj'], 'L2_cond_b_proj': _L2_cond_in['b_proj'], 'L2_cond_w_gate': _L2_cond_in['w_gate'], 'L2_cond_w1': _L2_cond_in['w1'], 'L2_cond_b1': _L2_cond_in['b1'], 'L2_cond_w2': _L2_cond_in['w2'], 'L2_cond_b2': _L2_cond_in['b2'], 'L3_cond_qkv_w': _L3_cond_in['qkv_w'], 'L3_cond_qkv_b': _L3_cond_in['qkv_b'], 'L3_cond_out_w': _L3_cond_in['out_w'], 'L3_cond_out_b': _L3_cond_in['out_b'], 'L3_cond_w1': _L3_cond_in['w1'], 'L3_cond_b1': _L3_cond_in['b1'], 'L3_cond_w2': _L3_cond_in['w2'], 'L3_cond_b2': _L3_cond_in['b2'], 'L3_cond_ada_w': _L3_cond_in['ada_w'], 'L3_cond_ada_b': _L3_cond_in['ada_b']}

def reference(x, cond_1152, L0_cond_P, L0_cond_W, L0_cond_b, L1_cond_W_qkv, L1_cond_b_qkv, L1_cond_W_proj, L1_cond_b_proj, L1_cond_W_fc1, L1_cond_b_fc1, L1_cond_W_fc2, L1_cond_b_fc2, L1_cond_W_ada, L1_cond_b_ada, L2_cond_w_adaln, L2_cond_b_adaln, L2_cond_w_qkv, L2_cond_b_qkv, L2_cond_w_proj, L2_cond_b_proj, L2_cond_w_gate, L2_cond_w1, L2_cond_b1, L2_cond_w2, L2_cond_b2, L3_cond_qkv_w, L3_cond_qkv_b, L3_cond_out_w, L3_cond_out_b, L3_cond_w1, L3_cond_b1, L3_cond_w2, L3_cond_b2, L3_cond_ada_w, L3_cond_ada_b):
    import jax
    import jax.numpy as jnp

    def _L0_cond_ref(x, cond, P, W, b):
        import jax, jax.numpy as jnp
        import numpy as np
        from jax.scipy.linalg import expm
        N, D, COND_DIM = (288, 64, 288)
        B, T = (16, 256)

        def _rotation(cond, W, b):
            v = jax.nn.silu(cond) @ W.T + b
            iu, ju = jnp.triu_indices(D, k=1)
            A = jnp.zeros((cond.shape[0], D, D), dtype=v.dtype)
            A = A.at[:, iu, ju].set(v).at[:, ju, iu].set(-v)
            return expm(A)
        U, _ = jnp.linalg.qr(P)
        R = _rotation(cond, W, b)
        z = jnp.einsum('btn,nd->btd', x, U)
        z_rot = jnp.einsum('btd,bde->bte', z, R)
        x_rot = x + jnp.einsum('btd,nd->btn', z_rot - z, U)
        return x_rot

    def _L1_cond_ref(x, c, W_qkv, b_qkv, W_proj, b_proj, W_fc1, b_fc1, W_fc2, b_fc2, W_ada, b_ada):
        import jax, jax.numpy as jnp
        import numpy as np
        B, L, C = (8, 256, 288)
        H = 16
        D = C // H
        FF = int(C * 4.0)
        EPS = 1e-06

        def _layernorm(x):
            mu = jnp.mean(x, axis=-1, keepdims=True)
            var = jnp.mean(jnp.square(x - mu), axis=-1, keepdims=True)
            return (x - mu) * jax.lax.rsqrt(var + EPS)

        def _modulate(x, shift, scale):
            return x * (1.0 + scale) + shift

        def _attention(h, W_qkv, b_qkv, W_proj, b_proj):
            b, l, c = h.shape
            qkv = h @ W_qkv + b_qkv
            qkv = qkv.reshape(b, l, 3, H, D)
            q, k, v = (qkv[:, :, 0], qkv[:, :, 1], qkv[:, :, 2])
            scale = D ** (-0.5)
            scores = jnp.einsum('blhd,bmhd->bhlm', q * scale, k)
            attn = jax.nn.softmax(scores, axis=-1)
            o = jnp.einsum('bhlm,bmhd->blhd', attn, v).reshape(b, l, c)
            return o @ W_proj + b_proj
        ada = jax.nn.silu(c) @ W_ada + b_ada
        shift_msa, scale_msa, gate_msa, shift_mlp, scale_mlp, gate_mlp = jnp.split(ada, 6, axis=-1)
        h = _modulate(_layernorm(x), shift_msa, scale_msa)
        x = x + gate_msa * _attention(h, W_qkv, b_qkv, W_proj, b_proj)
        h = _modulate(_layernorm(x), shift_mlp, scale_mlp)
        mlp = jax.nn.gelu(h @ W_fc1 + b_fc1, approximate=True) @ W_fc2 + b_fc2
        x = x + gate_mlp * mlp
        return x

    def _L2_cond_ref(x, c, w_adaln, b_adaln, w_qkv, b_qkv, w_proj, b_proj, w_gate, w1, b1, w2, b2):
        import jax, jax.numpy as jnp
        import numpy as np
        NUM_HEADS = 16
        NUM_EXPERTS = 4
        TOP_K = 2
        LN_EPS = 1e-06

        def _ln(h):
            mu = jnp.mean(h, axis=-1, keepdims=True)
            var = jnp.var(h, axis=-1, keepdims=True)
            return (h - mu) * jax.lax.rsqrt(var + LN_EPS)

        def _modulate(h, shift, scale):
            return h * (1.0 + scale[:, None, :]) + shift[:, None, :]
        B, N, C = x.shape
        nh = NUM_HEADS
        hd = C // nh
        mod = jax.nn.silu(c) @ w_adaln + b_adaln
        sh_msa, sc_msa, g_msa, sh_mlp, sc_mlp, g_mlp = jnp.split(mod, 6, axis=-1)
        h = _modulate(_ln(x), sh_msa, sc_msa)
        qkv = (h @ w_qkv + b_qkv).reshape(B, N, 3, nh, hd).transpose(2, 0, 3, 1, 4)
        q, k, v = (qkv[0], qkv[1], qkv[2])
        attn = jax.nn.softmax(jnp.einsum('bhqd,bhkd->bhqk', q, k) * hd ** (-0.5), axis=-1)
        o = jnp.einsum('bhqk,bhkd->bhqd', attn, v).transpose(0, 2, 1, 3).reshape(B, N, C)
        o = o @ w_proj + b_proj
        x = x + g_msa[:, None, :] * o
        xn = _modulate(_ln(x), sh_mlp, sc_mlp)
        xf = xn.reshape(-1, C)
        gate_logits = xf @ w_gate
        topk_logits, topk_idx = jax.lax.top_k(gate_logits, TOP_K)
        gates = jax.nn.softmax(topk_logits, axis=-1)
        cw = jnp.sum(jax.nn.one_hot(topk_idx, NUM_EXPERTS, dtype=xf.dtype) * gates[..., None], axis=1)
        hmid = jax.nn.gelu(jnp.einsum('tc,ech->eth', xf, w1) + b1[:, None, :], approximate=True)
        eo = jnp.einsum('eth,ehc->etc', hmid, w2) + b2[:, None, :]
        moe = jnp.einsum('te,etc->tc', cw, eo).reshape(B, N, C)
        return x + g_mlp[:, None, :] * moe

    def _L3_cond_ref(x, c, qkv_w, qkv_b, out_w, out_b, w1, b1, w2, b2, ada_w, ada_b):
        import math
        import jax, jax.numpy as jnp
        import numpy as np
        B, T, D = (8, 256, 288)
        H = 16
        E = 4
        EPS = 1e-06

        def _layer_norm(x):
            mu = jnp.mean(x, axis=-1, keepdims=True)
            var = jnp.mean(jnp.square(x - mu), axis=-1, keepdims=True)
            return (x - mu) * jax.lax.rsqrt(var + EPS)

        def _modulate(x, shift, scale):
            return x * (1.0 + scale) + shift

        def _attention(y, qkv_w, qkv_b, out_w, out_b):
            b, t, d = y.shape
            hd = d // H
            qkv = y @ qkv_w + qkv_b
            q, k, v = jnp.split(qkv, 3, axis=-1)
            q = q.reshape(b, t, H, hd).transpose(0, 2, 1, 3)
            k = k.reshape(b, t, H, hd).transpose(0, 2, 1, 3)
            v = v.reshape(b, t, H, hd).transpose(0, 2, 1, 3)
            scores = jnp.einsum('bhqd,bhkd->bhqk', q, k) / math.sqrt(hd)
            attn = jax.nn.softmax(scores, axis=-1)
            out = jnp.einsum('bhqk,bhkd->bhqd', attn, v)
            out = out.transpose(0, 2, 1, 3).reshape(b, t, d)
            return out @ out_w + out_b
        mods = (jax.nn.silu(c) @ ada_w + ada_b)[:, None, :]
        m0, m1, m2, m3, m4, m5 = jnp.split(mods, 6, axis=-1)
        y = _modulate(_layer_norm(x), m0, m1)
        x = x + m2 * _attention(y, qkv_w, qkv_b, out_w, out_b)
        y = _modulate(_layer_norm(x), m3, m4)
        y = jax.nn.gelu(y @ w1 + b1, approximate=True)
        x = x + m5 * (y @ w2 + b2)
        return x
    x = _L0_cond_ref(x, cond_1152, L0_cond_P, L0_cond_W, L0_cond_b)
    x = _L1_cond_ref(x, cond_1152[:, None, :], L1_cond_W_qkv, L1_cond_b_qkv, L1_cond_W_proj, L1_cond_b_proj, L1_cond_W_fc1, L1_cond_b_fc1, L1_cond_W_fc2, L1_cond_b_fc2, L1_cond_W_ada, L1_cond_b_ada)
    x = _L2_cond_ref(x, cond_1152, L2_cond_w_adaln, L2_cond_b_adaln, L2_cond_w_qkv, L2_cond_b_qkv, L2_cond_w_proj, L2_cond_b_proj, L2_cond_w_gate, L2_cond_w1, L2_cond_b1, L2_cond_w2, L2_cond_b2)
    x = _L3_cond_ref(x, cond_1152, L3_cond_qkv_w, L3_cond_qkv_b, L3_cond_out_w, L3_cond_out_b, L3_cond_w1, L3_cond_b1, L3_cond_w2, L3_cond_b2, L3_cond_ada_w, L3_cond_ada_b)
    return x

_drawn_inputs = setup_inputs


def setup_inputs(seed=0):
    import zlib

    import numpy as np

    out = dict(_drawn_inputs(seed))
    spreads = {'L1_cond_b_qkv': (0.0, 0.8),
     'L1_cond_b_proj': (0.0, 0.336),
     'L1_cond_b_fc1': (0.0, 0.8),
     'L1_cond_b_fc2': (0.0, 0.355),
     'L1_cond_b_ada': (0.0, 0.373),
     'L2_cond_b_adaln': (0.0, 0.444),
     'L2_cond_b_qkv': (0.0, 0.8),
     'L2_cond_b_proj': (0.0, 0.344),
     'L2_cond_b1': (0.0, 0.8),
     'L2_cond_b2': (0.0, 0.484),
     'L3_cond_qkv_b': (0.0, 0.8),
     'L3_cond_out_b': (0.0, 0.405),
     'L3_cond_b1': (0.0, 0.8),
     'L3_cond_b2': (0.0, 0.35),
     'L3_cond_ada_b': (0.0, 0.384)}
    factors = {'L1_cond_W_qkv': 8.0,
     'L1_cond_W_proj': 5.432,
     'L2_cond_w_qkv': 8.0,
     'L2_cond_w_proj': 5.588,
     'L2_cond_w_gate': 2.798,
     'L2_cond_w1': 2.729,
     'L3_cond_qkv_w': 8.0,
     'L3_cond_out_w': 5.949,
     'L3_cond_w1': 3.496}
    for name, (base, spread) in spreads.items():
        noise = np.random.default_rng([zlib.crc32(name.encode()), seed]).standard_normal(out[name].shape)
        drawn = base * np.exp(spread * noise) if base else spread * noise
        out[name] = jnp.asarray(drawn.astype(out[name].dtype))
    for name, factor in factors.items():
        out[name] = (out[name] * factor).astype(out[name].dtype)
    return out
```

```python
from contextlib import ExitStack

import concourse.bass as bass
from concourse import mybir

F32 = mybir.dt.float32
F16 = mybir.dt.float16
BF16 = mybir.dt.bfloat16
ALU = mybir.AluOpType
ACT = mybir.ActivationFunctionType
AX_X = mybir.AxisListType.X

B, NTOK, C = 4, 512, 288
NT = NTOK // 128
NK, KC = 3, 96
D0 = 64
NSKEW = D0 * (D0 - 1) // 2
NSQ = 18
TAYLOR = 12
H, D = 16, 18
NL = 3
FF = 4 * C
NF = FF // 128
NE = 4
WS = 256.0
EPS = 1e-6


class Order:

    def __init__(self, eng, sem, start=0):
        self.eng, self.sem, self.n = eng, sem, start

    def __call__(self, ins):
        self.n = self.n + 1
        ins.then_inc(self.sem, 1)
        self.eng.wait_ge(self.sem, self.n)


def prepare_and_rotate(nc, io, T):
    X, ident, mods = T["x"], T["ident"], T["mods"]
    with nc.cleanup_on_exit(), ExitStack() as ctx:
        def sb(name, shape, dt=F32):
            return ctx.enter_context(nc.sbuf_tensor(name, shape, dt))

        def sem(name):
            return nc.alloc_semaphore(name)

        Aw = sb("qr_work", [KC, NK, D0 + 1])
        Vn = sb("qr_vectors", [KC, NK, D0])
        from_row = sb("from_row", [KC, NK, D0 + 1])
        eye3 = sb("eye3", [KC, NK, D0 + 1])
        am = sb("column_masked", [KC, NK])
        ek = sb("unit_column", [KC, NK])
        vt = sb("minus_v", [KC, NK])
        vc = sb("v_times_c", [KC, NK])
        a_cols = sb("column_products", [KC, D0])
        v_cols = sb("vector_products", [KC, D0])
        n2 = sb("norm2_and_alpha", [KC, 2])
        nrm = sb("norm", [KC, 1])
        root = sb("exponent_half", [KC, 1])
        sgn = sb("minus_sign", [KC, 1])
        beta = sb("beta", [KC, 1])
        vv = sb("v_dot_v", [KC, 2])
        chalf = sb("half_c", [KC, 1])
        crow = sb("c_row", [KC, D0])
        cdia = sb("c_diagonal", [D0, D0])
        ccol = sb("c_col", [D0, 1])
        upper = sb("strict_upper", [D0, D0])
        lower = sb("strict_lower", [D0, D0])
        Xn = sb("nilpotent", [D0, 2, 2, D0])
        PT = sb("inverse_transposed", [D0, 2, D0])
        VT = sb("v_transposed", [D0, C])
        Tt = sb("T_transposed", [D0, D0])
        Y = sb("T_v1T", [D0, D0])
        U = sb("u_factor", [KC, NK, D0])
        UT = sb("u_transposed", [D0, C])
        Rm = sb("rotation_T_minus_one", [D0, B, D0])
        F = sb("rotated_minus_same", [D0, B, C])
        cT = sb("cond_T", [KC, NK, B])
        e1 = sb("silu_denominator", [KC, NK, B])
        sT = sb("silu_T", [KC, NK, B])
        Wsk = sb("skew_weights", [KC, NK, NSKEW])
        skb = sb("skew_bias", [B, NSKEW])
        sv = sb("skew_values", [B, NSKEW])
        Up = sb("skew_upper", [D0, B, D0])
        A = sb("skew", [D0, 2, B, D0])
        Ab = sb("skew_abs", [D0, B, D0])
        ones64 = sb("ones64", [D0, D0])
        nrm1 = sb("norm1", [D0, B])
        again = sb("square_again", [D0, NSQ, B])
        halves = sb("halvings", [D0, NSQ, B])
        down = sb("scale_down", [D0, B])
        hor = sb("horner", [D0, 2, B, D0])
        R = sb("rotation", [D0, 2, 2, B, D0])
        dif = sb("squared_minus_same", [D0, 2, B, D0])
        eyeB = sb("eye_batches", [D0, 2, B, D0])
        Wad = sb("ada_weights", [KC, NK, 6 * C])
        bad = sb("ada_bias", [B, 6 * C])
        mrow = sb("mod_rows", [B, 6 * C])
        xs = sb("x_of_batch", [128, NT, C])
        xT = sb("x_transposed", [KC, NK, NTOK])
        zT = sb("z_transposed", [D0, NTOK])
        bank = [ctx.enter_context(nc.psum_tensor(f"bank{i}", [128, 512], F32)) for i in range(8)]
        psq, psr = bank[0], bank[1]

        s_p, s_x, s_c, s_w, s_b = sem("p_in"), sem("x_in"), sem("cond_in"), sem("skew_w_in"), sem("skew_b_in")
        s_ad, s_adb = sem("ada_w_in"), sem("ada_b_in")
        s_clear, s_mask = sem("masks_cleared"), sem("masks_ready")
        s_dve = sem("dve_order")
        s_col, s_prod, s_sc, s_norm = sem("column_ready"), sem("products_ready"), sem("norm2_ready"), sem("norm_ready")
        s_vt, s_kept, s_half = sem("vector_ready"), sem("vector_kept"), sem("half_c_ready")
        s_e1, s_sT = sem("silu_exp_ready"), sem("silu_ready")
        s_skp, s_sv, s_up = sem("skew_products"), sem("skew_values_ready"), sem("skew_moved")
        s_upT, s_n1p = sem("upper_transposed"), sem("norm_products")
        s_abs, s_hp, s_h = sem("abs_ready"), sem("horner_product"), sem("horner_ready")
        s_rT, s_sqp, s_R = sem("r_transposed"), sem("square_products"), sem("squared")
        s_gp, s_X, s_PT = sem("gram_products"), sem("nilpotent_ready"), sem("inverse_ready")
        s_vT, s_xp, s_xr = sem("v_transposed_in_psum"), sem("nilpotent_products"), sem("nilpotent_step")
        s_Tt, s_yp, s_Y, s_up2, s_U = sem("t_ready"), sem("y_product"), sem("y_ready"), sem("u_products"), sem("u_ready")
        s_fp, s_F = sem("f_products"), sem("f_ready")
        s_mp, s_mr, s_go, s_tp, s_md = sem("mod_products"), sem("mod_rows_ready"), sem("gates_moved"), sem("mods_transposed"), sem("mods_ready")
        s_xt, s_xT, s_zp, s_z, s_dp, s_d = (sem("x_transposed_in_psum"), sem("x_transposed_ready"), sem("z_product"),
                                            sem("z_ready"), sem("delta_product"), sem("x_rotated"))
        s_xs = sem("x_of_batch_ready")
        block = ctx.enter_context(nc.Block())
        NG, NA = 4, 4
        GW, AW = NSKEW // NG, 6 * C // NA
        IJ = [(v, c) for v in (0, 1, 3, 4) for c in range(NK)]

        @block.sync
        def _(sp):
            sp.dma_start(Aw[:, :, 0:D0], io["P"].rearrange("(c p) d -> p c d", p=KC)).then_inc(s_p, 16)
            sp.dma_start(cT[:], io["condT"]).then_inc(s_c, 16)
            sp.dma_start(Wsk[:], io["skewT"].rearrange("(c p) n -> p c n", p=KC)).then_inc(s_w, 16)
            sp.dma_start(skb[:], io["skew_b"].partition_broadcast(B)).then_inc(s_b, 16)
            sp.dma_start(Wad[:], io["ada_w0"].rearrange("(c p) n -> p c n", p=KC)).then_inc(s_ad, 16)
            sp.dma_start(bad[:], io["ada_b0"].partition_broadcast(B)).then_inc(s_adb, 16)
            for b in range(B):
                sp.dma_start(X[:, b * NT:(b + 1) * NT, :],
                             io["x"][b].rearrange("(t p) c -> p t c", p=128)).then_inc(s_x, 16)
            sp.wait_ge(s_sv, NG)
            sp.wait_ge(s_clear, 5)
            off = 0
            for i in range(D0 - 1):
                n = D0 - 1 - i
                sp.dma_start(Up[i:i + 1, :, i + 1:D0], sv[:, off:off + n],
                             allow_slow_non_contiguous=(n == 1)).then_inc(s_up, 16)
                off += n
            for l in range(NL):
                if l + 1 < NL:
                    sp.wait_ge(s_mp, NA * (l + 1))
                    sp.wait_ge(s_mr, NA * (l + 1))
                    sp.dma_start(Wad[:], io[f"ada_w{l + 1}"].rearrange("(c p) n -> p c n", p=KC)).then_inc(s_ad, 16)
                    sp.dma_start(bad[:], io[f"ada_b{l + 1}"].partition_broadcast(B)).then_inc(s_adb, 16)
            load_attention_weights(sp, io, T, 0)

        @block.gpsimd
        def _(pool):
            for m, v in ((ident, 0.0), (from_row, 1.0), (eye3, 0.0), (upper, 1.0), (Up, 0.0), (lower, 1.0), (eyeB, 0.0),
                         (Aw[:, :, D0:D0 + 1], 0.0)):
                pool.memset(m[:], v).then_inc(s_clear, 1)
            pool.memset(ones64[:], 1.0).then_inc(s_clear, 1)
            pool.memset(T["ones_row"][:], 1.0).then_inc(s_clear, 1)
            pool.memset(T["minus_half"][:], -0.5).then_inc(s_clear, 1)
            pool.memset(root[:], 0.5).then_inc(s_clear, 1)
            pool.wait_ge(s_clear, 12)

            def select(m, pattern, op, base, mult, fill):
                pool.affine_select(out=m, in_=m, pattern=pattern, compare_op=op, fill=fill, base=base,
                                   channel_multiplier=mult).then_inc(s_mask, 1)

            select(ident[:], [[-1, 128]], ALU.not_equal, 0, 1, 1.0)
            select(from_row[:, 0, :], [[-1, D0 + 1]], ALU.is_ge, 0, 1, 0.0)
            select(eye3[:, 0, :], [[-1, D0 + 1]], ALU.not_equal, 0, 1, 1.0)
            select(upper[:], [[1, D0]], ALU.is_gt, 0, -1, 0.0)
            select(lower[:], [[-1, D0]], ALU.is_gt, 0, 1, 0.0)
            for i in range(2):
                select(eyeB[:, i, :, :], [[0, B], [-1, D0]], ALU.not_equal, 0, 1, 1.0)
            with pool.Fori(0, D0) as k:
                pool.wait_ge(s_sc, k + 1)
                pool.tensor_tensor(nrm[:], n2[:, 0:1], root[:], ALU.pow).then_inc(s_norm, 1)
                pool.wait_ge(s_vt, k + 1)
                pool.tensor_copy(Vn[:, :, bass.ds(k, 1)], vt[:].unsqueeze(2)).then_inc(s_kept, 1)
                pool.wait_ge(s_half, k + 1)
                pool.tensor_copy(crow[:, bass.ds(k, 1)], chalf[:]).then_inc(s_kept, 1)

        @block.scalar
        def _(act):
            act.wait_ge(s_c, 16)
            act.activation(e1[:], cT[:], ACT.Exp, scale=-1.0).then_inc(s_e1, 1)

        @block.tensor
        def _(pe):
            pe.wait_ge(s_sT, 1)
            pe.wait_ge(s_w, 16)
            for g in range(NG):
                for c in range(NK):
                    mm = pe.matmul(bank[2 + g][0:B, 0:GW], sT[:, c, :], Wsk[:, c, g * GW:(g + 1) * GW],
                                   start=(c == 0), stop=(c == NK - 1))
                mm.then_inc(s_skp, 1)
            pe.wait_ge(s_up, 16 * (D0 - 1))
            pe.wait_ge(s_mask, 7)
            pe.wait_ge(s_sv, NG)
            for b in range(B):
                mm = pe.transpose(bank[2][0:D0, b * D0:(b + 1) * D0], Up[:, b, :], ident[0:D0, 0:D0])
            mm.then_inc(s_upT, 1)
            pe.wait_ge(s_abs, 1)
            pe.matmul(bank[3][0:D0, 0:B * D0], ones64[:], Ab[:].rearrange("p b j -> p (b j)"),
                      start=True, stop=True).then_inc(s_n1p, 1)
            for n in range(TAYLOR - 1):
                pe.wait_ge(s_h, n + 1)
                for b in range(B):
                    mm = pe.matmul(bank[4][0:D0, b * D0:(b + 1) * D0], A[:, 1, b, :], hor[:, n % 2, b, :],
                                   start=True, stop=True)
                mm.then_inc(s_hp, 1)
            pe.wait_ge(s_h, TAYLOR)
            for b in range(B):
                mm = pe.transpose(bank[5][0:D0, b * D0:(b + 1) * D0], hor[:, (TAYLOR - 1) % 2, b, :], ident[0:D0, 0:D0])
            mm.then_inc(s_rT, 1)
            for n in range(NSQ):
                pe.wait_ge(s_R, n + 1)
                for i in range(2):
                    for b in range(B):
                        mm = pe.matmul(bank[4][0:D0, (i * B + b) * D0:(i * B + b + 1) * D0], R[:, n % 2, 1 - i, b, :],
                                       R[:, n % 2, i, b, :], start=True, stop=True)
                mm.then_inc(s_sqp, 1)
            pe.wait_ge(s_R, NSQ + 1)
            for l in range(NL):
                pe.wait_ge(s_ad, 16 * (l + 1))
                if l:
                    pe.wait_ge(s_mr, NA * l)
                for g in range(NA):
                    for c in range(NK):
                        mm = pe.matmul(bank[2 + g][0:B, 0:AW], sT[:, c, :], Wad[:, c, g * AW:(g + 1) * AW],
                                       start=(c == 0), stop=(c == NK - 1))
                    mm.then_inc(s_mp, 1)
                pe.wait_ge(s_mr, NA * (l + 1))
                if l:
                    pe.wait_ge(s_md, l)
                for n, (v, c) in enumerate(IJ):
                    mm = pe.transpose(bank[6][0:KC, n * B:(n + 1) * B], mrow[:, v * C + c * KC:v * C + (c + 1) * KC],
                                      ident[0:B, 0:B])
                mm.then_inc(s_tp, 1)
            pe.wait_ge(s_p, 16)
            with pe.Fori(0, D0) as k:
                pe.wait_ge(s_col, k + 1)
                for c in range(NK):
                    pe.matmul(psq[0:KC, 0:D0], am[:, c:c + 1].to_broadcast([KC, KC]), Aw[:, c, 0:D0],
                              start=(c == 0), stop=(c == NK - 1))
                pe.matmul(psr[0:KC, 0:D0], ek[:, 0:1].to_broadcast([KC, KC]), Aw[:, 0, 0:D0],
                          start=True, stop=True).then_inc(s_prod, 1)
            pe.wait_ge(s_kept, 2 * D0)
            pe.wait_ge(s_md, NL)
            for c in range(NK):
                mm = pe.matmul(bank[2][0:D0, 0:D0], Vn[:, c, :], Vn[:, c, :], start=(c == 0), stop=(c == NK - 1))
            mm.then_inc(s_gp, 1)
            for c in range(NK):
                mm = pe.transpose(bank[3][0:D0, c * KC:(c + 1) * KC], Vn[:, c, :], ident[0:KC, 0:KC])
            mm.then_inc(s_vT, 1)
            for n in range(5):
                pe.wait_ge(s_X, n + 1)
                pe.matmul(bank[4][0:D0, 0:D0], Xn[:, n % 2, 1, :], Xn[:, n % 2, 0, :], start=True, stop=True)
                pe.matmul(bank[4][0:D0, D0:2 * D0], Xn[:, n % 2, 0, :], Xn[:, n % 2, 1, :], start=True, stop=True).then_inc(s_xp, 1)
                pe.wait_ge(s_X, n + 2)
                pe.wait_ge(s_PT, n + 1)
                pe.matmul(bank[5][0:D0, 0:D0], Xn[:, (n + 1) % 2, 0, :], PT[:, n % 2, :], start=True, stop=True).then_inc(s_xr, 1)
            pe.wait_ge(s_Tt, 1)
            pe.matmul(bank[6][0:D0, 0:D0], Tt[:], VT[:, 0:D0], start=True, stop=True).then_inc(s_yp, 1)
            pe.wait_ge(s_Y, 1)
            for c in range(NK):
                mm = pe.matmul(bank[7][0:KC, c * D0:(c + 1) * D0], VT[:, c * KC:(c + 1) * KC], Y[:], start=True, stop=True)
            mm.then_inc(s_up2, 1)
            pe.matmul(bank[2][0:D0, 0:C], Y[:], VT[:], start=True, stop=True).then_inc(s_up2, 1)
            pe.wait_ge(s_U, 2)
            for b in range(B):
                if b >= 2:
                    pe.wait_ge(s_F, b - 1)
                pe.matmul(bank[3 + b % 2][0:D0, 0:C], Rm[:, b, :], UT[:], start=True, stop=True).then_inc(s_fp, 1)
            pe.wait_ge(s_x, 16 * B)
            pe.wait_ge(s_F, B)
            with pe.Fori(0, B) as b:
                pe.wait_ge(s_xs, b + 1)
                for c in range(NK):
                    pe.wait_ge(s_d, b * NT)
                    for t in range(NT):
                        mm = pe.transpose(bank[4 + c][0:KC, t * 128:(t + 1) * 128], xs[:, t, c * KC:(c + 1) * KC], ident[:])
                    mm.then_inc(s_xt, 1)
                pe.wait_ge(s_xT, b * NK + NK)
                for c in range(NK):
                    mm = pe.matmul(bank[7][0:D0, :], U[:, c, :], xT[:, c, :], start=(c == 0), stop=(c == NK - 1))
                mm.then_inc(s_zp, 1)
                pe.wait_ge(s_z, b + 1)
                for t in range(NT):
                    pe.matmul(bank[t][:, 0:C], zT[:, t * 128:(t + 1) * 128], F[:, bass.ds(b, 1), :].squeeze(1), start=True, stop=True).then_inc(s_dp, 1)

        @block.vector
        def _(dve):
            link = Order(dve, s_dve)
            dve.wait_ge(s_e1, 1)
            link(dve.tensor_scalar_add(e1[:], e1[:], 1.0))
            link(dve.reciprocal(e1[:], e1[:]))
            dve.wait_ge(s_c, 16)
            dve.tensor_tensor(sT[:], cT[:], e1[:], ALU.mult).then_inc(s_sT, 1)
            dve.wait_ge(s_b, 16)
            for g in range(NG):
                dve.wait_ge(s_skp, g + 1)
                dve.tensor_tensor(sv[:, g * GW:(g + 1) * GW], bank[2 + g][0:B, 0:GW], skb[:, g * GW:(g + 1) * GW],
                                  ALU.add).then_inc(s_sv, 1)
            dve.wait_ge(s_upT, 1)
            t4 = bank[2][0:D0, 0:B * D0].rearrange("p (b j) -> p b j", b=B)
            link(dve.tensor_tensor(A[:, 1, :, :], t4, Up[:], ALU.subtract))
            link(dve.tensor_scalar(A[:, 0, :, :], A[:, 1, :, :], -1.0, None, ALU.mult))
            dve.tensor_tensor(Ab[:], A[:, 0, :, :], A[:, 1, :, :], ALU.max).then_inc(s_abs, 1)
            dve.wait_ge(s_n1p, 1)
            link(dve.tensor_reduce(nrm1[:], bank[3][0:D0, 0:B * D0].rearrange("p (b j) -> p b j", b=B), AX_X, ALU.max))
            for i in range(NSQ):
                last = dve.tensor_scalar(again[:, i, :], nrm1[:], float(2 ** i), None, ALU.is_gt)
            link(last)
            link(dve.tensor_scalar(halves[:], again[:], -0.5, 1.0, ALU.mult, ALU.add))
            link(dve.tensor_copy(down[:], halves[:, 0, :]))
            for i in range(1, NSQ):
                link(dve.tensor_tensor(down[:], down[:], halves[:, i, :], ALU.mult))
            for i in range(2):
                link(dve.tensor_tensor(A[:, i, :, :], A[:, i, :, :], down[:].unsqueeze(2).to_broadcast([D0, B, D0]), ALU.mult))
            eye4 = eyeB[:, 0, :, :]
            dve.wait_ge(s_mask, 7)
            dve.scalar_tensor_tensor(hor[:, 0, :, :], A[:, 0, :, :], 1.0 / TAYLOR, eye4, ALU.mult, ALU.add).then_inc(s_h, 1)
            for n in range(TAYLOR - 1):
                dve.wait_ge(s_hp, n + 1)
                dve.scalar_tensor_tensor(hor[:, (n + 1) % 2, :, :], bank[4][0:D0, 0:B * D0].rearrange("p (b j) -> p b j", b=B),
                                         1.0 / (TAYLOR - 1 - n), eye4, ALU.mult, ALU.add).then_inc(s_h, 1)
            dve.wait_ge(s_h, TAYLOR)
            link(dve.tensor_copy(R[:, 0, 0, :, :], hor[:, (TAYLOR - 1) % 2, :, :]))
            dve.wait_ge(s_rT, 1)
            dve.tensor_copy(R[:, 0, 1, :, :], bank[5][0:D0, 0:B * D0].rearrange("p (b j) -> p b j", b=B)).then_inc(s_R, 1)
            for n in range(NSQ):
                flat = lambda x: x.rearrange("p i b j -> p (i b) j")
                dve.wait_ge(s_sqp, n + 1)
                dve.wait_ge(s_R, n + 1)
                link(dve.tensor_tensor(flat(dif[:]), bank[4][0:D0, :].rearrange("p (n j) -> p n j", j=D0),
                                       flat(R[:, n % 2, :, :, :]), ALU.subtract))
                for i in range(2):
                    last = dve.tensor_tensor(dif[:, i, :, :], dif[:, i, :, :],
                                             again[:, n, :].unsqueeze(2).to_broadcast([D0, B, D0]), ALU.mult)
                link(last)
                dve.tensor_tensor(R[:, (n + 1) % 2, :, :, :], R[:, n % 2, :, :, :], dif[:], ALU.add).then_inc(s_R, 1)
            dve.wait_ge(s_R, NSQ + 1)
            link(dve.tensor_tensor(Rm[:], R[:, NSQ % 2, 1, :, :], eye4, ALU.subtract))
            for l in range(NL):
                dve.wait_ge(s_adb, 16 * (l + 1))
                if l:
                    dve.wait_ge(s_go, 2 * l)
                    dve.wait_ge(s_tp, l)
                for g in range(NA):
                    dve.wait_ge(s_mp, NA * l + g + 1)
                    dve.tensor_tensor(mrow[:, g * AW:(g + 1) * AW], bank[2 + g][0:B, 0:AW], bad[:, g * AW:(g + 1) * AW],
                                      ALU.add).then_inc(s_mr, 1)
                dve.wait_ge(s_mr, NA * (l + 1))
                for g, v in enumerate((2, 5)):
                    dve.tensor_copy(T["gates"][:, l, g, :], mrow[:, v * C:(v + 1) * C]).then_inc(s_go, 1)
                dve.wait_ge(s_tp, l + 1)
                src = bank[6][0:KC, 0:len(IJ) * B].rearrange("p (v c b) -> p v c b", v=4, c=NK)
                for v in range(4):
                    last = dve.tensor_scalar(mods[:, l, v, :, :], src[:, v, :, :], float(v % 2), None, ALU.add)
                last.then_inc(s_md, 1)
            dve.wait_ge(s_p, 16)
            dve.wait_ge(s_clear, 12)

            def column(k):
                dve.tensor_copy(ek[:].unsqueeze(2), eye3[:, :, k]).then_inc(s_dve, 1)
                dve.tensor_tensor(am[:].unsqueeze(2), Aw[:, :, k], from_row[:, :, k], ALU.mult).then_inc(s_col, 1)

            link.n += 1
            column(slice(0, 1))
            STEP = 14
            start = link.n
            with dve.Fori(0, D0) as k:
                link = Order(dve, s_dve, k * STEP + start)
                at = bass.ds(k, 1)
                dve.wait_ge(s_prod, k + 1)
                dve.wait_ge(s_col, k + 1)
                dve.tensor_copy(n2[:, 0:1], psq[0:KC, at]).then_inc(s_dve, 1)
                dve.tensor_copy(n2[:, 1:2], psr[0:KC, at]).then_inc(s_sc, 1)
                dve.tensor_copy(a_cols[:], psq[0:KC, 0:D0]).then_inc(s_dve, 1)
                link.n = link.n + 2
                dve.wait_ge(s_sc, k + 1)
                link(dve.tensor_scalar(sgn[:], n2[:, 1:2], 0.0, -2.0, ALU.is_ge, ALU.mult))
                link(dve.tensor_scalar_add(sgn[:], sgn[:], 1.0))
                dve.wait_ge(s_norm, k + 1)
                link(dve.tensor_tensor(beta[:], sgn[:], nrm[:], ALU.mult))
                link(dve.scalar_tensor_tensor(vv[:, 0:1], n2[:, 1:2], -2.0, beta[:], ALU.mult, ALU.add))
                link(dve.scalar_tensor_tensor(vv[:, 1:2], vv[:, 0:1], beta[:, 0:1], n2[:, 0:1], ALU.mult, ALU.add))
                link(dve.tensor_scalar_max(vv[:, 1:2], vv[:, 1:2], 1e-30))
                dve.wait_ge(s_kept, k * 2)
                dve.reciprocal(chalf[:], vv[:, 1:2]).then_inc(s_half, 1)
                dve.scalar_tensor_tensor(vt[:], ek[:], beta[:, 0:1], am[:], ALU.mult, ALU.subtract).then_inc(s_vt, 1)
                dve.scalar_tensor_tensor(v_cols[:], psr[0:KC, 0:D0], beta[:, 0:1], a_cols[:], ALU.mult,
                                         ALU.subtract).then_inc(s_dve, 1)
                link.n = link.n + 1
                dve.wait_ge(s_vt, k + 1)
                dve.wait_ge(s_half, k + 1)
                link(dve.tensor_scalar(vc[:], vt[:], chalf[:, 0:1], -2.0, ALU.mult, ALU.mult))
                for c in range(NK):
                    last = dve.scalar_tensor_tensor(Aw[:, c, 0:D0], v_cols[:], vc[:, c:c + 1], Aw[:, c, 0:D0], ALU.mult, ALU.add)
                    last.then_inc(s_dve, 1)
                link.n = link.n + NK
                dve.wait_ge(s_dve, link.n)
                nxt = bass.ds(k + 1, 1)
                dve.tensor_copy(ek[:].unsqueeze(2), eye3[:, :, nxt]).then_inc(s_dve, 1)
                dve.tensor_tensor(am[:].unsqueeze(2), Aw[:, :, nxt], from_row[:, :, nxt], ALU.mult).then_inc(s_col, 1)
            link = Order(dve, s_dve, start + D0 * STEP)
            dve.wait_ge(s_kept, 2 * D0)
            dve.wait_ge(s_mask, 7)
            link(dve.tensor_scalar(crow[:], crow[:], 2.0, None, ALU.mult))
            link(dve.tensor_tensor(cdia[:], crow[0:D0, :], ident[0:D0, 0:D0], ALU.mult))
            link(dve.tensor_reduce(ccol[:], cdia[:], AX_X, ALU.add))
            dve.wait_ge(s_gp, 1)
            gram = bank[2][0:D0, 0:D0]
            link(dve.tensor_tensor(cdia[:], gram, crow[0:D0, :], ALU.mult))
            link(dve.tensor_tensor(Xn[:, 0, 1, :], cdia[:], lower[:], ALU.mult))
            link(dve.tensor_tensor(PT[:, 0, :], ident[0:D0, 0:D0], Xn[:, 0, 1, :], ALU.subtract))
            dve.scalar_tensor_tensor(Xn[:, 0, 0, :], gram, ccol[:, 0:1], upper[:], ALU.mult, ALU.mult).then_inc(s_X, 1)
            dve.wait_ge(s_vT, 1)
            dve.tensor_copy(VT[:], bank[3][0:D0, 0:C]).then_inc(s_PT, 1)
            for n in range(5):
                dve.wait_ge(s_xp, n + 1)
                dve.tensor_copy(Xn[:, (n + 1) % 2, :, :], bank[4][0:D0, 0:2 * D0].rearrange("p (i j) -> p i j", i=2)).then_inc(s_X, 1)
                dve.wait_ge(s_xr, n + 1)
                dve.wait_ge(s_PT, n + 1)
                dve.tensor_tensor(PT[:, (n + 1) % 2, :], bank[5][0:D0, 0:D0], PT[:, n % 2, :], ALU.add).then_inc(s_PT, 1)
            dve.wait_ge(s_PT, 6)
            dve.tensor_scalar(Tt[:], PT[:, 1, :], ccol[:, 0:1], None, ALU.mult).then_inc(s_Tt, 1)
            dve.wait_ge(s_yp, 1)
            dve.tensor_copy(Y[:], bank[6][0:D0, 0:D0]).then_inc(s_Y, 1)
            dve.wait_ge(s_up2, 2)
            dve.tensor_tensor(U[:], eye3[:, :, 0:D0], bank[7][0:KC, 0:NK * D0].rearrange("p (c d) -> p c d", c=NK),
                              ALU.subtract).then_inc(s_U, 1)
            link(dve.tensor_scalar(UT[:], bank[2][0:D0, 0:C], -1.0, None, ALU.mult))
            dve.tensor_tensor(UT[:, 0:D0], UT[:, 0:D0], ident[0:D0, 0:D0], ALU.add).then_inc(s_U, 1)
            for b in range(B):
                dve.wait_ge(s_fp, b + 1)
                dve.tensor_copy(F[:, b, :], bank[3 + b % 2][0:D0, 0:C]).then_inc(s_F, 1)
            dve.wait_ge(s_x, 16 * B)
            with dve.Fori(0, B) as b:
                dve.wait_ge(s_xt, b * NK)
                dve.tensor_copy(xs[:], X[:, bass.ds(b * NT, NT), :]).then_inc(s_xs, 1)
                for c in range(NK):
                    dve.wait_ge(s_xt, b * NK + c + 1)
                    dve.wait_ge(s_zp, b)
                    dve.tensor_copy(xT[:, c, :], bank[4 + c][0:KC, :]).then_inc(s_xT, 1)
                dve.wait_ge(s_zp, b + 1)
                dve.wait_ge(s_dp, b * NT)
                dve.tensor_copy(zT[:], bank[7][0:D0, :]).then_inc(s_z, 1)
                for t in range(NT):
                    dve.wait_ge(s_dp, b * NT + t + 1)
                    dve.tensor_tensor(X[:, bass.ds(b * NT + t, 1), :].squeeze(1), X[:, bass.ds(b * NT + t, 1), :].squeeze(1), bank[t][:, 0:C], ALU.add).then_inc(s_d, 1)


HD_ROWS = [6 * D, 5 * D, 5 * D]
QK_OFF = [0, 6 * D, 11 * D]
NPARTS = NK * (2 * NK + 1)
NTRI = 6
PRODUCTS = [(0, 0), (0, 1), (0, 2), (1, 0), (1, 1), (2, 0)]
KS_ROWS = len(PRODUCTS) * D
LEAD = 6
SPLITS = [(0, 0), (1, 0), (0, 1)]


def attention_half(nc, io, T, l):
    X, ident, mods = T["x"], T["ident"], T["mods"]
    with nc.cleanup_on_exit(), ExitStack() as ctx:
        def sb(name, shape, dt=F32):
            return ctx.enter_context(nc.sbuf_tensor(f"a{l}_{name}", shape, dt))

        def ps(name, shape=(128, 512)):
            return ctx.enter_context(nc.psum_tensor(f"a{l}_{name}", list(shape), F32))

        def sem(name):
            return nc.alloc_semaphore(f"a{l}_{name}")

        W = sb("w_parts", [KC, 2, NK, 4 * C], F16)
        qkb = sb("qk_bias", [6 * D, 2, NK])
        bv = sb("v_bias", [128, C])
        bp = sb("proj_bias", [128, C])
        st6 = sb("ln_stats", [128, NT, 6])
        mv = sb("ln_mean_var", [128, NT, 2])
        ve = sb("ln_var_eps", [128, NT])
        rstd = sb("ln_rstd", [128, NT])
        xn = sb("normalized_or_o", [128, NT, C])
        h32 = sb("h32", [KC, 2, NTOK])
        hT = sb("h_parts", [KC, 2, NK, NTOK], F16)
        v32 = sb("qk32", [6 * D, 2, NTOK])
        rest = sb("qk_rest", [6 * D, NTOK])
        PT3 = sb("qk_parts", [6 * D, 2, NK, 3, NTOK], BF16)
        Vn = sb("v_next", [128, NT, H, D])
        V = sb("v_with_ones", [128, NT, H, 32])
        QS = sb("q_stack", [128, H, NTOK], BF16)
        KS = sb("k_stack", [128, H, NTOK], BF16)
        MX = sb("minus_max", [128, 2, 16])
        MT = sb("minus_max_T", [16, 2, 128], BF16)
        E = sb("exp_scores", [128, 2, 4, NTOK])
        oT = sb("o_T", [128, 4, NTOK])
        rs = sb("sum_inverse", [128, H])
        oc = sb("o_channels", [KC, 2, NK * 128])
        gsel = sb("gate_of_batch", [B, C])
        gbc = sb("gate_rows", [128, C])
        y = sb("branch", [128, C])
        raw = T["staging"]
        mx = [ps(f"mx{i}") for i in range(2)]
        st = [ps(f"st{i}") for i in range(2)]
        av = [ps(f"av{i}") for i in range(2)]
        DA, DD = ps("da"), ps("dd")

        s_small, s_whi, s_wlo, s_set = sem("biases_in"), sem("weights_high"), sem("weights_split"), sem("constants_set")
        s_dve, s_var, s_rstd, s_xn = sem("dve_order"), sem("var_ready"), sem("rstd_ready"), sem("xn_ready")
        s_h, s_part, s_V = sem("h_ready"), sem("qk_parts_ready"), sem("v_ready")
        s_da, s_daev, s_dd, s_ddev = sem("da_written"), sem("da_read"), sem("dd_written"), sem("dd_read")
        s_stk = [sem(f"stack{i}_loaded") for i in range(NTRI)]
        s_mm, s_mr, s_mt, s_md = sem("mx_written"), sem("mx_read"), sem("max_T_ready"), sem("max_row_loaded")
        s_st, s_exp, s_av, s_oT = sem("st_written"), sem("st_read"), sem("av_unit_done"), sem("o_T_ready")
        s_go = sem("waits_taken")
        s_g, s_O, s_oh = sem("gate_picked"), sem("o_tokens_ready"), sem("o_parts_ready")
        block = ctx.enter_context(nc.Block())

        DD0, DDN = 5 + 1, 5 + 4 + 1 + NT
        DA0, DAN = 8, 8
        MX0, MXN = 4 * LEAD, 64 + NT
        STN = 64 + NT

        @block.sync
        def _(sp):
            sp.dma_start(qkb[:], io[f"qk_b{l}"]).then_inc(s_small, 16)
            sp.dma_start(bv[:], io[f"qkv_b{l}"][2 * C:3 * C].partition_broadcast(128)).then_inc(s_small, 16)
            sp.dma_start(bp[:], io[f"proj_b{l}"].partition_broadcast(128)).then_inc(s_small, 16)

            def stacks(i, free):
                sp.wait_ge(s_part, 6 * i + 6)
                for s in range(NTRI):
                    if free is not None:
                        sp.wait_ge(s_st, STN * free + 16 * ((3 * s + 2) // 4 + 1) if s < 5 else STN * free + 64)
                    n = min(3, H - 3 * s)
                    for side, S in ((1, KS), (0, QS)):
                        for r, pq in enumerate(PRODUCTS):
                            sp.dma_start(S[r * D:(r + 1) * D, 3 * s:3 * s + n, :],
                                         PT3[s * D:(s + 1) * D, side, 0:n, pq[side], :]).then_inc(s_stk[s], 16)

            sp.wait_ge(s_set, 3)
            stacks(0, None)
            with sp.Fori(0, B - 1) as i:
                stacks(i + 1, i)
            sp.wait_ge(s_wlo, NPARTS)
            sp.dma_start(raw[0:KC, 0:NK * FF].rearrange("p (c n) -> p c n", c=NK),
                         io[f"w1_{T['mlp_of'][l][0]}"].rearrange("(c p) n -> p c n", p=KC)).then_inc(T["s_raw"], 16)

        attention_raw = T["raw_count"]
        T["raw_count"] += 16

        @block.gpsimd
        def _(pool):
            pool.memset(KS[:], 1.0).then_inc(s_set, 1)
            pool.memset(QS[:], 0.0).then_inc(s_set, 1)
            pool.memset(V[:], 1.0).then_inc(s_set, 1)

            def rsqrt(i):
                pool.wait_ge(s_var, i + 1)
                pool.wait_ge(s_xn, NT * i)
                pool.tensor_tensor(rstd[:], ve[:], T["minus_half"][:], ALU.pow).then_inc(s_rstd, 1)

            def max_row(i, g):
                pool.wait_ge(s_mt, 4 * i + g + 1)
                if not first(i):
                    pool.wait_ge(s_st, STN * (i - 1) + 16 * (g + 1))
                pool.sem_inc(s_go, 1)
                pool.dma_start(QS[KS_ROWS:KS_ROWS + 1, 4 * g:4 * g + 4, :], MT[:, g % 2, :]).then_inc(s_md, 16)

            rsqrt(0)
            max_row(0, 0)
            with pool.Fori(0, B - 1) as i:
                rsqrt(i + 1)
                for g in (1, 2, 3):
                    pool.wait_ge(s_mt, 4 * i + g + 1)
                    pool.wait_ge(s_st, STN * i)
                    pool.sem_inc(s_go, 1)
                    pool.dma_start(QS[KS_ROWS:KS_ROWS + 1, 4 * g:4 * g + 4, :], MT[:, g % 2, :]).then_inc(s_md, 16)
                max_row(i + 1, 0)
            for g in (1, 2, 3):
                max_row(B - 1, g)
            pool.wait_ge(s_md, 16 * 4 * B)

        @block.scalar
        def _(act):
            def qkv(i, da):
                for n, c in enumerate((0, 2)):
                    act.wait_ge(s_da, da + n + 1)
                    act.wait_ge(s_h, NK * i + n)
                    act.activation(h32[:, 0, :], DA[0:KC, :], ACT.Identity, bias=mods[:, l, 0, c, at(i)],
                                   scale=mods[:, l, 1, c, at(i)]).then_inc(s_daev, 1)
                act.wait_ge(s_small, 48)
                for n in range(6):
                    side, c = 1 - n // NK, n % NK
                    M = HD_ROWS[c]
                    act.wait_ge(s_da, da + 2 + n + 1)
                    act.wait_ge(s_part, 6 * i + max(0, n - 1))
                    act.activation(v32[0:M, n % 2, :], DA[0:M, :], ACT.Identity, bias=qkb[0:M, side, c:c + 1],
                                   scale=1.0 / WS).then_inc(s_daev, 1)

            def attend(i):
                for U in range(16):
                    g = U // 4
                    for hd in range(4):
                        act.wait_ge(s_av, 16 * i + max(0, U - 1))
                        act.wait_ge(s_st, STN * i + 4 * U + hd + 1)
                        act.activation(E[:, U % 2, hd, :], st[hd % 2][:], ACT.Exp, scale=float(D) ** -0.5).then_inc(s_exp, 1)
                    if U % 4 == 1 and U > 1:
                        o_group(i, g - 1)
                o_group(i, 3)

            def o_group(i, g):
                act.wait_ge(s_av, 16 * i + 4 * g + 4)
                act.wait_ge(s_O, 4 * i)
                act.activation(oT[:, g, :], av[g % 2][:], ACT.Copy).then_inc(s_oT, 1)

            def project(i):
                for t in range(NT):
                    act.wait_ge(s_st, STN * i + 64 + t + 1)
                    act.wait_ge(s_oh, NT * i + max(0, t - 1))
                    act.activation(oc[:, t % 2, :], st[t % 2][0:KC, 0:NK * 128], ACT.Copy).then_inc(s_exp, 1)

            qkv(0, 0)
            with act.Fori(0, B - 1) as i:
                qkv(i + 1, DA0 + DAN * i)
                attend(i)
                project(i)
            attend(B - 1)
            project(B - 1)

        @block.tensor
        def _(pe):
            def dense(out, lhs, rhs, count, sem_):
                n = 0
                for c in range(NK):
                    for a, w in SPLITS:
                        mm = pe.matmul(out, lhs(c, a, w), rhs(c, a, w), start=(n == 0), stop=(n == 3 * NK - 1))
                        n += 1
                mm.then_inc(sem_, 1)

            def qkv(i, da, dd):
                pe.wait_ge(s_xn, NT * (i + 1))
                for c in range(NK):
                    bank, written, read, n = (DD, s_dd, s_ddev, dd) if c == 1 else (DA, s_da, s_daev, da)
                    pe.wait_ge(read, n)
                    for t in range(NT):
                        mm = pe.transpose(bank[0:KC, t * 128:(t + 1) * 128], xn[:, t, c * KC:(c + 1) * KC], ident[:])
                    mm.then_inc(written, 1)
                    if c == 1:
                        dd = dd + 1
                    else:
                        da = da + 1
                pe.wait_ge(s_h, NK * (i + 1))
                if first(i):
                    pe.wait_ge(s_wlo, NPARTS)
                for n in range(6):
                    side, c = 1 - n // NK, n % NK
                    pe.wait_ge(s_daev, da)
                    to = side * C + QK_OFF[c]
                    cols = lambda k, w: W[:, w, k, to:to + HD_ROWS[c]]
                    dense(DA[0:HD_ROWS[c], :], lambda k, a, w: cols(k, w), lambda k, a, w: hT[:, a, k, :], NK, s_da)
                    da = da + 1
                    if n < NT:
                        pe.wait_ge(s_ddev, dd)
                        dense(DD[:, 0:C], lambda k, a, w: hT[:, a, k, n * 128:(n + 1) * 128],
                              lambda k, a, w: W[:, w, k, 2 * C:3 * C], NK, s_dd)
                        dd = dd + 1

            def scores_for_max(i, h, t, m):
                if t == 0:
                    pe.wait_ge(s_stk[h // 3], 16 * 12 * (i + 1))
                if not (isinstance(m, int) and m < 2):
                    pe.wait_ge(s_mr, m - 1)
                pe.matmul(mx[t % 2][:], QS[0:KS_ROWS, h, t * 128:(t + 1) * 128], KS[0:KS_ROWS, h, :],
                          start=True, stop=True).then_inc(s_mm, 1)

            def attend(i, dd, m, last):
                pe.wait_ge(s_g, i + 1)
                pe.wait_ge(s_ddev, dd)
                pe.matmul(DD[:, 0:C], T["ones_row"][0:B, :], gsel[:], start=True, stop=True).then_inc(s_dd, 1)
                dd = dd + 1
                pe.wait_ge(s_V, i + 1)
                for U in range(17):
                    g, j = U // 4, U % 4
                    hm = U + LEAD
                    for hd in range(4):
                        h = 4 * g + hd
                        if U < 16:
                            if j == 0 and hd == 0:
                                pe.wait_ge(s_md, 16 * (4 * i + g + 1))
                            if hd == 0 and j == 0:
                                pe.wait_ge(s_stk[(h + 3) // 3], 16 * 12 * (i + 1))
                            n = 4 * U + hd
                            pe.wait_ge(s_exp, STN * i + max(0, n - 1))
                            pe.matmul(st[hd % 2][:], KS[0:KS_ROWS + 1, h, j * 128:(j + 1) * 128],
                                      QS[0:KS_ROWS + 1, h, :], start=True, stop=True).then_inc(s_st, 1)
                        if U < 16 and (hm < H or not last):
                            scores_for_max(i + hm // H, hm % H, hd, m)
                            m = m + 1
                        if U > 0:
                            g1, j1 = (U - 1) // 4, (U - 1) % 4
                            if j1 == 0 and hd == 0:
                                pe.wait_ge(s_oT, 4 * i + max(0, g1 - 1))
                            pe.wait_ge(s_exp, STN * i + 4 * (U - 1) + hd + 1)
                            mm = pe.matmul(av[g1 % 2][32 * hd:32 * hd + 32, :], V[:, j1, 4 * g1 + hd, :],
                                           E[:, (U - 1) % 2, hd, :], start=(j1 == 0), stop=(j1 == 3))
                        if hd == 2 and U < 16 and (hm - 1) % 4 == 3 and (hm - 1 < H or not last):
                            pe.wait_ge(s_mr, m - (3 if hm < H or not last else 0))
                            pe.wait_ge(s_ddev, dd)
                            pe.transpose(DD[0:16, 0:128], MX[:, (hm - 1) // 4 % 2, :], ident[:]).then_inc(s_dd, 1)
                            dd = dd + 1
                    if U > 0:
                        mm.then_inc(s_av, 1)
                return dd, m

            def project(i, dd, m):
                def by_token(t, m):
                    pe.wait_ge(s_mr, m - 1)
                    for g in range(4):
                        mm = pe.transpose(mx[t % 2][:, g * 128:(g + 1) * 128], oT[:, g, t * 128:(t + 1) * 128], ident[:])
                    mm.then_inc(s_mm, 1)

                def by_channel(t):
                    pe.wait_ge(s_O, NT * i + t + 1)
                    pe.wait_ge(s_exp, STN * i + 64 + t - 1)
                    for c in range(NK):
                        mm = pe.transpose(st[t % 2][0:KC, c * 128:(c + 1) * 128], xn[:, t, c * KC:(c + 1) * KC], ident[:])
                    mm.then_inc(s_st, 1)

                def out(t, dd):
                    pe.wait_ge(s_oh, NT * i + t + 1)
                    pe.wait_ge(s_ddev, dd)
                    dense(DD[:, 0:C], lambda k, a, w: hT[:, a, k, t * 128:(t + 1) * 128],
                          lambda k, a, w: W[:, w, k, 3 * C:4 * C], NK, s_dd)

                pe.wait_ge(s_oT, 4 * (i + 1))
                by_token(0, m)
                by_token(1, m + 1)
                by_channel(0)
                by_token(2, m + 2)
                by_channel(1)
                out(0, dd)
                by_token(3, m + 3)
                by_channel(2)
                out(1, dd + 1)
                by_channel(3)
                out(2, dd + 2)
                out(3, dd + 3)

            qkv(0, 0, 0)
            for h in range(LEAD):
                for t in range(4):
                    scores_for_max(0, h, t, 4 * h + t)
            pe.wait_ge(s_mr, 16)
            pe.wait_ge(s_ddev, 5)
            pe.transpose(DD[0:16, 0:128], MX[:, 0, :], ident[:]).then_inc(s_dd, 1)
            with pe.Fori(0, B - 1) as i:
                qkv(i + 1, DA0 + DAN * i, DD0 + DDN * i)
                dd, m = attend(i, DD0 + DDN * i + 5, MX0 + MXN * i, False)
                project(i, dd, m)
            dd, m = attend(B - 1, DD0 + DDN * (B - 1), MX0 + MXN * (B - 1), True)
            project(B - 1, dd, m)

        @block.vector
        def _(dve):
            def split16(link, hi, lo, src):
                link(dve.tensor_copy(hi, src))
                return dve.tensor_tensor(lo, src, hi, ALU.subtract)

            def split_weights():
                dve.wait_ge(T["s_raw"], attention_raw)
                view = raw[0:KC, 0:NK * 4 * C].rearrange("p (c n) -> p c n", c=NK)
                parts = []
                for k in range(NK):
                    for side in range(2):
                        heads = view[:, k, side * C:(side + 1) * C].rearrange("p (h d) -> p h d", d=D)
                        for c in range(NK):
                            to = side * C + QK_OFF[c]
                            parts.append((heads[:, c::NK, :], lambda p, k=k, to=to, c=c:
                                          W[:, p, k, to:to + HD_ROWS[c]].rearrange("p (h d) -> p h d", d=D)))
                    parts.append((view[:, k, 2 * C:], lambda p, k=k: W[:, p, k, 2 * C:]))
                for src, dst in parts:
                    dve.tensor_scalar(dst(0), src, WS, None, ALU.mult).then_inc(s_whi, 1)
                for n, (src, dst) in enumerate(parts):
                    dve.wait_ge(s_whi, n + 1)
                    dve.scalar_tensor_tensor(dst(1), src, WS, dst(0), ALU.mult, ALU.subtract).then_inc(s_wlo, 1)

            def norm(link, i):
                for t in range(NT):
                    last = dve.bn_stats(st6[:, t, :], X[:, one(i * NT + t), :].squeeze(1))
                    link(last)
                dve.sem_inc(s_go, 1)
                for t in range(NT):
                    dve.bn_aggr(mv[:, t, :], st6[:, t, :]).then_inc(s_dve, 1)
                link.n = link.n + NT
                dve.wait_ge(s_dve, link.n)
                dve.tensor_scalar_add(ve[:], mv[:, :, 1:2].squeeze(2), EPS).then_inc(s_var, 1)

            def normalize(link, i):
                dve.wait_ge(s_rstd, i + 1)
                if not first(i):
                    dve.wait_ge(s_st, STN * (i - 1))
                for t in range(NT):
                    dve.tensor_scalar(xn[:, t, :], X[:, one(i * NT + t), :].squeeze(1), mv[:, t, 0:1], rstd[:, t:t + 1],
                                      ALU.subtract, ALU.mult).then_inc(s_xn, 1)

            def modulated(link, i, da, dd):
                for n, c in enumerate((0, 1, 2)):
                    if c == 1:
                        dve.wait_ge(s_dd, dd + 1)
                        dve.tensor_scalar(h32[:, 1, :], DD[0:KC, :], mods[:, l, 1, c, at(i)], mods[:, l, 0, c, at(i)],
                                          ALU.mult, ALU.add).then_inc(s_ddev, 1)
                        dve.wait_ge(s_ddev, dd + 1)
                    else:
                        dve.wait_ge(s_daev, da + n // 2 + 1)
                    split16(link, hT[:, 0, c, :], hT[:, 1, c, :], h32[:, c % 2, :]).then_inc(s_h, 1)

            def qk_split(link, i, n, da):
                side, c = 1 - n // NK, n % NK
                M = HD_ROWS[c]
                src = v32[0:M, n % 2, :]
                P = lambda p: PT3[0:M, side, c, p, :]
                dve.wait_ge(s_daev, da + 2 + n + 1)
                link(dve.tensor_copy(P(0), src))
                link(dve.tensor_tensor(rest[0:M, :], src, P(0), ALU.subtract))
                link(dve.tensor_copy(P(1), rest[0:M, :]))
                dve.tensor_tensor(P(2), rest[0:M, :], P(1), ALU.subtract).then_inc(s_part, 1)
                dve.wait_ge(s_part, 6 * i + n + 1)

            def v_rows(i, t, dd):
                dve.wait_ge(s_dd, dd + 2 + t)
                dve.scalar_tensor_tensor(Vn[:, t, :, :].rearrange("p h d -> p (h d)"), DD[:, 0:C], 1.0 / WS, bv[:],
                                         ALU.mult, ALU.add).then_inc(s_ddev, 1)

            def qkv(link, i, da, dd):
                norm(link, i)
                normalize(link, i)
                modulated(link, i, da, dd)
                if not first(i):
                    for s in range(NTRI):
                        dve.wait_ge(s_stk[s], (16 * 12) * i)
                for n in range(6):
                    qk_split(link, i, n, da)
                    if n < NT:
                        v_rows(i, n, dd)
                return link

            def take_max(i, h, t, m):
                g = h // 4
                dve.wait_ge(s_mm, m + 1)
                if t == 0 and h % 4 == 0 and not (isinstance(i, int) and i == 0 and g < 2):
                    dve.wait_ge(s_mt, 4 * i + g - 1)
                dve.tensor_reduce(MX[:, g % 2, 4 * (h % 4) + t:4 * (h % 4) + t + 1], mx[t % 2][:], AX_X, ALU.max,
                                  negate=True).then_inc(s_mr, 1)

            def attend(link, i, dd, m, last):
                dve.wait_ge(s_dd, dd + 1)
                dve.tensor_copy(gbc[:], DD[:, 0:C]).then_inc(s_ddev, 1)
                dd = dd + 1
                for U in range(16):
                    hm = U + LEAD
                    for hd in range(4):
                        if hm < H or not last:
                            take_max(i + hm // H, hm % H, hd, m)
                            m = m + 1
                        if hd == 2 and (hm - 1) % 4 == 3 and (hm - 1 < H or not last):
                            g = (hm - 1) // 4
                            dve.wait_ge(s_dd, dd + 1)
                            dve.wait_ge(s_md, 16 * (4 * i + g - 1))
                            dve.tensor_copy(MT[:, g % 2, :], DD[0:16, 0:128]).then_inc(s_mt, 1)
                            dve.wait_ge(s_mt, 4 * i + g + 1)
                            dve.sem_inc(s_ddev, 1)
                            dd = dd + 1
                return dd, m

            def project(link, i, dd, m):
                def o_rows(t):
                    o = mx[t % 2][:].rearrange("p (h e) -> p h e", e=32)
                    dve.wait_ge(s_mm, m + t + 1)
                    link(dve.reciprocal(rs[:], o[:, :, D:D + 1].squeeze(2)))
                    dve.tensor_tensor(xn[:, t, :].rearrange("p (h d) -> p h d", d=D), o[:, :, 0:D],
                                      rs[:].unsqueeze(2).to_broadcast([128, H, D]), ALU.mult).then_inc(s_O, 1)
                    dve.wait_ge(s_O, NT * i + t + 1)
                    dve.sem_inc(s_mr, 1)

                def o_split(t):
                    dve.wait_ge(s_exp, STN * i + 64 + t + 1)
                    v = lambda p: hT[:, p, :, t * 128:(t + 1) * 128]
                    split16(link, v(0), v(1), oc[:, t % 2, :].rearrange("p (c n) -> p c n", c=NK)).then_inc(s_oh, 1)

                def update(t):
                    dve.wait_ge(s_dd, dd + t + 1)
                    dve.scalar_tensor_tensor(y[:], DD[:, 0:C], 1.0 / WS, bp[:], ALU.mult, ALU.add).then_inc(s_ddev, 1)
                    dve.wait_ge(s_ddev, dd + t + 1)
                    link(dve.tensor_tensor(y[:], y[:], gbc[:], ALU.mult))
                    xt = X[:, one(i * NT + t), :].squeeze(1)
                    link(dve.tensor_tensor(xt, xt, y[:], ALU.add))

                o_rows(0)
                o_rows(1)
                o_split(0)
                o_rows(2)
                o_split(1)
                update(0)
                o_rows(3)
                o_split(2)
                update(1)
                o_split(3)
                update(2)
                update(3)

            def values_and_gate(link, i):
                dve.wait_ge(s_av, 16 * i)
                dve.tensor_copy(V[:, :, :, 0:D], Vn[:]).then_inc(s_V, 1)
                dve.wait_ge(s_V, i + 1)
                dve.tensor_scalar(gsel[:], T["gates"][:, l, 0, :], ident[0:B, at(i)], None, ALU.mult).then_inc(s_g, 1)

            split_weights()
            dve.wait_ge(s_small, 48)
            dve.wait_ge(s_set, 3)
            link = Order(dve, s_dve)
            qkv(link, 0, 0, 0)
            for h in range(LEAD):
                for t in range(4):
                    take_max(0, h, t, 4 * h + t)
            dve.wait_ge(s_dd, 6)
            dve.tensor_copy(MT[:, 0, :], DD[0:16, 0:128]).then_inc(s_mt, 1)
            dve.wait_ge(s_mt, 1)
            dve.sem_inc(s_ddev, 1)
            start = link.n
            TURN = 8 + 3 + 18 + NT * (1 + 1 + 2)
            with dve.Fori(0, B - 1) as i:
                link = Order(dve, s_dve, i * TURN + start)
                values_and_gate(link, i)
                qkv(link, i + 1, DA0 + DAN * i, DD0 + DDN * i)
                dd, m = attend(link, i, DD0 + DDN * i + 5, MX0 + MXN * i, False)
                project(link, i, dd, m)
            link = Order(dve, s_dve, start + (B - 1) * TURN)
            values_and_gate(link, B - 1)
            dd, m = attend(link, B - 1, DD0 + DDN * (B - 1), MX0 + MXN * (B - 1), True)
            project(link, B - 1, dd, m)


def one(n):
    return slice(n, n + 1) if isinstance(n, int) else bass.ds(n, 1)


at = one


def first(i):
    return isinstance(i, int) and i == 0


def mlp_half(nc, io, T, l):
    X, ident, mods, raw = T["x"], T["ident"], T["mods"], T["staging"]
    passes = T["mlp_of"][l]
    routed = len(passes) > 1
    with nc.cleanup_on_exit(), ExitStack() as ctx:
        def sb(name, shape, dt=F32):
            return ctx.enter_context(nc.sbuf_tensor(f"m{l}_{name}", shape, dt))

        def ps(name):
            return ctx.enter_context(nc.psum_tensor(f"m{l}_{name}", [128, 512], F32))

        def sem(name):
            return nc.alloc_semaphore(f"m{l}_{name}")

        W1 = [T["w1_parts"]] + ([sb("w1_odd", [KC, 2, NK, FF], F16)] if routed else [])
        W2 = [T["w2_parts"]] + ([sb("w2_odd", [128, 2, NF, C], F16)] if routed else [])
        raw2 = sb("w2_raw", [128, NF, C])
        b1 = sb("b1", [128, len(passes), NF])
        b2 = sb("b2_rows", [128, len(passes), C])
        st6 = sb("ln_stats", [128, NT, 6])
        mv = sb("ln_mean_var", [128, NT, 2])
        ve = sb("ln_var_eps", [128, NT])
        rstd = sb("ln_rstd", [128, NT])
        xn = sb("normalized", [128, NT, C])
        h32 = sb("h32", [KC, NTOK])
        hT = sb("h_parts", [KC, 2, NK, B * NTOK], F16)
        gsel = sb("gate_of_batch", [B, C])
        gbc = sb("gate_rows", [128, B, C])
        g32 = sb("hidden32", [128, 2, NTOK])
        Hs = sb("hidden_parts", [128, 2, 3, NTOK], F16)
        y = sb("branch", [128, C])
        wg = sb("router_w", [KC, NK, NE])
        wgs = sb("router_w_parts", [KC, 2, NK, NE], F16)
        lg = sb("logits", [128, NT, NE])
        cmp = sb("beaten_by", [128, NT, NE, NE])
        rank = sb("rank", [128, NT, NE])
        sel = sb("selected", [128, NT, NE])
        tot = sb("half_total", [128, NT])
        arg = sb("sigmoid_arg", [128, NT, NE])
        cw = sb("expert_weight", [128, B * NT, NE])
        hb = [ps(f"hidden{i}") for i in range(3)]
        ob = [ps(f"out{t}") for t in range(NT)]
        DD = ps("dd")

        s_small, s_raw2, s_w1, s_w2 = sem("biases_in"), sem("w2_raw_in"), sem("w1_split"), sem("w2_split")
        s_dve, s_pool, s_var, s_rstd, s_xn, s_h = (sem("dve_order"), sem("pool_order"), sem("var_ready"), sem("rstd_ready"),
                                                   sem("xn_ready"), sem("h_ready"))
        s_dd, s_ddev, s_g, s_th, s_arg, s_cw = (sem("dd_written"), sem("dd_read"), sem("gate_picked"), sem("tanh_ready"),
                                                sem("arg_ready"), sem("weights_ready"))
        s_hb, s_gelu, s_hs, s_out, s_ob = (sem("hidden_written"), sem("gelu_done"), sem("hidden_split"), sem("out_added"),
                                                sem("out_read"))
        s_wgs, s_clr, s_go = sem("router_w_split"), sem("cleared"), sem("waits_taken")
        block = ctx.enter_context(nc.Block())
        DDL = NK + 1 + (1 if routed else 0)
        base_raw = T["raw_count"]

        @block.sync
        def _(sp):
            sp.dma_start(raw2[:], io[f"w2_{passes[0]}"].rearrange("(f p) n -> p f n", p=128)).then_inc(s_raw2, 16)
            for n, m in enumerate(passes):
                sp.dma_start(b1[:, n, :], io[f"b1_{m}"]).then_inc(s_small, 16)
                sp.dma_start(b2[:, n, :], io[f"b2_{m}"].partition_broadcast(128)).then_inc(s_small, 16)
            if routed:
                sp.dma_start(wg[:], io["gate_w"].rearrange("(c p) n -> p c n", p=KC)).then_inc(s_small, 16)
            for n, m in enumerate(passes[1:], 1):
                sp.wait_ge(s_w1, n)
                sp.dma_start(raw[0:KC, :].rearrange("p (c n) -> p c n", c=NK),
                             io[f"w1_{m}"].rearrange("(c p) n -> p c n", p=KC)).then_inc(T["s_raw"], 16)
                sp.wait_ge(s_w2, NF * n)
                sp.dma_start(raw2[:], io[f"w2_{m}"].rearrange("(f p) n -> p f n", p=128)).then_inc(s_raw2, 16)
            if l + 1 < NL:
                sp.wait_ge(s_w1, len(passes))
                load_attention_weights(sp, io, T, l + 1)

        T["raw_count"] = base_raw + 16 * (len(passes) - 1) + (32 if l + 1 < NL else 0)

        @block.gpsimd
        def _(pool):
            order = Order(pool, s_pool)
            if routed:
                pool.memset(cmp[:], 0.0).then_inc(s_clr, 1)

            def rsqrt(i):
                pool.wait_ge(s_var, i + 1)
                pool.tensor_tensor(rstd[:], ve[:], T["minus_half"][:], ALU.pow).then_inc(s_rstd, 1)

            def split(dst, src, done):
                order(pool.tensor_scalar(src, src, WS, 1.0, ALU.mult, ALU.mult))
                order(pool.tensor_copy(dst(0), src))
                pool.tensor_tensor(dst(1), src, dst(0), ALU.subtract).then_inc(*done)

            def split_w1(n):
                pool.wait_ge(T["s_raw"], base_raw + 16 * n)
                if n >= 2:
                    pool.wait_ge(s_out, NF * B * (n - 1))
                v = raw[0:KC, :].rearrange("p (c n) -> p c n", c=NK)
                split(lambda p: W1[n % 2][:, p, :, :], v, (s_w1, 1))

            def split_w2(n):
                pool.wait_ge(s_raw2, 16 * (n + 1))
                for f in range(NF):
                    split(lambda p: W2[n % 2][:, p, f, :], raw2[:, f, :], (s_w2, 1))

            rsqrt(0)
            split_w1(0)
            split_w2(0)
            for i in range(1, B):
                rsqrt(i)
            for n in range(1, len(passes)):
                split_w1(n)
                split_w2(n)

        @block.scalar
        def _(act):
            act.wait_ge(s_small, 32 * len(passes) + (16 if routed else 0))

            def hidden(n, i):
                k = (n * B + i) * NF
                for f in range(NF):
                    act.wait_ge(s_hb, k + f + 1)
                    act.wait_ge(s_hs, k + max(0, f - 1) if f else k)
                    act.activation(g32[:, f % 2, :], hb[f % 3][:], ACT.Gelu_apprx_tanh, bias=b1[:, n, f:f + 1],
                                   scale=1.0 / WS).then_inc(s_gelu, 1)

            def router(i):
                act.wait_ge(s_arg, i + 1)
                act.activation(arg[:], arg[:], ACT.Tanh).then_inc(s_th, 1)

            if routed:
                router(0)
            with act.Fori(0, B - 1) as i:
                if routed:
                    router(i + 1)
                hidden(0, i)
            hidden(0, B - 1)
            for n in range(1, len(passes)):
                with act.Fori(0, B) as i:
                    hidden(n, i)

        @block.tensor
        def _(pe):
            def layernorm(i):
                dd = DDL * i
                pe.wait_ge(s_xn, NT * (i + 1))
                for c in range(NK):
                    pe.wait_ge(s_ddev, dd + c)
                    for t in range(NT):
                        mm = pe.transpose(DD[0:KC, t * 128:(t + 1) * 128], xn[:, t, c * KC:(c + 1) * KC], ident[:])
                    mm.then_inc(s_dd, 1)
                pe.wait_ge(s_g, i + 1)
                pe.wait_ge(s_ddev, dd + NK)
                pe.matmul(DD[:, 0:C], T["ones_row"][0:B, :], gsel[:], start=True, stop=True).then_inc(s_dd, 1)
                if routed:
                    pe.wait_ge(s_wgs, 1)
                    pe.wait_ge(s_ddev, dd + NK + 1)
                    pe.wait_ge(s_h, NK * (i + 1))
                    for t in range(NT):
                        n = 0
                        for c in range(NK):
                            for a, w in SPLITS:
                                mm = pe.matmul(DD[:, t * NE:(t + 1) * NE], hT[:, a, c, tokens(i, t, 128)], wgs[:, w, c, :],
                                               start=(n == 0), stop=(n == 3 * NK - 1))
                                n += 1
                    mm.then_inc(s_dd, 1)

            def mlp(n, i):
                k = (n * B + i) * NF
                pe.wait_ge(s_h, NK * (i + 1) if n == 0 else NK * B)

                def out(f):
                    if isinstance(i, int) and i == 0 and n == 0 or not isinstance(i, int):
                        pe.wait_ge(s_w2, NF * n + f + 1)
                    pe.wait_ge(s_hs, k + f + 1)
                    if f == 0:
                        pe.wait_ge(s_ob, (n * B + i) * NT)
                    for t in range(NT):
                        for q, (a, w) in enumerate(SPLITS):
                            mm = pe.matmul(ob[t][:, 0:C], Hs[:, a, f % 3, t * 128:(t + 1) * 128], W2[n % 2][:, w, f, :],
                                           start=(f == 0 and q == 0), stop=(f == NF - 1 and q == 2))
                    mm.then_inc(s_out, 1)

                pe.wait_ge(s_w1, n + 1)
                for f in range(NF):
                    pe.wait_ge(s_gelu, k + max(0, f - 2))
                    q = 0
                    for c in range(NK):
                        for a, w in SPLITS:
                            mm = pe.matmul(hb[f % 3][:], W1[n % 2][:, w, c, f * 128:(f + 1) * 128],
                                           hT[:, a, c, tokens(i, 0, NTOK)], start=(q == 0), stop=(q == 3 * NK - 1))
                            q += 1
                    mm.then_inc(s_hb, 1)
                    if f >= 2:
                        out(f - 2)
                out(NF - 2)
                out(NF - 1)

            layernorm(0)
            with pe.Fori(0, B - 1) as i:
                layernorm(i + 1)
                mlp(0, i)
            mlp(0, B - 1)
            for n in range(1, len(passes)):
                with pe.Fori(0, B) as i:
                    mlp(n, i)

        @block.vector
        def _(dve):
            def layernorm(link, i):
                dd = DDL * i
                for t in range(NT):
                    link(dve.bn_stats(st6[:, t, :], X[:, one(i * NT + t), :].squeeze(1)))
                dve.sem_inc(s_go, 1)
                for t in range(NT):
                    dve.bn_aggr(mv[:, t, :], st6[:, t, :]).then_inc(s_dve, 1)
                link.n = link.n + NT
                dve.wait_ge(s_dve, link.n)
                dve.tensor_scalar_add(ve[:], mv[:, :, 1:2].squeeze(2), EPS).then_inc(s_var, 1)
                dve.tensor_scalar(gsel[:], T["gates"][:, l, 1, :], ident[0:B, one(i)], None, ALU.mult).then_inc(s_g, 1)
                dve.wait_ge(s_rstd, i + 1)
                dve.wait_ge(s_dd, dd)
                for t in range(NT):
                    dve.tensor_scalar(xn[:, t, :], X[:, one(i * NT + t), :].squeeze(1), mv[:, t, 0:1], rstd[:, t:t + 1],
                                      ALU.subtract, ALU.mult).then_inc(s_xn, 1)
                for c in range(NK):
                    dve.wait_ge(s_dd, dd + c + 1)
                    dve.tensor_scalar(h32[:], DD[0:KC, :], mods[:, l, 3, c, one(i)], mods[:, l, 2, c, one(i)],
                                      ALU.mult, ALU.add).then_inc(s_ddev, 1)
                    dve.wait_ge(s_ddev, dd + c + 1)
                    v = lambda p: hT[:, p, c, tokens(i, 0, NTOK)]
                    link(dve.tensor_copy(v(0), h32[:]))
                    dve.tensor_tensor(v(1), h32[:], v(0), ALU.subtract).then_inc(s_h, 1)
                    dve.wait_ge(s_h, NK * i + c + 1)
                dve.wait_ge(s_dd, dd + NK + 1)
                dve.tensor_copy(gbc[:, one(i), :].squeeze(1), DD[:, 0:C]).then_inc(s_ddev, 1)
                if routed:
                    router(link, i, dd)

            def router(link, i, dd):
                dve.wait_ge(s_dd, dd + NK + 2)
                dve.tensor_scalar(lg[:], DD[:, 0:NT * NE].rearrange("p (t e) -> p t e", e=NE), 1.0 / WS, None,
                                  ALU.mult).then_inc(s_ddev, 1)
                dve.wait_ge(s_ddev, dd + NK + 2)
                for e in range(NE):
                    for lo, hi, op in ((0, e, ALU.is_ge), (e + 1, NE, ALU.is_gt)):
                        if lo < hi:
                            last = dve.tensor_tensor(cmp[:, :, e, lo:hi], lg[:, :, lo:hi],
                                                     lg[:, :, e:e + 1].to_broadcast([128, NT, hi - lo]), op)
                            link(last)
                link(dve.tensor_reduce(rank[:], cmp[:], AX_X, ALU.add))
                link(dve.tensor_scalar(sel[:], rank[:], 2.0, None, ALU.is_lt))
                link(dve.tensor_tensor(rank[:], lg[:], sel[:], ALU.mult))
                link(dve.tensor_reduce(tot[:], rank[:], AX_X, ALU.add))
                dve.scalar_tensor_tensor(arg[:], tot[:].unsqueeze(2).to_broadcast([128, NT, NE]), -0.5, lg[:], ALU.mult,
                                         ALU.add).then_inc(s_arg, 1)
                dve.wait_ge(s_th, i + 1)
                link(dve.tensor_scalar(arg[:], arg[:], 0.5, 0.5, ALU.mult, ALU.add))
                dve.tensor_tensor(cw[:, tokens(i, 0, NT, NT), :], arg[:], sel[:], ALU.mult).then_inc(s_cw, 1)

            def mlp(link, n, i):
                k = (n * B + i) * NF
                for f in range(NF):
                    dve.wait_ge(s_gelu, k + f + 1)
                    dve.wait_ge(s_out, k + max(0, f - 2))
                    v = lambda p: Hs[:, p, f % 3, :]
                    link(dve.tensor_copy(v(0), g32[:, f % 2, :]))
                    dve.tensor_tensor(v(1), g32[:, f % 2, :], v(0), ALU.subtract).then_inc(s_hs, 1)
                dve.wait_ge(s_out, k + NF)
                for t in range(NT):
                    xt = X[:, one(i * NT + t), :].squeeze(1)
                    dve.scalar_tensor_tensor(y[:], ob[t][:, 0:C], 1.0 / WS, b2[:, n, :], ALU.mult, ALU.add).then_inc(s_ob, 1)
                    dve.wait_ge(s_ob, (n * B + i) * NT + t + 1)
                    g = gbc[:, one(i), :].squeeze(1)
                    if routed:
                        link(dve.scalar_tensor_tensor(y[:], y[:], cw[:, one(i * NT + t), n:n + 1].squeeze(1), g, ALU.mult, ALU.mult))
                    else:
                        link(dve.tensor_tensor(y[:], y[:], g, ALU.mult))
                    link(dve.tensor_tensor(xt, xt, y[:], ALU.add))

            dve.wait_ge(s_small, 32 * len(passes) + (16 if routed else 0))
            link = Order(dve, s_dve)
            if routed:
                dve.wait_ge(s_clr, 1)
                link(dve.tensor_scalar(wg[:], wg[:], WS, None, ALU.mult))
                link(dve.tensor_copy(wgs[:, 0, :, :], wg[:]))
                dve.tensor_tensor(wgs[:, 1, :, :], wg[:], wgs[:, 0, :, :], ALU.subtract).then_inc(s_wgs, 1)
            layernorm(link, 0)
            start, LN, MLP = link.n, 2 * NT + NK + (6 + 4 + 1 if routed else 0), NF + 2 * NT
            with dve.Fori(0, B - 1) as i:
                link = Order(dve, s_dve, i * (LN + MLP) + start)
                layernorm(link, i + 1)
                mlp(link, 0, i)
            link = Order(dve, s_dve, start + (B - 1) * (LN + MLP))
            mlp(link, 0, B - 1)
            start = link.n
            for n in range(1, len(passes)):
                with dve.Fori(0, B) as i:
                    mlp(Order(dve, s_dve, i * MLP + start), n, i)
                start += B * MLP


def tokens(i, t, n, per=NTOK):
    at0 = i * per + t * 128
    return slice(at0, at0 + n) if isinstance(i, int) else bass.ds(at0, n)


def load_attention_weights(sp, io, T, l):
    v = T["staging"][0:KC, 0:NK * 4 * C].rearrange("p (c n) -> p c n", c=NK)
    sp.dma_start(v[:, :, 0:3 * C], io[f"qkv_w{l}"].rearrange("(c p) n -> p c n", p=KC)).then_inc(T["s_raw"], 16)
    sp.dma_start(v[:, :, 3 * C:4 * C], io[f"proj_w{l}"].rearrange("(c p) n -> p c n", p=KC)).then_inc(T["s_raw"], 16)





def build(nc, io, out):
    with ExitStack() as ctx:
        def sb(name, shape, dt=F32):
            return ctx.enter_context(nc.sbuf_tensor(name, shape, dt))

        T = {
            "x": sb("x_tokens", [128, B * NT, C]),
            "ident": sb("identity", [128, 128]),
            "ones_row": sb("ones_rows", [B, 128]),
            "minus_half": sb("minus_half", [128, NT]),
            "mods": sb("mods", [KC, NL, 4, NK, B]),
            "gates": sb("gates", [B, NL, 2, C]),
            "staging": sb("raw_weights", [128, NK * FF]),
            "w1_parts": sb("w1_parts", [KC, 2, NK, FF], F16),
            "w2_parts": sb("w2_parts", [128, 2, NF, C], F16),
            "s_raw": nc.alloc_semaphore("raw_weights_in"),
            "raw_count": 32,
            "mlp_of": [[0], [1, 2, 3, 4], [5]],
        }
        prepare_and_rotate(nc, io, T)
        for l in range(NL):
            attention_half(nc, io, T, l)
            mlp_half(nc, io, T, l)
        store(nc, T, out)


def store(nc, T, out):
    with ExitStack() as ctx:
        s_out = nc.alloc_semaphore("out_written")
        block = ctx.enter_context(nc.Block())

        @block.sync
        def _(sp):
            for b in range(B):
                sp.dma_start(out[b].rearrange("(t p) c -> p t c", p=128), T["x"][:, b * NT:(b + 1) * NT, :]).then_inc(s_out, 16)
            sp.wait_ge(s_out, 16 * B)


def layouts(inputs):
    import numpy as np

    a = {k: np.asarray(v) for k, v in inputs.items()}
    L = {1: "L1_cond_", 2: "L2_cond_", 3: "L3_cond_"}
    ada_w = [a["L1_cond_W_ada"], a["L2_cond_w_adaln"], a["L3_cond_ada_w"]]
    ada_b = [a["L1_cond_b_ada"], a["L2_cond_b_adaln"], a["L3_cond_ada_b"]]
    per_layer = {
        "qkv_w": [a["L1_cond_W_qkv"], a["L2_cond_w_qkv"], a["L3_cond_qkv_w"]],
        "qkv_b": [a["L1_cond_b_qkv"], a["L2_cond_b_qkv"], a["L3_cond_qkv_b"]],
        "proj_w": [a["L1_cond_W_proj"], a["L2_cond_w_proj"], a["L3_cond_out_w"]],
        "proj_b": [a["L1_cond_b_proj"], a["L2_cond_b_proj"], a["L3_cond_out_b"]],
    }
    put = {"x": a["x"], "P": a["L0_cond_P"], "skewT": a["L0_cond_W"].T, "skew_b": a["L0_cond_b"],
           "condT": a["cond_1152"].T.reshape(NK, KC, B).transpose(1, 0, 2), "gate_w": a["L2_cond_w_gate"]}
    for l in range(NL):
        put[f"ada_w{l}"], put[f"ada_b{l}"] = ada_w[l], ada_b[l]
        for k, v in per_layer.items():
            put[f"{k}{l}"] = v[l]
        qk = np.pad(per_layer["qkv_b"][l][:2 * C].reshape(2, H, D), ((0, 0), (0, 2), (0, 0)))
        put[f"qk_b{l}"] = qk.reshape(2, 6, NK, D).transpose(1, 3, 0, 2).reshape(6 * D, 2, NK)
    mlp = [("L1_cond_W_fc1", "L1_cond_b_fc1", "L1_cond_W_fc2", "L1_cond_b_fc2", None)]
    mlp += [("L2_cond_w1", "L2_cond_b1", "L2_cond_w2", "L2_cond_b2", e) for e in range(NE)]
    mlp += [("L3_cond_w1", "L3_cond_b1", "L3_cond_w2", "L3_cond_b2", None)]
    for m, (w1, b1, w2, b2, e) in enumerate(mlp):
        get = lambda n: a[n] if e is None else a[n][e]
        put[f"w1_{m}"], put[f"w2_{m}"], put[f"b2_{m}"] = get(w1), get(w2), get(b2)
        put[f"b1_{m}"] = get(b1).reshape(NF, 128).T
    return {k: np.ascontiguousarray(v) for k, v in put.items()}


def kernel(**inputs):
    import concourse.bacc as bacc
    from concourse.bass_utils import run_bass_kernel_spmd as run

    nc = bacc.Bacc("TRN2", target_bir_lowering=False, num_devices=1)
    arrays = layouts(inputs)
    io = {k: nc.dram_tensor(f"in_{k}", v.shape, mybir.dt.from_np(v.dtype), kind="ExternalInput").ap()
          for k, v in arrays.items()}
    out = nc.dram_tensor("out_x", (B, NTOK, C), F32, kind="ExternalOutput").ap()
    build(nc, io, out)
    r = run(nc, [{f"in_{k}": v for k, v in arrays.items()}], core_ids=[0])
    return r.results[0]["out_x"]
```

```python
from contextlib import ExitStack

import concourse.bass as bass
from concourse import mybir

F32 = mybir.dt.float32
F16 = mybir.dt.float16
BF16 = mybir.dt.bfloat16
ALU = mybir.AluOpType
ACT = mybir.ActivationFunctionType
AX_X = mybir.AxisListType.X

B, NTOK, C = 4, 512, 288
NT = NTOK // 128
NK, KC = 3, 96
D0 = 64
NSKEW = D0 * (D0 - 1) // 2
NSQ = 18
TAYLOR = 13
H, D = 16, 18
NL = 3
FF = 4 * C
NF = FF // 128
NE = 4
WS = 256.0
EPS = 1e-6


FREE = 1


def free_at_start(eng, *sems):
    for sem in sems:
        eng.sem_inc(sem, FREE)


class Order:

    def __init__(self, eng, sem, start=0):
        self.eng, self.sem, self.n = eng, sem, start

    def __call__(self, ins):
        self.n = self.n + 1
        ins.then_inc(self.sem, 1)
        self.eng.wait_ge(self.sem, self.n)

    def pass_by(self, count):
        self.n = self.n + count


def split(pool, hi, lo, src, s_hi, n, s_done):
    pool.tensor_scalar(src, src, WS, 1.0, ALU.mult, ALU.mult).then_inc(s_hi, 1)
    pool.wait_ge(s_hi, 2 * n + 1)
    pool.tensor_copy(hi, src).then_inc(s_hi, 1)
    pool.wait_ge(s_hi, 2 * n + 2)
    pool.tensor_tensor(lo, src, hi, ALU.subtract).then_inc(s_done, 1)


def load_w1(sp, io, to, m, sem):
    sp.dma_start(to[0:KC, :].rearrange("p (c n) -> p c n", c=NK),
                 io[f"w1_{m}"].rearrange("(c p) n -> p c n", p=KC)).then_inc(sem, 16)


def load_w2(sp, io, to, m, sem):
    sp.dma_start(to[:, 0:NF * C].rearrange("p (f n) -> p f n", f=NF),
                 io[f"w2_{m}"].rearrange("(f p) n -> p f n", p=128)).then_inc(sem, 16)


def load_attention_weights(sp, io, T, l):
    v = T["staging"][0:KC, 0:NK * 4 * C].rearrange("p (c n) -> p c n", c=NK)
    sp.dma_start(v[:, :, 0:3 * C], io[f"qkv_w{l}"].rearrange("(c p) n -> p c n", p=KC)).then_inc(T["s_raw"], 16)
    sp.dma_start(v[:, :, 3 * C:4 * C], io[f"proj_w{l}"].rearrange("(c p) n -> p c n", p=KC)).then_inc(T["s_raw"], 16)


def split_w1(pool, raw, W1, s_hi, n, s_done):
    view = raw[0:KC, :].rearrange("p (c n) -> p c n", c=NK)
    split(pool, W1[:, 0, :, :], W1[:, 1, :, :], view, s_hi, n, s_done)


def split_w2(pool, raw, W2, s_hi, n, s_done):
    for f in range(NF):
        split(pool, W2[:, 0, f, :], W2[:, 1, f, :], raw[:, f * C:(f + 1) * C], s_hi, n + f, s_done)


def split_attention_weights(pool, T, s_hi, n, s_done):
    W = T["w_att"]
    view = T["staging"][0:KC, 0:NK * 4 * C].rearrange("p (c n) -> p c n", c=NK)
    for k in range(NK):
        for side in range(2):
            heads = view[:, k, side * C:(side + 1) * C].rearrange("p (h d) -> p h d", d=D)
            for c in range(NK):
                to = side * C + QK_OFF[c]
                part = lambda p: W[:, p, k, to:to + HD_ROWS[c]].rearrange("p (h d) -> p h d", d=D)
                split(pool, part(0), part(1), heads[:, c::NK, :], s_hi, n, s_done)
                n += 1
        split(pool, W[:, 0, k, 2 * C:], W[:, 1, k, 2 * C:], view[:, k, 2 * C:], s_hi, n, s_done)
        n += 1


def prepare_and_rotate(nc, io, T):
    X, ident, mods = T["x"], T["ident"], T["mods"]
    with nc.cleanup_on_exit(), ExitStack() as ctx:
        def sb(name, shape, dt=F32):
            return ctx.enter_context(nc.sbuf_tensor(name, shape, dt))

        def sem(name):
            return nc.alloc_semaphore(name)

        Aw = sb("qr_work", [KC, NK, D0 + 1])
        Vn = sb("qr_vectors", [KC, NK, D0])
        from_row = sb("from_row", [KC, NK, D0 + 1])
        eye3 = sb("eye3", [KC, NK, D0 + 1])
        am = sb("column_masked", [KC, NK])
        ek = sb("unit_column", [KC, NK])
        vt = sb("minus_v", [KC, NK])
        vc = sb("v_times_c", [KC, NK])
        a_cols = sb("column_products", [KC, D0])
        v_cols = sb("vector_products", [KC, D0])
        n2 = sb("norm2", [KC, 1])
        nrm = sb("norm", [KC, 1])
        root = sb("exponent_half", [KC, 1])
        sgn = sb("minus_sign", [KC, 1])
        beta = sb("beta", [KC, 1])
        vv = sb("half_v_dot_v", [KC, 1])
        cv = sb("c_factor", [KC, 1])
        crow = sb("c_row", [KC, D0])
        cdia = sb("c_diagonal", [D0, D0])
        ccol = sb("c_col", [D0, 1])
        upper = sb("strict_upper", [D0, D0])
        lower = sb("strict_lower", [D0, D0])
        Xn = sb("nilpotent", [D0, 2, 2, D0])
        PT = sb("inverse_transposed", [D0, 2, D0])
        VT = sb("v_transposed", [D0, C])
        Tt = sb("T_transposed", [D0, D0])
        Y = sb("T_v1T", [D0, D0])
        U = sb("u_factor", [KC, NK, D0])
        UT = sb("u_transposed", [D0, C])
        Rm = sb("rotation_T_minus_one", [D0, B, D0])
        F = sb("rotated_minus_same", [D0, B, C])
        cT = sb("cond_T", [KC, NK, B])
        e1 = sb("silu_denominator", [KC, NK, B])
        sT = sb("silu_T", [KC, NK, B])
        Wsk = sb("skew_weights", [KC, NK, NSKEW])
        skb = sb("skew_bias", [B, NSKEW])
        sv = sb("skew_values", [B, NSKEW])
        Up = sb("skew_upper", [D0, B, D0])
        A = sb("skew", [D0, 2, B, D0])
        Ab = sb("skew_abs", [D0, B, D0])
        ones64 = sb("ones64", [D0, D0])
        nrm1 = sb("norm1", [D0, B])
        again = sb("square_again", [D0, NSQ, B])
        halves = sb("halvings", [D0, NSQ, B])
        down = sb("scale_down", [D0, B])
        hor = sb("horner", [D0, 2, B, D0])
        R = sb("rotation", [D0, 2, 2, B, D0])
        dif = sb("squared_minus_same", [D0, 2, B, D0])
        eyeB = sb("eye_batches", [D0, 2, B, D0])
        Wad = sb("ada_weights", [KC, NK, 6 * C])
        bad = sb("ada_bias", [B, 6 * C])
        mrow = sb("mod_rows", [B, 6 * C])
        xs = sb("x_of_batch", [128, NT, C])
        xT = sb("x_transposed", [KC, NK, B * NTOK])
        inv = sb("inverse_of_step", [D0, TAYLOR])
        n2g, alpha, absa = sb("norm2_guarded", [KC, 1]), sb("alpha", [KC, 1]), sb("alpha_abs", [KC, 1])
        zT = sb("z_transposed", [D0, NTOK])
        bank = [ctx.enter_context(nc.psum_tensor(f"bank{i}", [128, 512], F32)) for i in range(8)]
        psq, psr = bank[0], bank[1]

        s_p, s_x, s_c, s_w, s_b = sem("p_in"), sem("x_in"), sem("cond_in"), sem("skew_w_in"), sem("skew_b_in")
        s_ad, s_adb = sem("ada_w_in"), sem("ada_b_in")
        s_clear, s_mask = sem("masks_cleared"), sem("masks_ready")
        s_dve, s_whi, s_wlo = sem("dve_order"), sem("weights_high"), sem("weights_split")
        s_col, s_prod, s_sc, s_norm = sem("column_ready"), sem("products_ready"), sem("norm2_ready"), sem("norm_ready")
        s_vt, s_kept, s_half = sem("vector_ready"), sem("vector_kept"), sem("c_factor_ready")
        s_e1, s_sT = sem("silu_exp_ready"), sem("silu_ready")
        s_skp, s_sv, s_up = sem("skew_products"), sem("skew_values_ready"), sem("skew_moved")
        s_upT, s_n1p = sem("upper_transposed"), sem("norm_products")
        s_abs, s_hp, s_h = sem("abs_ready"), sem("horner_product"), sem("horner_ready")
        s_rT, s_sqp, s_R = sem("r_transposed"), sem("square_products"), sem("squared")
        s_gp, s_X, s_PT = sem("gram_products"), sem("nilpotent_ready"), sem("inverse_ready")
        s_vT, s_xp, s_xr = sem("v_transposed_in_psum"), sem("nilpotent_products"), sem("nilpotent_step")
        s_Tt, s_yp, s_Y, s_up2, s_U = sem("t_ready"), sem("y_product"), sem("y_ready"), sem("u_products"), sem("u_ready")
        s_fp, s_F = sem("f_products"), sem("f_ready")
        s_mp, s_mr, s_tp, s_md = sem("mod_products"), sem("mod_rows_ready"), sem("mods_transposed"), sem("mods_ready")
        s_xt, s_xT, s_zp, s_z, s_dp, s_d = (sem("x_transposed_in_psum"), sem("x_transposed_ready"), sem("z_product"),
                                            sem("z_ready"), sem("delta_product"), sem("x_rotated"))
        s_xs, s_inv, s_go = sem("x_of_batch_ready"), sem("inverses_set"), sem("waits_taken")
        block = ctx.enter_context(nc.Block())
        NG, NA = 4, 4
        GW, AW = NSKEW // NG, 6 * C // NA
        MODS, HORNER, SQUARES, XT = NA, TAYLOR - 1, NSQ, B
        WAIT_SKEW = 6
        REST = D0 - NL * MODS - WAIT_SKEW - HORNER - SQUARES - XT
        IJ = [(v, c) for v in range(6) for c in range(NK)]

        @block.sync
        def _(sp):
            sp.dma_start(Aw[:, :, 0:D0], io["P"].rearrange("(c p) d -> p c d", p=KC)).then_inc(s_p, 16)
            sp.dma_start(cT[:], io["condT"]).then_inc(s_c, 16)
            sp.dma_start(Wsk[:], io["skewT"].rearrange("(c p) n -> p c n", p=KC)).then_inc(s_w, 16)
            sp.dma_start(skb[:], io["skew_b"].partition_broadcast(B)).then_inc(s_b, 16)
            sp.dma_start(Wad[:], io["ada_w0"].rearrange("(c p) n -> p c n", p=KC)).then_inc(s_ad, 16)
            sp.dma_start(bad[:], io["ada_b0"].partition_broadcast(B)).then_inc(s_adb, 16)
            for b in range(B):
                sp.dma_start(X[:, b * NT:(b + 1) * NT, :],
                             io["x"][b].rearrange("(t p) c -> p t c", p=128)).then_inc(s_x, 16)
            sp.wait_ge(s_sv, NG)
            sp.wait_ge(s_clear, 5)
            off = 0
            for i in range(D0 - 1):
                n = D0 - 1 - i
                sp.dma_start(Up[i:i + 1, :, i + 1:D0], sv[:, off:off + n],
                             allow_slow_non_contiguous=(n == 1)).then_inc(s_up, 16)
                off += n
            for l in range(NL):
                if l + 1 < NL:
                    sp.wait_ge(s_mp, NA * (l + 1))
                    sp.wait_ge(s_mr, FREE + NA * (l + 1))
                    sp.dma_start(Wad[:], io[f"ada_w{l + 1}"].rearrange("(c p) n -> p c n", p=KC)).then_inc(s_ad, 16)
                    sp.dma_start(bad[:], io[f"ada_b{l + 1}"].partition_broadcast(B)).then_inc(s_adb, 16)
            load_attention_weights(sp, io, T, 0)

        @block.gpsimd
        def _(pool):
            free_at_start(pool, s_kept)
            for m, v in ((ident, 0.0), (from_row, 1.0), (eye3, 0.0), (upper, 1.0), (Up, 0.0), (lower, 1.0), (eyeB, 0.0),
                         (Aw[:, :, D0:D0 + 1], 0.0)):
                pool.memset(m[:], v).then_inc(s_clear, 1)
            pool.memset(ones64[:], 1.0).then_inc(s_clear, 1)
            pool.memset(T["minus_half"][:], -0.5).then_inc(s_clear, 1)
            pool.memset(root[:], 0.5).then_inc(s_clear, 1)
            pool.wait_ge(s_clear, 11)

            def select(m, pattern, op, base, mult, fill):
                pool.affine_select(out=m, in_=m, pattern=pattern, compare_op=op, fill=fill, base=base,
                                   channel_multiplier=mult).then_inc(s_mask, 1)

            select(ident[:], [[-1, 128]], ALU.not_equal, 0, 1, 1.0)
            select(from_row[:, 0, :], [[-1, D0 + 1]], ALU.is_ge, 0, 1, 0.0)
            select(eye3[:, 0, :], [[-1, D0 + 1]], ALU.not_equal, 0, 1, 1.0)
            select(upper[:], [[1, D0]], ALU.is_gt, 0, -1, 0.0)
            select(lower[:], [[-1, D0]], ALU.is_gt, 0, 1, 0.0)
            for i in range(2):
                select(eyeB[:, i, :, :], [[0, B], [-1, D0]], ALU.not_equal, 0, 1, 1.0)
            for n in range(TAYLOR - 1):
                pool.memset(inv[:, n:n + 1], 1.0 / (TAYLOR - 1 - n)).then_inc(s_inv, 1)
                pool.wait_ge(s_inv, n + 1)
            with pool.Fori(0, D0) as k:
                pool.wait_ge(s_sc, k + 1)
                pool.tensor_tensor(nrm[:], n2[:], root[:], ALU.pow).then_inc(s_norm, 1)
                pool.wait_ge(s_vt, k + 1)
                pool.tensor_copy(Vn[:, :, bass.ds(k, 1)], vt[:].unsqueeze(2)).then_inc(s_kept, 1)
                pool.wait_ge(s_half, k + 1)
                pool.tensor_copy(crow[:, bass.ds(k, 1)], cv[:]).then_inc(s_kept, 1)
            pool.wait_ge(T["s_raw"], T["raw_count"])
            split_attention_weights(pool, T, s_whi, 0, s_wlo)

        @block.scalar
        def _(act):
            act.wait_ge(s_c, 16)
            act.activation(e1[:], cT[:], ACT.Exp, scale=-1.0).then_inc(s_e1, 1)

        @block.tensor
        def _(pe):
            free_at_start(pe, s_xt, s_dp)
            pe.wait_ge(s_sT, 1)
            pe.wait_ge(s_w, 16)
            for g in range(NG):
                for c in range(NK):
                    mm = pe.matmul(bank[2 + g][0:B, 0:GW], sT[:, c, :], Wsk[:, c, g * GW:(g + 1) * GW],
                                   start=(c == 0), stop=(c == NK - 1))
                mm.then_inc(s_skp, 1)

            def step(k):
                pe.wait_ge(s_col, k + 1)
                for c in range(NK):
                    pe.matmul(psq[0:KC, 0:D0], am[:, c:c + 1].to_broadcast([KC, KC]), Aw[:, c, 0:D0],
                              start=(c == 0), stop=(c == NK - 1))
                pe.matmul(psr[0:KC, 0:D0], ek[:, 0:1].to_broadcast([KC, KC]), Aw[:, 0, 0:D0],
                          start=True, stop=True).then_inc(s_prod, 1)

            def mods_of(l, k):
                pe.wait_ge(s_ad, 16 * (l + 1))
                with pe.Fori(0, MODS) as g:
                    step(g + k)
                    pe.wait_ge(s_mr, FREE + g + NA * l)
                    for c in range(NK):
                        mm = pe.matmul(bank[2][0:B, 0:AW], sT[:, c, :], Wad[:, c, bass.ds(g * AW, AW)],
                                       start=(c == 0), stop=(c == NK - 1))
                    mm.then_inc(s_mp, 1)
                pe.wait_ge(s_mr, FREE + NA * (l + 1))
                if l:
                    pe.wait_ge(s_md, l)
                for n, (v, c) in enumerate(IJ):
                    mm = pe.transpose(bank[6][0:KC, n * B:(n + 1) * B], mrow[:, v * C + c * KC:v * C + (c + 1) * KC],
                                      ident[0:B, 0:B])
                mm.then_inc(s_tp, 1)

            pe.wait_ge(s_p, 16)
            pe.wait_ge(s_mask, 7)
            with pe.Fori(0, WAIT_SKEW) as n:
                step(n + 0)
            pe.wait_ge(s_sv, NG)
            mods_of(0, WAIT_SKEW)
            k = WAIT_SKEW + MODS
            pe.wait_ge(s_up, 16 * (D0 - 1))
            for b in range(B):
                mm = pe.transpose(bank[3][0:D0, b * D0:(b + 1) * D0], Up[:, b, :], ident[0:D0, 0:D0])
            mm.then_inc(s_upT, 1)
            pe.wait_ge(s_abs, 1)
            pe.matmul(bank[7][0:D0, 0:B * D0], ones64[:], Ab[:].rearrange("p b j -> p (b j)"),
                      start=True, stop=True).then_inc(s_n1p, 1)
            with pe.Fori(0, HORNER // 2) as m:
                for n in range(2):
                    step(2 * m + (k + n))
                    pe.wait_ge(s_h, 2 * m + (n + 1))
                    pe.sem_inc(s_go, 1)
                    for b in range(B):
                        mm = pe.matmul(bank[4][0:D0, b * D0:(b + 1) * D0], A[:, 1, b, :], hor[:, n, b, :],
                                       start=True, stop=True)
                    mm.then_inc(s_hp, 1)
            k += HORNER
            pe.wait_ge(s_h, TAYLOR)
            for b in range(B):
                mm = pe.transpose(bank[5][0:D0, b * D0:(b + 1) * D0], hor[:, (TAYLOR - 1) % 2, b, :], ident[0:D0, 0:D0])
            mm.then_inc(s_rT, 1)
            with pe.Fori(0, SQUARES // 2) as m:
                for n in range(2):
                    step(2 * m + (k + n))
                    pe.wait_ge(s_R, 2 * m + (n + 1))
                    pe.sem_inc(s_go, 1)
                    for i in range(2):
                        for b in range(B):
                            mm = pe.matmul(bank[4][0:D0, (i * B + b) * D0:(i * B + b + 1) * D0], R[:, n, 1 - i, b, :],
                                           R[:, n, i, b, :], start=True, stop=True)
                    mm.then_inc(s_sqp, 1)
            k += SQUARES
            for l in range(1, NL):
                mods_of(l, k)
                k += MODS
            pe.wait_ge(s_md, NL)
            pe.wait_ge(s_R, NSQ + 1)
            with pe.Fori(0, XT) as b:
                step(b + k)
                pe.wait_ge(s_xs, b + 1)
                for c in range(NK):
                    pe.wait_ge(s_xT, FREE + NK * b + c)
                    for t in range(NT):
                        mm = pe.transpose(bank[4 + c][0:KC, t * 128:(t + 1) * 128], xs[:, t, c * KC:(c + 1) * KC], ident[:])
                    mm.then_inc(s_xt, 1)
            k += XT
            with pe.Fori(0, REST) as n:
                step(n + k)
            pe.wait_ge(s_kept, FREE + 2 * D0)
            pe.wait_ge(s_xT, FREE + NK * B)
            pe.wait_ge(s_md, NL)
            for c in range(NK):
                mm = pe.matmul(bank[2][0:D0, 0:D0], Vn[:, c, :], Vn[:, c, :], start=(c == 0), stop=(c == NK - 1))
            mm.then_inc(s_gp, 1)
            for c in range(NK):
                mm = pe.transpose(bank[3][0:D0, c * KC:(c + 1) * KC], Vn[:, c, :], ident[0:KC, 0:KC])
            mm.then_inc(s_vT, 1)
            for n in range(5):
                pe.wait_ge(s_X, n + 1)
                pe.matmul(bank[4][0:D0, 0:D0], Xn[:, n % 2, 1, :], Xn[:, n % 2, 0, :], start=True, stop=True)
                pe.matmul(bank[4][0:D0, D0:2 * D0], Xn[:, n % 2, 0, :], Xn[:, n % 2, 1, :], start=True, stop=True).then_inc(s_xp, 1)
                pe.wait_ge(s_X, n + 2)
                pe.wait_ge(s_PT, n + 1)
                pe.matmul(bank[5][0:D0, 0:D0], Xn[:, (n + 1) % 2, 0, :], PT[:, n % 2, :], start=True, stop=True).then_inc(s_xr, 1)
            pe.wait_ge(s_Tt, 1)
            pe.matmul(bank[6][0:D0, 0:D0], Tt[:], VT[:, 0:D0], start=True, stop=True).then_inc(s_yp, 1)
            pe.wait_ge(s_Y, 1)
            for c in range(NK):
                mm = pe.matmul(bank[7][0:KC, c * D0:(c + 1) * D0], VT[:, c * KC:(c + 1) * KC], Y[:], start=True, stop=True)
            mm.then_inc(s_up2, 1)
            pe.matmul(bank[2][0:D0, 0:C], Y[:], VT[:], start=True, stop=True).then_inc(s_up2, 1)
            pe.wait_ge(s_U, 2)
            for b in range(B):
                if b >= 2:
                    pe.wait_ge(s_F, b - 1)
                pe.matmul(bank[3 + b % 2][0:D0, 0:C], Rm[:, b, :], UT[:], start=True, stop=True).then_inc(s_fp, 1)
            def z(b):
                pe.wait_ge(s_xT, FREE + NK * B)
                for c in range(NK):
                    mm = pe.matmul(bank[7][0:D0, :], U[:, c, :], xT[:, c, tokens(b, 0, NTOK)], start=(c == 0), stop=(c == NK - 1))
                mm.then_inc(s_zp, 1)

            def delta(b):
                for t in range(NT):
                    pe.wait_ge(s_d, FREE + b * NT)
                    pe.sem_inc(s_go, 1)
                    pe.matmul(bank[t][:, 0:C], zT[:, t * 128:(t + 1) * 128], F[:, one(b), :].squeeze(1),
                              start=True, stop=True).then_inc(s_dp, 1)

            pe.wait_ge(s_F, B)
            z(0)
            with pe.Fori(0, B - 1) as b:
                pe.wait_ge(s_z, b + 1)
                z(b + 1)
                delta(b)
            pe.wait_ge(s_z, B)
            delta(B - 1)

        @block.vector
        def _(dve):
            free_at_start(dve, s_d, s_mr, s_xT)
            link = Order(dve, s_dve)
            dve.wait_ge(s_e1, 1)
            link(dve.tensor_scalar_add(e1[:], e1[:], 1.0))
            link(dve.reciprocal(e1[:], e1[:]))
            dve.wait_ge(s_c, 16)
            dve.tensor_tensor(sT[:], cT[:], e1[:], ALU.mult).then_inc(s_sT, 1)
            dve.wait_ge(s_b, 16)
            for g in range(NG):
                dve.wait_ge(s_skp, g + 1)
                dve.tensor_tensor(sv[:, g * GW:(g + 1) * GW], bank[2 + g][0:B, 0:GW], skb[:, g * GW:(g + 1) * GW],
                                  ALU.add).then_inc(s_sv, 1)
            dve.wait_ge(s_p, 16)
            dve.wait_ge(s_clear, 11)
            dve.wait_ge(s_mask, 7)

            def column(k):
                link(dve.tensor_copy(ek[:].unsqueeze(2), eye3[:, :, k]))
                dve.tensor_tensor(am[:].unsqueeze(2), Aw[:, :, k], from_row[:, :, k], ALU.mult).then_inc(s_col, 1)

            column(slice(0, 1))
            STEP = 14

            def step(link, k):
                at = bass.ds(k, 1)
                dve.wait_ge(s_prod, k + 1)
                dve.wait_ge(s_col, k + 1)
                dve.tensor_copy(n2[:], psq[0:KC, at]).then_inc(s_sc, 1)
                dve.tensor_copy(alpha[:], psr[0:KC, at]).then_inc(s_dve, 1)
                dve.tensor_scalar_add(n2g[:], psq[0:KC, at], 1e-30).then_inc(s_dve, 1)
                dve.tensor_copy(a_cols[:], psq[0:KC, 0:D0]).then_inc(s_dve, 1)
                link.pass_by(3)
                dve.wait_ge(s_dve, link.n)
                link(dve.tensor_scalar(sgn[:], alpha[:], 0.0, -2.0, ALU.is_ge, ALU.mult))
                link(dve.tensor_scalar_add(sgn[:], sgn[:], 1.0))
                link(dve.scalar_tensor_tensor(absa[:], alpha[:], -1.0, sgn[:], ALU.mult, ALU.mult))
                dve.wait_ge(s_norm, k + 1)
                dve.tensor_tensor(beta[:], sgn[:], nrm[:], ALU.mult).then_inc(s_dve, 1)
                dve.tensor_scalar(vv[:], nrm[:], absa[:, 0:1], n2g[:, 0:1], ALU.mult, ALU.add).then_inc(s_dve, 1)
                link.pass_by(2)
                dve.wait_ge(s_dve, link.n)
                dve.wait_ge(s_kept, FREE + k * 2)
                dve.reciprocal(cv[:], vv[:]).then_inc(s_half, 1)
                dve.scalar_tensor_tensor(vt[:], ek[:], beta[:, 0:1], am[:], ALU.mult, ALU.subtract).then_inc(s_vt, 1)
                dve.scalar_tensor_tensor(v_cols[:], psr[0:KC, 0:D0], beta[:, 0:1], a_cols[:], ALU.mult,
                                         ALU.subtract).then_inc(s_dve, 1)
                dve.wait_ge(s_vt, k + 1)
                dve.wait_ge(s_half, k + 1)
                dve.tensor_scalar(vc[:], vt[:], cv[:, 0:1], -1.0, ALU.mult, ALU.mult).then_inc(s_dve, 1)
                nxt = bass.ds(k + 1, 1)
                dve.tensor_copy(ek[:].unsqueeze(2), eye3[:, :, nxt]).then_inc(s_dve, 1)
                link.pass_by(3)
                dve.wait_ge(s_dve, link.n)
                for c in range(NK):
                    dve.scalar_tensor_tensor(Aw[:, c, 0:D0], v_cols[:], vc[:, c:c + 1], Aw[:, c, 0:D0], ALU.mult,
                                             ALU.add).then_inc(s_dve, 1)
                link.pass_by(NK)
                dve.wait_ge(s_dve, link.n)
                dve.tensor_tensor(am[:].unsqueeze(2), Aw[:, :, nxt], from_row[:, :, nxt], ALU.mult).then_inc(s_col, 1)

            def mods_of(l, k, start):
                dve.wait_ge(s_adb, 16 * (l + 1))
                if l:
                    dve.wait_ge(s_tp, l)
                with dve.Fori(0, MODS) as g:
                    step(Order(dve, s_dve, g * STEP + start), g + k)
                    dve.wait_ge(s_mp, g + (NA * l + 1))
                    dve.tensor_tensor(mrow[:, bass.ds(g * AW, AW)], bank[2][0:B, 0:AW], bad[:, bass.ds(g * AW, AW)],
                                      ALU.add).then_inc(s_mr, 1)
                dve.wait_ge(s_tp, l + 1)
                src = bank[6][0:KC, 0:len(IJ) * B].rearrange("p (v c b) -> p v c b", v=6, c=NK)
                for v in range(6):
                    last = dve.tensor_scalar(mods[:, l, v, :, :], src[:, v, :, :], float(v % 3 == 1), None, ALU.add)
                last.then_inc(s_md, 1)

            def steps_alone(count, k, start):
                with dve.Fori(0, count) as n:
                    step(Order(dve, s_dve, n * STEP + start), n + k)

            k, start = 0, link.n
            steps_alone(WAIT_SKEW, k, start)
            k, start = k + WAIT_SKEW, start + WAIT_SKEW * STEP
            mods_of(0, k, start)
            k, start = k + MODS, start + MODS * STEP
            link = Order(dve, s_dve, start)
            dve.wait_ge(s_upT, 1)
            t4 = bank[3][0:D0, 0:B * D0].rearrange("p (b j) -> p b j", b=B)
            link(dve.tensor_tensor(A[:, 1, :, :], t4, Up[:], ALU.subtract))
            link(dve.tensor_scalar(A[:, 0, :, :], A[:, 1, :, :], -1.0, None, ALU.mult))
            dve.tensor_tensor(Ab[:], A[:, 0, :, :], A[:, 1, :, :], ALU.max).then_inc(s_abs, 1)
            dve.wait_ge(s_n1p, 1)
            link(dve.tensor_reduce(nrm1[:], bank[7][0:D0, 0:B * D0].rearrange("p (b j) -> p b j", b=B), AX_X, ALU.max))
            for i in range(NSQ):
                last = dve.tensor_scalar(again[:, i, :], nrm1[:], float(2 ** i), None, ALU.is_gt)
            link(last)
            link(dve.tensor_scalar(halves[:], again[:], -0.5, 1.0, ALU.mult, ALU.add))
            link(dve.tensor_copy(down[:], halves[:, 0, :]))
            for i in range(1, NSQ):
                link(dve.tensor_tensor(down[:], down[:], halves[:, i, :], ALU.mult))
            for i in range(2):
                link(dve.tensor_tensor(A[:, i, :, :], A[:, i, :, :], down[:].unsqueeze(2).to_broadcast([D0, B, D0]), ALU.mult))
            eye4 = eyeB[:, 0, :, :]
            dve.wait_ge(s_mask, 7)
            dve.scalar_tensor_tensor(hor[:, 0, :, :], A[:, 0, :, :], 1.0 / TAYLOR, eye4, ALU.mult, ALU.add).then_inc(s_h, 1)
            dve.wait_ge(s_inv, TAYLOR - 1)
            start = link.n
            with dve.Fori(0, HORNER // 2) as m:
                link = Order(dve, s_dve, m * (2 * STEP) + start)
                for n in range(2):
                    step(link, 2 * m + (k + n))
                    dve.wait_ge(s_hp, 2 * m + (n + 1))
                    dve.wait_ge(s_h, 2 * m + (n + 1))
                    dve.scalar_tensor_tensor(hor[:, 1 - n, :, :], bank[4][0:D0, 0:B * D0].rearrange("p (b j) -> p b j", b=B),
                                             inv[:, one(2 * m + n)], eye4, ALU.mult, ALU.add).then_inc(s_h, 1)
            k, start = k + HORNER, start + HORNER * STEP
            link = Order(dve, s_dve, start)
            dve.wait_ge(s_h, TAYLOR)
            link(dve.tensor_copy(R[:, 0, 0, :, :], hor[:, (TAYLOR - 1) % 2, :, :]))
            dve.wait_ge(s_rT, 1)
            dve.tensor_copy(R[:, 0, 1, :, :], bank[5][0:D0, 0:B * D0].rearrange("p (b j) -> p b j", b=B)).then_inc(s_R, 1)
            start = link.n
            turn = 2 * (STEP + 3)
            with dve.Fori(0, SQUARES // 2) as m:
                link = Order(dve, s_dve, m * turn + start)
                for n in range(2):
                    step(link, 2 * m + (k + n))
                    flat = lambda x: x.rearrange("p i b j -> p (i b) j")
                    dve.wait_ge(s_sqp, 2 * m + (n + 1))
                    dve.wait_ge(s_R, 2 * m + (n + 1))
                    link(dve.tensor_tensor(flat(dif[:]), bank[4][0:D0, :].rearrange("p (n j) -> p n j", j=D0),
                                           flat(R[:, n, :, :, :]), ALU.subtract))
                    for i in range(2):
                        dve.tensor_tensor(dif[:, i, :, :], dif[:, i, :, :],
                                          again[:, bass.ds(2 * m + n, 1), :].squeeze(1).unsqueeze(2).to_broadcast([D0, B, D0]),
                                          ALU.mult).then_inc(s_dve, 1)
                    link.pass_by(2)
                    dve.wait_ge(s_dve, link.n)
                    dve.tensor_tensor(R[:, 1 - n, :, :, :], R[:, n, :, :, :], dif[:], ALU.add).then_inc(s_R, 1)
            k, start = k + SQUARES, start + SQUARES // 2 * turn
            for l in range(1, NL):
                mods_of(l, k, start)
                k, start = k + MODS, start + MODS * STEP
            dve.wait_ge(s_x, 16 * B)
            with dve.Fori(0, XT) as b:
                dve.wait_ge(s_xt, FREE + NK * b)
                dve.tensor_copy(xs[:], X[:, bass.ds(b * NT, NT), :]).then_inc(s_xs, 1)
                step(Order(dve, s_dve, b * STEP + start), b + k)
                for c in range(NK):
                    dve.wait_ge(s_xt, FREE + b * NK + c + 1)
                    dve.tensor_copy(xT[:, c, tokens(b, 0, NTOK)], bank[4 + c][0:KC, :]).then_inc(s_xT, 1)
            k, start = k + XT, start + XT * STEP
            steps_alone(REST, k, start)
            link = Order(dve, s_dve, start + REST * STEP)
            dve.wait_ge(s_R, NSQ + 1)
            link(dve.tensor_tensor(Rm[:], R[:, NSQ % 2, 1, :, :], eye4, ALU.subtract))
            dve.wait_ge(s_kept, FREE + 2 * D0)
            dve.wait_ge(s_mask, 7)
            link(dve.tensor_tensor(cdia[:], crow[0:D0, :], ident[0:D0, 0:D0], ALU.mult))
            link(dve.tensor_reduce(ccol[:], cdia[:], AX_X, ALU.add))
            dve.wait_ge(s_gp, 1)
            gram = bank[2][0:D0, 0:D0]
            link(dve.tensor_tensor(cdia[:], gram, crow[0:D0, :], ALU.mult))
            link(dve.tensor_tensor(Xn[:, 0, 1, :], cdia[:], lower[:], ALU.mult))
            link(dve.tensor_tensor(PT[:, 0, :], ident[0:D0, 0:D0], Xn[:, 0, 1, :], ALU.subtract))
            dve.scalar_tensor_tensor(Xn[:, 0, 0, :], gram, ccol[:, 0:1], upper[:], ALU.mult, ALU.mult).then_inc(s_X, 1)
            dve.wait_ge(s_vT, 1)
            dve.tensor_copy(VT[:], bank[3][0:D0, 0:C]).then_inc(s_PT, 1)
            for n in range(5):
                dve.wait_ge(s_xp, n + 1)
                dve.tensor_copy(Xn[:, (n + 1) % 2, :, :], bank[4][0:D0, 0:2 * D0].rearrange("p (i j) -> p i j", i=2)).then_inc(s_X, 1)
                dve.wait_ge(s_xr, n + 1)
                dve.wait_ge(s_PT, n + 1)
                dve.tensor_tensor(PT[:, (n + 1) % 2, :], bank[5][0:D0, 0:D0], PT[:, n % 2, :], ALU.add).then_inc(s_PT, 1)
            dve.wait_ge(s_PT, 6)
            dve.tensor_scalar(Tt[:], PT[:, 1, :], ccol[:, 0:1], None, ALU.mult).then_inc(s_Tt, 1)
            dve.wait_ge(s_yp, 1)
            dve.tensor_copy(Y[:], bank[6][0:D0, 0:D0]).then_inc(s_Y, 1)
            dve.wait_ge(s_up2, 2)
            dve.tensor_tensor(U[:], eye3[:, :, 0:D0], bank[7][0:KC, 0:NK * D0].rearrange("p (c d) -> p c d", c=NK),
                              ALU.subtract).then_inc(s_U, 1)
            link(dve.tensor_scalar(UT[:], bank[2][0:D0, 0:C], -1.0, None, ALU.mult))
            dve.tensor_tensor(UT[:, 0:D0], UT[:, 0:D0], ident[0:D0, 0:D0], ALU.add).then_inc(s_U, 1)
            for b in range(B):
                dve.wait_ge(s_fp, b + 1)
                dve.tensor_copy(F[:, b, :], bank[3 + b % 2][0:D0, 0:C]).then_inc(s_F, 1)
            with dve.Fori(0, B) as b:
                dve.wait_ge(s_zp, b + 1)
                dve.wait_ge(s_dp, FREE + b * NT)
                dve.tensor_copy(zT[:], bank[7][0:D0, :]).then_inc(s_z, 1)
                for t in range(NT):
                    xt = X[:, one(b * NT + t), :].squeeze(1)
                    dve.wait_ge(s_dp, FREE + b * NT + t + 1)
                    dve.tensor_tensor(xt, xt, bank[t][:, 0:C], ALU.add).then_inc(s_d, 1)


HD_ROWS = [6 * D, 5 * D, 5 * D]
QK_OFF = [0, 6 * D, 11 * D]
NPARTS = NK * (2 * NK + 1)
NTRI = 6
PRODUCTS = [(0, 0), (0, 1), (0, 2), (1, 0), (1, 1), (2, 0)]
KS_ROWS = len(PRODUCTS) * D
LEAD = 6
SPLITS = [(0, 0), (1, 0), (0, 1)]


class Uses:

    def __init__(self, banks, turns=0, k=0):
        self.banks, self.turns, self.k = banks, turns, k

    @property
    def n(self):
        return self.turns + self.k

    @property
    def bank(self):
        return self.banks[self.k % 2]


def attention_half(nc, io, T, l):
    X, ident, mods = T["x"], T["ident"], T["mods"]
    with nc.cleanup_on_exit(), ExitStack() as ctx:
        def sb(name, shape, dt=F32):
            return ctx.enter_context(nc.sbuf_tensor(f"a{l}_{name}", shape, dt))

        def ps(name, shape=(128, 512)):
            return ctx.enter_context(nc.psum_tensor(f"a{l}_{name}", list(shape), F32))

        def sem(name):
            return nc.alloc_semaphore(f"a{l}_{name}")

        W = T["w_att"]
        qkb = sb("qk_bias", [6 * D, 2, NK])
        bv = sb("v_bias", [128, C])
        bp = sb("proj_bias", [128, C])
        st6 = sb("ln_stats", [128, NT, 6])
        mv = sb("ln_mean_var", [128, NT, 2])
        ve = sb("ln_var_eps", [128, NT])
        rstd = sb("ln_rstd", [128, NT])
        xn = sb("normalized", [128, NT, C])
        hT = sb("h_parts", [KC, 2, NK, NTOK], F16)
        v32 = sb("h_or_qk32", [6 * D, 2, NTOK])
        rest = sb("h_or_qk_rest", [6 * D, NTOK])
        PT3 = sb("qk_parts", [6 * D, 2, NK, 3, NTOK], BF16)
        Vn = sb("v_next", [128, NT, H, D])
        V = sb("v_with_ones", [128, NT, H, 32])
        QS = sb("q_stack", [128, 2, H, NTOK], BF16)
        KS = sb("k_stack", [128, 2, H, NTOK], BF16)
        MX = sb("minus_max", [128, 2, 16])
        MT = sb("minus_max_T", [16, 2, 128], BF16)
        E = sb("exp_scores", [128, 2, 4, NTOK])
        oT = sb("o_T", [128, 4, NTOK])
        rs = sb("sum_inverse", [128, H])
        on = sb("o_normalized", [128, 2, C])
        oP = sb("o_parts", [KC, 2, 2, NK, 128], F16)
        gcol = sb("gate_of_batch", [KC, NK])
        gbc = sb("gate_rows", [128, C])
        st_banks = [ps(f"st{i}") for i in range(2)]
        mx_banks = [ps(f"mx{i}") for i in range(2)]
        dd_banks = [ps(f"dd{i}") for i in range(2)]
        av = [ps(f"av{i}") for i in range(2)]

        s_small, s_w, s_set = sem("biases_in"), sem("w1_split"), sem("constants_set")
        s_dve, s_var, s_rstd, s_xn = sem("dve_order"), sem("var_ready"), sem("rstd_ready"), sem("xn_ready")
        s_h, s_part, s_V, s_go = sem("h_ready"), sem("qk_parts_ready"), sem("v_ready"), sem("waits_taken")
        s_stk = [sem(f"stack{i}_loaded") for i in range(NTRI)]
        s_st, s_str = sem("st_written"), sem("st_read")
        s_mm, s_mmr = sem("mx_written"), sem("mx_read")
        s_dd, s_ddr = sem("dd_written"), sem("dd_read")
        s_mt, s_md, s_av, s_oT = sem("max_T_ready"), sem("max_row_loaded"), sem("av_unit_done"), sem("o_T_ready")
        s_hi = sem("w1_high")
        s_g, s_O, s_oh = sem("gate_picked"), sem("o_tokens_ready"), sem("o_parts_ready")
        block = ctx.enter_context(nc.Block())

        QKV_ST, QKV_DD = 8, 5
        ATT_ST, ATT_MM, ATT_DD = 4 * H, 4 * H, 1 + 4
        PROJ_MM, PROJ_DD = 2 * NT, NT
        TURN_ST, TURN_MM, TURN_DD = QKV_ST + ATT_ST, ATT_MM + PROJ_MM, QKV_DD + ATT_DD + PROJ_DD
        BEFORE_ST, BEFORE_MM, BEFORE_DD = 2 * QKV_ST, 4 * LEAD, 2 * QKV_DD + 1

        @block.sync
        def _(sp):
            load_w1(sp, io, T["staging"], T["mlp_of"][l][0], T["s_raw"])
            sp.dma_start(qkb[:], io[f"qk_b{l}"]).then_inc(s_small, 16)
            sp.dma_start(bv[:], io[f"qkv_b{l}"][2 * C:3 * C].partition_broadcast(128)).then_inc(s_small, 16)
            sp.dma_start(bp[:], io[f"proj_b{l}"].partition_broadcast(128)).then_inc(s_small, 16)

            def stacks(i):
                sp.wait_ge(s_part, 6 * i + 6)
                if not isinstance(i, int):
                    sp.wait_ge(s_st, BEFORE_ST + TURN_ST * (i - 2) + ATT_ST)
                for s in range(NTRI):
                    n = min(3, H - 3 * s)
                    for side, S in ((1, KS), (0, QS)):
                        for r, pq in enumerate(PRODUCTS):
                            sp.dma_start(S[r * D:(r + 1) * D, one(i % 2), 3 * s:3 * s + n, :].squeeze(1),
                                         PT3[s * D:(s + 1) * D, side, 0:n, pq[side], :]).then_inc(s_stk[s], 16)

            sp.wait_ge(s_set, 3)
            stacks(0)
            stacks(1)
            with sp.Fori(0, B - 2) as i:
                stacks(i + 2)
            sp.wait_ge(s_w, 1)
            load_w2(sp, io, T["staging"], T["mlp_of"][l][0], T["s_raw"])

        w1_raw = T["raw_count"] + 16
        T["raw_count"] += 32

        @block.gpsimd
        def _(pool):
            def rsqrt(i):
                pool.wait_ge(s_var, i + 1)
                pool.tensor_tensor(rstd[:], ve[:], T["minus_half"][:], ALU.pow).then_inc(s_rstd, 1)
                pool.wait_ge(s_rstd, i + 1)

            rsqrt(0)
            for i in range(2):
                pool.memset(KS[96:KS_ROWS + 1, i, :, :], 1.0).then_inc(s_set, 1)
                pool.wait_ge(s_set, i + 1)
            pool.memset(V[:], 1.0).then_inc(s_set, 1)
            pool.wait_ge(s_set, 3)

            def max_row(i, g):
                pool.wait_ge(s_mt, 4 * i + g + 1)
                pool.sem_inc(s_go, 1)
                pool.dma_start(QS[KS_ROWS:KS_ROWS + 1, one(i % 2), 4 * g:4 * g + 4, :].squeeze(1),
                               MT[:, g % 2, :]).then_inc(s_md, 16)

            rsqrt(1)
            max_row(0, 0)
            pool.wait_ge(T["s_raw"], w1_raw)
            split_w1(pool, T["staging"], T["w1_parts"], s_hi, 0, s_w)
            with pool.Fori(0, B - 2) as i:
                for g in (1, 2):
                    max_row(i, g)
                rsqrt(i + 2)
                max_row(i, 3)
                max_row(i + 1, 0)
            for i in (B - 2, B - 1):
                for g in range(0 if i == B - 1 else 1, 4):
                    max_row(i, g)
            pool.wait_ge(s_md, 16 * 4 * B)

        @block.scalar
        def _(act):
            free_at_start(act, s_oT, s_str)

            def qkv(i, st):
                act.wait_ge(s_small, 48)
                for n, c in enumerate((0, 2)):
                    act.wait_ge(s_st, st.n + 1)
                    if not first(i):
                        act.wait_ge(s_part, 6 * i)
                    act.activation(v32[0:KC, n, :], st.bank[0:KC, :], ACT.Identity, bias=mods[:, l, 0, c, one(i)],
                                   scale=mods[:, l, 1, c, one(i)]).then_inc(s_str, 1)
                    st.k += 1
                for n in range(6):
                    side, c = 1 - n // NK, n % NK
                    M = HD_ROWS[c]
                    act.wait_ge(s_st, st.n + 1)
                    if n < 2:
                        act.wait_ge(s_h, NK * i + 1 + 2 * n)
                    else:
                        act.wait_ge(s_part, 6 * i + n - 1)
                    act.activation(v32[0:M, n % 2, :], st.bank[0:M, :], ACT.Identity, bias=qkb[0:M, side, c:c + 1],
                                   scale=1.0 / WS).then_inc(s_str, 1)
                    st.k += 1

            def attend(i, st):
                for U in range(16):
                    for hd in range(4):
                        act.wait_ge(s_av, FREE + 16 * i + max(0, U - 1))
                        act.wait_ge(s_st, st.n + 1)
                        act.activation(E[:, U % 2, hd, :], st.bank[:], ACT.Exp, scale=float(D) ** -0.5).then_inc(s_str, 1)
                        st.k += 1
                    if U % 4 == 1 and U > 1:
                        o_group(i, U // 4 - 1)
                o_group(i, 3)

            def o_group(i, g):
                act.wait_ge(s_av, FREE + 16 * i + 4 * g + 4)
                act.activation(oT[:, g, :], av[g % 2][:], ACT.Copy).then_inc(s_oT, 1)

            st = Uses(st_banks)
            qkv(0, st)
            qkv(1, st)
            with act.Fori(0, B - 2) as i:
                st = Uses(st_banks, TURN_ST * i, BEFORE_ST)
                attend(i, st)
                qkv(i + 2, st)
            st = Uses(st_banks, 0, BEFORE_ST + (B - 2) * TURN_ST)
            attend(B - 2, st)
            attend(B - 1, st)

        @block.tensor
        def _(pe):
            free_at_start(pe, s_av)

            def dense(out, lhs, rhs, sem_):
                n = 0
                for c in range(NK):
                    for a, w in SPLITS:
                        mm = pe.matmul(out, lhs(c, a, w), rhs(c, a, w), start=(n == 0), stop=(n == 3 * NK - 1))
                        n += 1
                mm.then_inc(sem_, 1)

            def h_chunk(i, c, use, written, read):
                pe.wait_ge(s_xn, NT * (i + 1))
                pe.wait_ge(read, FREE + use.n - 1)
                for t in range(NT):
                    mm = pe.transpose(use.bank[0:KC, t * 128:(t + 1) * 128], xn[:, t, c * KC:(c + 1) * KC], ident[:])
                mm.then_inc(written, 1)
                use.k += 1

            def qk_tile(i, n, st):
                pe.wait_ge(s_h, NK * (i + 1))
                pe.wait_ge(s_str, FREE + st.n - 1)
                side, c = 1 - n // NK, n % NK
                to = side * C + QK_OFF[c]
                dense(st.bank[0:HD_ROWS[c], :], lambda k, a, w: W[:, w, k, to:to + HD_ROWS[c]],
                      lambda k, a, w: hT[:, a, k, :], s_st)
                st.k += 1

            def v_tile(t, dd):
                pe.wait_ge(s_ddr, FREE + dd.n - 1)
                dense(dd.bank[:, 0:C], lambda k, a, w: hT[:, a, k, t * 128:(t + 1) * 128],
                      lambda k, a, w: W[:, w, k, 2 * C:3 * C], s_dd)
                dd.k += 1

            def by_token(i, t, mm):
                pe.wait_ge(s_oT, FREE + 4 * (i + 1))
                pe.wait_ge(s_mmr, FREE + mm.n - 1)
                for g in range(4):
                    tr = pe.transpose(mm.bank[:, g * 128:(g + 1) * 128], oT[:, g, t * 128:(t + 1) * 128], ident[:])
                tr.then_inc(s_mm, 1)
                mm.k += 1

            def by_channel(i, t, mm):
                pe.wait_ge(s_O, NT * i + t + 1)
                pe.wait_ge(s_mmr, FREE + mm.n - 1)
                for c in range(NK):
                    tr = pe.transpose(mm.bank[0:KC, c * 128:(c + 1) * 128], on[:, t % 2, c * KC:(c + 1) * KC], ident[:])
                tr.then_inc(s_mm, 1)
                mm.k += 1

            def proj_tile(i, t, dd):
                pe.wait_ge(s_oh, NT * i + t + 1)
                pe.wait_ge(s_ddr, FREE + dd.n - 1)
                dense(dd.bank[:, 0:C], lambda k, a, w: oP[:, t % 2, a, k, :], lambda k, a, w: W[:, w, k, 3 * C:4 * C], s_dd)
                dd.k += 1

            def scores_for_max(i, h, t, mm):
                if t == 0:
                    pe.wait_ge(s_stk[h // 3], 16 * 12 * (i + 1))
                pe.wait_ge(s_mmr, FREE + mm.n - 1)
                pe.matmul(mm.bank[:], QS[0:KS_ROWS, one(i % 2), h, t * 128:(t + 1) * 128].squeeze(1),
                          KS[0:KS_ROWS, one(i % 2), h, :].squeeze(1), start=True, stop=True).then_inc(s_mm, 1)
                mm.k += 1

            def transpose_maxima(g, taken, dd):
                pe.wait_ge(s_mmr, FREE + taken)
                pe.wait_ge(s_ddr, FREE + dd.n - 1)
                pe.transpose(dd.bank[0:16, 0:128], MX[:, g % 2, :], ident[:]).then_inc(s_dd, 1)
                dd.k += 1

            def attend(i, st, mm, dd, last):
                pe.wait_ge(s_g, i + 1)
                pe.wait_ge(s_ddr, FREE + dd.n - 1)
                for c in range(NK):
                    m = pe.matmul(dd.bank[:, c * KC:(c + 1) * KC], gcol[:, c:c + 1].to_broadcast([KC, 128]),
                                  ident[0:KC, 0:KC], start=True, stop=True)
                m.then_inc(s_dd, 1)
                dd.k += 1
                pe.wait_ge(s_V, i + 1)
                st0 = st.n
                for U in range(17):
                    g, j = U // 4, U % 4
                    hm = U + LEAD
                    more = U < 16 and (hm < H or not last)
                    for hd in range(4):
                        h = 4 * g + hd
                        if U < 16:
                            if j == 0 and hd == 0:
                                pe.wait_ge(s_md, 16 * (4 * i + g + 1))
                                pe.wait_ge(s_stk[(h + 3) // 3], 16 * 12 * (i + 1))
                            pe.wait_ge(s_str, FREE + st.n - 1)
                            pe.matmul(st.bank[:], KS[0:KS_ROWS + 1, one(i % 2), h, j * 128:(j + 1) * 128].squeeze(1),
                                      QS[0:KS_ROWS + 1, one(i % 2), h, :].squeeze(1), start=True, stop=True).then_inc(s_st, 1)
                            st.k += 1
                        if more:
                            scores_for_max(i + hm // H, hm % H, hd, mm)
                        if U > 0:
                            g1, j1 = (U - 1) // 4, (U - 1) % 4
                            if j1 == 0 and hd == 0:
                                pe.wait_ge(s_oT, FREE + 4 * i + max(0, g1 - 1))
                            pe.wait_ge(s_str, FREE + st0 + 4 * (U - 1) + hd + 1)
                            m = pe.matmul(av[g1 % 2][32 * hd:32 * hd + 32, :], V[:, j1, 4 * g1 + hd, :],
                                          E[:, (U - 1) % 2, hd, :], start=(j1 == 0), stop=(j1 == 3))
                        if hd == 2 and U < 16 and (hm - 1) % 4 == 3 and (hm - 1 < H or not last):
                            transpose_maxima((hm - 1) // 4, mm.n - (3 if more else 0), dd)
                    if U > 0:
                        m.then_inc(s_av, 1)

            def between(done, new, st, mm, dd):
                if new is not None:
                    h_chunk(new, 0, st, s_st, s_str)
                    h_chunk(new, 1, dd, s_dd, s_ddr)
                    h_chunk(new, 2, st, s_st, s_str)
                if done is not None:
                    by_token(done, 0, mm)
                    by_token(done, 1, mm)
                for n in range(6):
                    if new is not None:
                        qk_tile(new, n, st)
                    if done is not None and 1 <= n < 1 + NT:
                        proj_tile(done, n - 1, dd)
                    if done is not None and n < NT:
                        by_channel(done, n, mm)
                        if n < 2:
                            by_token(done, n + 2, mm)
                    if new is not None and n < NT:
                        v_tile(n, dd)

            st, mm, dd = Uses(st_banks), Uses(mx_banks), Uses(dd_banks)
            between(None, 0, st, mm, dd)
            for h in range(LEAD):
                for t in range(4):
                    scores_for_max(0, h, t, mm)
                if h == 4:
                    transpose_maxima(0, 16, dd)
            between(None, 1, st, mm, dd)
            with pe.Fori(0, B - 2) as i:
                st, mm = Uses(st_banks, TURN_ST * i, BEFORE_ST), Uses(mx_banks, TURN_MM * i, BEFORE_MM)
                dd = Uses(dd_banks, TURN_DD * i, BEFORE_DD)
                attend(i, st, mm, dd, False)
                between(i, i + 2, st, mm, dd)
            st = Uses(st_banks, 0, BEFORE_ST + (B - 2) * TURN_ST)
            mm = Uses(mx_banks, 0, BEFORE_MM + (B - 2) * TURN_MM)
            dd = Uses(dd_banks, 0, BEFORE_DD + (B - 2) * TURN_DD)
            attend(B - 2, st, mm, dd, False)
            between(B - 2, None, st, mm, dd)
            attend(B - 1, st, mm, dd, True)
            between(B - 1, None, st, mm, dd)

        @block.vector
        def _(dve):
            free_at_start(dve, s_mmr, s_ddr)

            def split16(link, hi, lo, src):
                link(dve.tensor_copy(hi, src))
                return dve.tensor_tensor(lo, src, hi, ALU.subtract)

            def norm(link, i):
                for t in range(NT):
                    link(dve.bn_stats(st6[:, t, :], X[:, one(i * NT + t), :].squeeze(1)))
                dve.sem_inc(s_go, 1)
                for t in range(NT):
                    dve.bn_aggr(mv[:, t, :], st6[:, t, :]).then_inc(s_dve, 1)
                link.pass_by(NT)
                dve.wait_ge(s_dve, link.n)
                dve.tensor_scalar_add(ve[:], mv[:, :, 1:2].squeeze(2), EPS).then_inc(s_var, 1)

            def normalize(i):
                dve.wait_ge(s_rstd, i + 1)
                for t in range(NT):
                    dve.tensor_scalar(xn[:, t, :], X[:, one(i * NT + t), :].squeeze(1), mv[:, t, 0:1], rstd[:, t:t + 1],
                                      ALU.subtract, ALU.mult).then_inc(s_xn, 1)

            def modulated(link, i, st, dd):
                for n, c in enumerate((0, 1, 2)):
                    src = v32[0:KC, c // 2, :]
                    if c == 1:
                        src = rest[0:KC, :]
                        dve.wait_ge(s_dd, dd.n + 1)
                        dve.tensor_scalar(src, dd.bank[0:KC, :], mods[:, l, 1, c, one(i)], mods[:, l, 0, c, one(i)],
                                          ALU.mult, ALU.add).then_inc(s_ddr, 1)
                        dve.wait_ge(s_ddr, FREE + dd.n + 1)
                        dd.k += 1
                    else:
                        dve.wait_ge(s_str, FREE + st.n + 1)
                        st.k += 1
                    split16(link, hT[:, 0, c, :], hT[:, 1, c, :], src).then_inc(s_h, 1)

            def qk_split(link, i, n, st):
                side, c = 1 - n // NK, n % NK
                M = HD_ROWS[c]
                src = v32[0:M, n % 2, :]
                P = lambda p: PT3[0:M, side, c, p, :]
                dve.wait_ge(s_str, FREE + st.n + 1)
                st.k += 1
                link(dve.tensor_copy(P(0), src))
                link(dve.tensor_tensor(rest[0:M, :], src, P(0), ALU.subtract))
                link(dve.tensor_copy(P(1), rest[0:M, :]))
                dve.tensor_tensor(P(2), rest[0:M, :], P(1), ALU.subtract).then_inc(s_part, 1)
                dve.wait_ge(s_part, 6 * i + n + 1)

            def v_rows(t, dd):
                dve.wait_ge(s_dd, dd.n + 1)
                dve.scalar_tensor_tensor(Vn[:, t, :, :].rearrange("p h d -> p (h d)"), dd.bank[:, 0:C], 1.0 / WS, bv[:],
                                         ALU.mult, ALU.add).then_inc(s_ddr, 1)
                dd.k += 1

            def take_max(i, h, t, mm):
                dve.wait_ge(s_mm, mm.n + 1)
                at0 = 4 * (h % 4) + t
                dve.tensor_reduce(MX[:, h // 4 % 2, at0:at0 + 1], mm.bank[:], AX_X, ALU.max, negate=True).then_inc(s_mmr, 1)
                mm.k += 1

            def maxima_row(i, g, dd):
                dve.wait_ge(s_dd, dd.n + 1)
                if not first(i):
                    dve.wait_ge(s_md, 16 * (4 * i + max(1, g - 1)))
                dve.tensor_copy(MT[:, g % 2, :], dd.bank[0:16, 0:128]).then_inc(s_mt, 1)
                dve.wait_ge(s_mt, 4 * i + g + 1)
                dve.sem_inc(s_ddr, 1)
                dd.k += 1

            def attend(link, i, mm, dd, last, new=None):
                dve.wait_ge(s_dd, dd.n + 1)
                dve.tensor_copy(gbc[:], dd.bank[:, 0:C]).then_inc(s_ddr, 1)
                dd.k += 1
                for U in range(16):
                    hm = U + LEAD
                    if new is not None and U == 9:
                        norm(link, new)
                    if new is not None and U == 10:
                        normalize(new)
                    for hd in range(4):
                        if hm < H or not last:
                            take_max(i + hm // H, hm % H, hd, mm)
                        if hd == 2 and (hm - 1) % 4 == 3 and (hm - 1 < H or not last):
                            maxima_row(i, (hm - 1) // 4, dd)

            def values_and_gate(i):
                if not first(i):
                    dve.wait_ge(s_av, FREE + 16 * i)
                dve.tensor_copy(V[:, :, :, 0:D], Vn[:]).then_inc(s_V, 1)
                dve.wait_ge(s_V, i + 1)
                dve.tensor_copy(gcol[:], mods[:, l, 2, :, one(i)].squeeze(2)).then_inc(s_g, 1)

            def o_rows(link, i, t, mm):
                o = mm.bank[:].rearrange("p (h e) -> p h e", e=32)
                dve.wait_ge(s_mm, mm.n + 1)
                link(dve.reciprocal(rs[:], o[:, :, D:D + 1].squeeze(2)))
                dve.tensor_tensor(on[:, t % 2, :].rearrange("p (h d) -> p h d", d=D), o[:, :, 0:D],
                                  rs[:].unsqueeze(2).to_broadcast([128, H, D]), ALU.mult).then_inc(s_O, 1)
                dve.wait_ge(s_O, NT * i + t + 1)
                dve.sem_inc(s_mmr, 1)
                mm.k += 1

            def o_split(link, i, t, mm):
                dve.wait_ge(s_mm, mm.n + 1)
                src = mm.bank[0:KC, 0:NK * 128].rearrange("p (c n) -> p c n", c=NK)
                split16(link, oP[:, t % 2, 0, :, :], oP[:, t % 2, 1, :, :], src).then_inc(s_oh, 1)
                dve.wait_ge(s_oh, NT * i + t + 1)
                dve.sem_inc(s_mmr, 1)
                mm.k += 1

            def update(link, i, t, dd):
                y = xn[:, t, :]
                dve.wait_ge(s_dd, dd.n + 1)
                dve.scalar_tensor_tensor(y, dd.bank[:, 0:C], 1.0 / WS, bp[:], ALU.mult, ALU.add).then_inc(s_ddr, 1)
                dve.wait_ge(s_ddr, FREE + dd.n + 1)
                dd.k += 1
                link(dve.tensor_tensor(y, y, gbc[:], ALU.mult))
                xt = X[:, one(i * NT + t), :].squeeze(1)
                link(dve.tensor_tensor(xt, xt, y, ALU.add))

            def between(link, done, new, st, mm, dd):
                if new is not None:
                    modulated(link, new, st, dd)
                if done is not None:
                    o_rows(link, done, 0, mm)
                    o_rows(link, done, 1, mm)
                if new is not None and not first(new):
                    for s in range(NTRI):
                        dve.wait_ge(s_stk[s], 16 * 12 * new)
                for n in range(6):
                    if new is not None:
                        qk_split(link, new, n, st)
                    if done is not None and 1 <= n < 1 + NT:
                        update(link, done, n - 1, dd)
                    if done is not None and n < NT:
                        o_split(link, done, n, mm)
                        if n < 2:
                            o_rows(link, done, n + 2, mm)
                    if new is not None and n < NT:
                        v_rows(n, dd)

            dve.wait_ge(s_small, 48)
            link = Order(dve, s_dve)
            st, mm, dd = Uses(st_banks), Uses(mx_banks), Uses(dd_banks)
            norm(link, 0)
            normalize(0)
            between(link, None, 0, st, mm, dd)
            norm(link, 1)
            normalize(1)
            for h in range(LEAD):
                for t in range(4):
                    take_max(0, h, t, mm)
                if h == 4:
                    maxima_row(0, 0, dd)
            dve.wait_ge(s_set, 3)
            values_and_gate(0)
            between(link, None, 1, st, mm, dd)
            before, turn = link.n, 8 + 3 + 18 + NT * (1 + 1 + 2)
            with dve.Fori(0, B - 2) as i:
                link = Order(dve, s_dve, i * turn + before)
                st, mm = Uses(st_banks, TURN_ST * i, BEFORE_ST + ATT_ST), Uses(mx_banks, TURN_MM * i, BEFORE_MM)
                dd = Uses(dd_banks, TURN_DD * i, BEFORE_DD)
                attend(link, i, mm, dd, False, i + 2)
                values_and_gate(i + 1)
                between(link, i, i + 2, st, mm, dd)
            link = Order(dve, s_dve, before + (B - 2) * turn)
            mm = Uses(mx_banks, 0, BEFORE_MM + (B - 2) * TURN_MM)
            dd = Uses(dd_banks, 0, BEFORE_DD + (B - 2) * TURN_DD)
            attend(link, B - 2, mm, dd, False)
            values_and_gate(B - 1)
            between(link, B - 2, None, None, mm, dd)
            attend(link, B - 1, mm, dd, True)
            between(link, B - 1, None, None, mm, dd)


def one(n):
    return slice(n, n + 1) if isinstance(n, int) else bass.ds(n, 1)


def first(i):
    return isinstance(i, int) and i == 0


def mlp_half(nc, io, T, l):
    X, ident, mods = T["x"], T["ident"], T["mods"]
    passes = T["mlp_of"][l]
    routed = len(passes) > 1
    with nc.cleanup_on_exit(), ExitStack() as ctx:
        def sb(name, shape, dt=F32):
            return ctx.enter_context(nc.sbuf_tensor(f"m{l}_{name}", shape, dt))

        def ps(name):
            return ctx.enter_context(nc.psum_tensor(f"m{l}_{name}", [128, 512], F32))

        def sem(name):
            return nc.alloc_semaphore(f"m{l}_{name}")

        W1 = [T["w1_parts"]] + ([sb("w1_odd", [KC, 2, NK, FF], F16)] if routed else [])
        W2 = [sb("w2_even", [128, 2, NF, C], F16)] + ([sb("w2_odd", [128, 2, NF, C], F16)] if routed else [])
        raw1 = T["staging"]
        raw2 = sb("w2_raw", [128, NF * C]) if routed else None
        b1 = sb("b1", [128, len(passes), NF])
        b2 = sb("b2_rows", [128, len(passes), C])
        st6 = sb("ln_stats", [128, NT, 6])
        mv = sb("ln_mean_var", [128, NT, 2])
        ve = sb("ln_var_eps", [128, NT])
        rstd = sb("ln_rstd", [128, NT])
        xn = sb("normalized", [128, NT, C])
        h32 = sb("h32", [KC, NTOK])
        hT = sb("h_parts", [KC, 2, NK, B * NTOK], F16)
        gcol = sb("gate_of_batch", [KC, NK])
        gbc = sb("gate_rows", [128, B, C])
        g32 = sb("hidden32", [128, 2, NTOK])
        Hs = sb("hidden_parts", [128, 2, 3, NTOK], F16)
        y = sb("branch", [128, C])
        wg = sb("router_w", [KC, NK, NE])
        wgs = sb("router_w_parts", [KC, 2, NK, NE], F16)
        lg = sb("logits", [128, NT, NE])
        cmp = sb("beaten_by", [128, NT, NE, NE])
        rank = sb("rank", [128, NT, NE])
        sel = sb("selected", [128, NT, NE])
        tot = sb("half_total", [128, NT])
        arg = sb("sigmoid_arg", [128, NT, NE])
        cw = sb("expert_weight", [128, B * NT, NE])
        hb = [ps(f"hidden{i}") for i in range(3)]
        ob = [ps(f"out{t}") for t in range(NT)]
        DD = ps("dd")

        s_small, s_raw2, s_w1, s_w2 = sem("biases_in"), sem("w2_raw_in"), sem("w1_split"), sem("w2_split")
        s_dve, s_var, s_rstd, s_xn, s_h = (sem("dve_order"), sem("var_ready"), sem("rstd_ready"),
                                                   sem("xn_ready"), sem("h_ready"))
        s_dd, s_ddev, s_g, s_th, s_arg, s_cw = (sem("dd_written"), sem("dd_read"), sem("gate_picked"), sem("tanh_ready"),
                                                sem("arg_ready"), sem("weights_ready"))
        s_hb, s_gelu, s_hs, s_out, s_ob = (sem("hidden_written"), sem("gelu_done"), sem("hidden_split"), sem("out_added"),
                                                sem("out_read"))
        s_hi, s_wlo = sem("weights_high"), sem("attention_weights_split")
        s_wgs, s_clr, s_go = sem("router_w_split"), sem("cleared"), sem("waits_taken")
        block = ctx.enter_context(nc.Block())
        DDL = NK + 1 + (1 if routed else 0)
        PE_STEPS, DVE_STEPS = (2, 4, 6, 7, 8), (0, 1, 3, 5, 7, 8)
        base_raw = T["raw_count"]

        @block.sync
        def _(sp):
            for n, m in enumerate(passes):
                sp.dma_start(b1[:, n, :], io[f"b1_{m}"]).then_inc(s_small, 16)
                sp.dma_start(b2[:, n, :], io[f"b2_{m}"].partition_broadcast(128)).then_inc(s_small, 16)
            if routed:
                sp.dma_start(wg[:], io["gate_w"].rearrange("(c p) n -> p c n", p=KC)).then_inc(s_small, 16)
            for n, m in enumerate(passes[1:], 1):
                if n == 1:
                    sp.wait_ge(s_w2, NF)
                else:
                    sp.wait_ge(s_w1, n - 1)
                load_w1(sp, io, raw1, m, T["s_raw"])
                if n > 1:
                    sp.wait_ge(s_w2, NF * n)
                load_w2(sp, io, raw2, m, s_raw2)
            if l + 1 < NL:
                if routed:
                    sp.wait_ge(s_w1, len(passes) - 1)
                else:
                    sp.wait_ge(s_w2, NF)
                load_attention_weights(sp, io, T, l + 1)

        T["raw_count"] = base_raw + 16 * (len(passes) - 1) + (32 if l + 1 < NL else 0)

        @block.gpsimd
        def _(pool):
            if routed:
                pool.memset(cmp[:], 0.0).then_inc(s_clr, 1)

            def rsqrt(i):
                pool.wait_ge(s_var, i + 1)
                pool.tensor_tensor(rstd[:], ve[:], T["minus_half"][:], ALU.pow).then_inc(s_rstd, 1)

            rsqrt(0)
            pool.wait_ge(T["s_raw"], base_raw)
            split_w2(pool, raw1, W2[0], s_hi, 0, s_w2)
            for i in range(1, B):
                rsqrt(i)
            done = NF
            for n in range(1, len(passes)):
                if n >= 2:
                    pool.wait_ge(s_out, FREE + NF * B * (n - 1))
                pool.wait_ge(T["s_raw"], base_raw + 16 * n)
                split_w1(pool, raw1, W1[n % 2], s_hi, done, s_w1)
                pool.wait_ge(s_raw2, 16 * n)
                split_w2(pool, raw2, W2[n % 2], s_hi, done + 1, s_w2)
                done += 1 + NF
            if l + 1 < NL:
                pool.wait_ge(T["s_raw"], T["raw_count"])
                split_attention_weights(pool, T, s_hi, done, s_wlo)

        @block.scalar
        def _(act):
            free_at_start(act, s_gelu)
            act.wait_ge(s_small, 32 * len(passes) + (16 if routed else 0))

            def hidden(n, i):
                k = (n * B + i) * NF
                for f in range(NF):
                    act.wait_ge(s_hb, k + f + 1)
                    act.wait_ge(s_hs, FREE + k + max(0, f - 1))
                    act.activation(g32[:, f % 2, :], hb[f % 3][:], ACT.Gelu_apprx_tanh, bias=b1[:, n, f:f + 1],
                                   scale=1.0 / WS).then_inc(s_gelu, 1)

            def router(i):
                act.wait_ge(s_arg, i + 1)
                act.activation(arg[:], arg[:], ACT.Tanh).then_inc(s_th, 1)

            if routed:
                router(0)
            with act.Fori(0, B - 1) as i:
                hidden(0, i)
                if routed:
                    router(i + 1)
            hidden(0, B - 1)
            for n in range(1, len(passes)):
                with act.Fori(0, B) as i:
                    hidden(n, i)

        @block.tensor
        def _(pe):
            free_at_start(pe, s_out)
            def chunk(i, c):
                dd = DDL * i
                pe.wait_ge(s_xn, NT * (i + 1))
                pe.wait_ge(s_ddev, FREE + dd + c)
                for t in range(NT):
                    mm = pe.transpose(DD[0:KC, t * 128:(t + 1) * 128], xn[:, t, c * KC:(c + 1) * KC], ident[:])
                mm.then_inc(s_dd, 1)

            def gate(i):
                pe.wait_ge(s_g, i + 1)
                pe.wait_ge(s_ddev, FREE + DDL * i + NK)
                for c in range(NK):
                    mm = pe.matmul(DD[:, c * KC:(c + 1) * KC], gcol[:, c:c + 1].to_broadcast([KC, 128]),
                                   ident[0:KC, 0:KC], start=True, stop=True)
                mm.then_inc(s_dd, 1)

            def router(i):
                pe.wait_ge(s_wgs, 1)
                pe.wait_ge(s_ddev, FREE + DDL * i + NK + 1)
                pe.wait_ge(s_h, NK * (i + 1))
                for t in range(NT):
                    n = 0
                    for c in range(NK):
                        for a, w in SPLITS:
                            mm = pe.matmul(DD[:, t * NE:(t + 1) * NE], hT[:, a, c, tokens(i, t, 128)], wgs[:, w, c, :],
                                           start=(n == 0), stop=(n == 3 * NK - 1))
                            n += 1
                mm.then_inc(s_dd, 1)

            def layernorm(i, step):
                if step < NK:
                    chunk(i, step)
                elif step == NK:
                    gate(i)
                elif routed and step == NK + 1:
                    router(i)

            def mlp(n, i, ahead=None):
                k = (n * B + i) * NF
                pe.wait_ge(s_h, NK * (i + 1) if n == 0 else NK * B)

                def out(f):
                    if isinstance(i, int) and i == 0 and n == 0 or not isinstance(i, int):
                        pe.wait_ge(s_w2, NF * n + f + 1)
                    pe.wait_ge(s_hs, FREE + k + f + 1)
                    if f == 0:
                        pe.wait_ge(s_ob, FREE + (n * B + i) * NT)
                    for t in range(NT):
                        for q, (a, w) in enumerate(SPLITS):
                            mm = pe.matmul(ob[t][:, 0:C], Hs[:, a, f % 3, t * 128:(t + 1) * 128], W2[n % 2][:, w, f, :],
                                           start=(f == 0 and q == 0), stop=(f == NF - 1 and q == 2))
                    mm.then_inc(s_out, 1)

                if n:
                    pe.wait_ge(s_w1, n)
                for f in range(NF):
                    pe.wait_ge(s_gelu, FREE + k + max(0, f - 2))
                    q = 0
                    for c in range(NK):
                        for a, w in SPLITS:
                            mm = pe.matmul(hb[f % 3][:], W1[n % 2][:, w, c, f * 128:(f + 1) * 128],
                                           hT[:, a, c, tokens(i, 0, NTOK)], start=(q == 0), stop=(q == 3 * NK - 1))
                            q += 1
                    mm.then_inc(s_hb, 1)
                    if f >= 2:
                        out(f - 2)
                    if ahead is not None and f in PE_STEPS:
                        layernorm(ahead, PE_STEPS.index(f))
                out(NF - 2)
                out(NF - 1)

            for step in range(NK + 2):
                layernorm(0, step)
            with pe.Fori(0, B - 1) as i:
                mlp(0, i, i + 1)
            mlp(0, B - 1)
            for n in range(1, len(passes)):
                with pe.Fori(0, B) as i:
                    mlp(n, i)

        @block.vector
        def _(dve):
            free_at_start(dve, s_hs, s_ob, s_ddev)
            def layernorm(link, i, step):
                dd = DDL * i
                if step == 0:
                    for t in range(NT):
                        link(dve.bn_stats(st6[:, t, :], X[:, one(i * NT + t), :].squeeze(1)))
                    dve.sem_inc(s_go, 1)
                    for t in range(NT):
                        dve.bn_aggr(mv[:, t, :], st6[:, t, :]).then_inc(s_dve, 1)
                    link.pass_by(NT)
                    dve.wait_ge(s_dve, link.n)
                    dve.tensor_scalar_add(ve[:], mv[:, :, 1:2].squeeze(2), EPS).then_inc(s_var, 1)
                    dve.tensor_copy(gcol[:], mods[:, l, 5, :, one(i)].squeeze(2)).then_inc(s_g, 1)
                elif step == 1:
                    dve.wait_ge(s_rstd, i + 1)
                    for t in range(NT):
                        dve.tensor_scalar(xn[:, t, :], X[:, one(i * NT + t), :].squeeze(1), mv[:, t, 0:1], rstd[:, t:t + 1],
                                          ALU.subtract, ALU.mult).then_inc(s_xn, 1)
                elif 2 <= step < 2 + NK:
                    c = step - 2
                    dve.wait_ge(s_dd, dd + c + 1)
                    dve.tensor_scalar(h32[:], DD[0:KC, :], mods[:, l, 4, c, one(i)], mods[:, l, 3, c, one(i)],
                                      ALU.mult, ALU.add).then_inc(s_ddev, 1)
                    dve.wait_ge(s_ddev, FREE + dd + c + 1)
                    v = lambda p: hT[:, p, c, tokens(i, 0, NTOK)]
                    link(dve.tensor_copy(v(0), h32[:]))
                    dve.tensor_tensor(v(1), h32[:], v(0), ALU.subtract).then_inc(s_h, 1)
                    dve.wait_ge(s_h, NK * i + c + 1)
                elif step == 2 + NK:
                    dve.wait_ge(s_dd, dd + NK + 1)
                    dve.tensor_copy(gbc[:, one(i), :].squeeze(1), DD[:, 0:C]).then_inc(s_ddev, 1)
                elif routed and step == 3 + NK:
                    router(link, i, dd)

            def router(link, i, dd):
                dve.wait_ge(s_dd, dd + NK + 2)
                dve.tensor_scalar(lg[:], DD[:, 0:NT * NE].rearrange("p (t e) -> p t e", e=NE), 1.0 / WS, None,
                                  ALU.mult).then_inc(s_ddev, 1)
                dve.wait_ge(s_ddev, FREE + dd + NK + 2)
                for e in range(NE):
                    for lo, hi, op in ((0, e, ALU.is_ge), (e + 1, NE, ALU.is_gt)):
                        if lo < hi:
                            last = dve.tensor_tensor(cmp[:, :, e, lo:hi], lg[:, :, lo:hi],
                                                     lg[:, :, e:e + 1].to_broadcast([128, NT, hi - lo]), op)
                            link(last)
                link(dve.tensor_reduce(rank[:], cmp[:], AX_X, ALU.add))
                link(dve.tensor_scalar(sel[:], rank[:], 2.0, None, ALU.is_lt))
                link(dve.tensor_tensor(rank[:], lg[:], sel[:], ALU.mult))
                link(dve.tensor_reduce(tot[:], rank[:], AX_X, ALU.add))
                dve.scalar_tensor_tensor(arg[:], tot[:].unsqueeze(2).to_broadcast([128, NT, NE]), -0.5, lg[:], ALU.mult,
                                         ALU.add).then_inc(s_arg, 1)

            def expert_weights(link, i):
                dve.wait_ge(s_th, i + 1)
                link(dve.tensor_scalar(arg[:], arg[:], 0.5, 0.5, ALU.mult, ALU.add))
                dve.tensor_tensor(cw[:, tokens(i, 0, NT, NT), :], arg[:], sel[:], ALU.mult).then_inc(s_cw, 1)

            def mlp(link, n, i, ahead=None):
                k = (n * B + i) * NF
                for f in range(NF):
                    dve.wait_ge(s_gelu, FREE + k + f + 1)
                    dve.wait_ge(s_out, FREE + k + max(0, f - 2))
                    v = lambda p: Hs[:, p, f % 3, :]
                    link(dve.tensor_copy(v(0), g32[:, f % 2, :]))
                    dve.tensor_tensor(v(1), g32[:, f % 2, :], v(0), ALU.subtract).then_inc(s_hs, 1)
                    if ahead is not None:
                        if f in DVE_STEPS:
                            layernorm(link, ahead, DVE_STEPS.index(f))
                if ahead is not None and routed:
                    layernorm(link, ahead, 3 + NK)
                dve.wait_ge(s_out, FREE + k + NF)
                for t in range(NT):
                    xt = X[:, one(i * NT + t), :].squeeze(1)
                    dve.scalar_tensor_tensor(y[:], ob[t][:, 0:C], 1.0 / WS, b2[:, n, :], ALU.mult, ALU.add).then_inc(s_ob, 1)
                    dve.wait_ge(s_ob, FREE + (n * B + i) * NT + t + 1)
                    g = gbc[:, one(i), :].squeeze(1)
                    if routed:
                        link(dve.scalar_tensor_tensor(y[:], y[:], cw[:, one(i * NT + t), n:n + 1].squeeze(1), g, ALU.mult, ALU.mult))
                    else:
                        link(dve.tensor_tensor(y[:], y[:], g, ALU.mult))
                    link(dve.tensor_tensor(xt, xt, y[:], ALU.add))
                if ahead is not None and routed:
                    expert_weights(link, ahead)

            dve.wait_ge(s_small, 32 * len(passes) + (16 if routed else 0))
            link = Order(dve, s_dve)
            if routed:
                dve.wait_ge(s_clr, 1)
                link(dve.tensor_scalar(wg[:], wg[:], WS, None, ALU.mult))
                link(dve.tensor_copy(wgs[:, 0, :, :], wg[:]))
                dve.tensor_tensor(wgs[:, 1, :, :], wg[:], wgs[:, 0, :, :], ALU.subtract).then_inc(s_wgs, 1)
            for step in range(4 + NK):
                layernorm(link, 0, step)
            if routed:
                expert_weights(link, 0)
            start, LN, MLP = link.n, 2 * NT + NK + (6 + 4 + 1 if routed else 0), NF + 2 * NT
            with dve.Fori(0, B - 1) as i:
                link = Order(dve, s_dve, i * (LN + MLP) + start)
                mlp(link, 0, i, i + 1)
            link = Order(dve, s_dve, start + (B - 1) * (LN + MLP))
            mlp(link, 0, B - 1)
            start = link.n
            for n in range(1, len(passes)):
                with dve.Fori(0, B) as i:
                    mlp(Order(dve, s_dve, i * MLP + start), n, i)
                start += B * MLP


def tokens(i, t, n, per=NTOK):
    at0 = i * per + t * 128
    return slice(at0, at0 + n) if isinstance(i, int) else bass.ds(at0, n)


def build(nc, io, out):
    with ExitStack() as ctx:
        def sb(name, shape, dt=F32):
            return ctx.enter_context(nc.sbuf_tensor(name, shape, dt))

        T = {
            "x": sb("x_tokens", [128, B * NT, C]),
            "ident": sb("identity", [128, 128]),
            "minus_half": sb("minus_half", [128, NT]),
            "mods": sb("mods", [KC, NL, 6, NK, B]),
            "staging": sb("raw_weights", [128, NK * FF]),
            "w_att": sb("w_att_parts", [KC, 2, NK, 4 * C], F16),
            "w1_parts": sb("w1_parts", [KC, 2, NK, FF], F16),
            "s_raw": nc.alloc_semaphore("raw_weights_in"),
            "raw_count": 32,
            "mlp_of": [[0], [1, 2, 3, 4], [5]],
        }
        prepare_and_rotate(nc, io, T)
        for l in range(NL):
            attention_half(nc, io, T, l)
            mlp_half(nc, io, T, l)
        store(nc, T, out)


def store(nc, T, out):
    with ExitStack() as ctx:
        s_out = nc.alloc_semaphore("out_written")
        block = ctx.enter_context(nc.Block())

        @block.sync
        def _(sp):
            for b in range(B):
                sp.dma_start(out[b].rearrange("(t p) c -> p t c", p=128), T["x"][:, b * NT:(b + 1) * NT, :]).then_inc(s_out, 16)
            sp.wait_ge(s_out, 16 * B)


def layouts(inputs):
    import numpy as np

    a = {k: np.asarray(v) for k, v in inputs.items()}
    L = {1: "L1_cond_", 2: "L2_cond_", 3: "L3_cond_"}
    ada_w = [a["L1_cond_W_ada"], a["L2_cond_w_adaln"], a["L3_cond_ada_w"]]
    ada_b = [a["L1_cond_b_ada"], a["L2_cond_b_adaln"], a["L3_cond_ada_b"]]
    per_layer = {
        "qkv_w": [a["L1_cond_W_qkv"], a["L2_cond_w_qkv"], a["L3_cond_qkv_w"]],
        "qkv_b": [a["L1_cond_b_qkv"], a["L2_cond_b_qkv"], a["L3_cond_qkv_b"]],
        "proj_w": [a["L1_cond_W_proj"], a["L2_cond_w_proj"], a["L3_cond_out_w"]],
        "proj_b": [a["L1_cond_b_proj"], a["L2_cond_b_proj"], a["L3_cond_out_b"]],
    }
    put = {"x": a["x"], "P": a["L0_cond_P"], "skewT": a["L0_cond_W"].T, "skew_b": a["L0_cond_b"],
           "condT": a["cond_1152"].T.reshape(NK, KC, B).transpose(1, 0, 2), "gate_w": a["L2_cond_w_gate"]}
    for l in range(NL):
        put[f"ada_w{l}"], put[f"ada_b{l}"] = ada_w[l], ada_b[l]
        for k, v in per_layer.items():
            put[f"{k}{l}"] = v[l]
        qk = np.pad(per_layer["qkv_b"][l][:2 * C].reshape(2, H, D), ((0, 0), (0, 2), (0, 0)))
        put[f"qk_b{l}"] = qk.reshape(2, 6, NK, D).transpose(1, 3, 0, 2).reshape(6 * D, 2, NK)
    mlp = [("L1_cond_W_fc1", "L1_cond_b_fc1", "L1_cond_W_fc2", "L1_cond_b_fc2", None)]
    mlp += [("L2_cond_w1", "L2_cond_b1", "L2_cond_w2", "L2_cond_b2", e) for e in range(NE)]
    mlp += [("L3_cond_w1", "L3_cond_b1", "L3_cond_w2", "L3_cond_b2", None)]
    for m, (w1, b1, w2, b2, e) in enumerate(mlp):
        get = lambda n: a[n] if e is None else a[n][e]
        put[f"w1_{m}"], put[f"w2_{m}"], put[f"b2_{m}"] = get(w1), get(w2), get(b2)
        put[f"b1_{m}"] = get(b1).reshape(NF, 128).T
    return {k: np.ascontiguousarray(v) for k, v in put.items()}


def kernel(**inputs):
    import concourse.bacc as bacc
    from concourse.bass_utils import run_bass_kernel_spmd as run

    nc = bacc.Bacc("TRN2", target_bir_lowering=False, num_devices=1)
    arrays = layouts(inputs)
    io = {k: nc.dram_tensor(f"in_{k}", v.shape, mybir.dt.from_np(v.dtype), kind="ExternalInput").ap()
          for k, v in arrays.items()}
    out = nc.dram_tensor("out_x", (B, NTOK, C), F32, kind="ExternalOutput").ap()
    build(nc, io, out)
    r = run(nc, [{f"in_{k}": v for k, v in arrays.items()}], core_ids=[0])
    return r.results[0]["out_x"]
```

```python
from contextlib import ExitStack

import concourse.bass as bass
from concourse import mybir

F32 = mybir.dt.float32
F16 = mybir.dt.float16
BF16 = mybir.dt.bfloat16
ALU = mybir.AluOpType
ACT = mybir.ActivationFunctionType
AX_X = mybir.AxisListType.X

B, NTOK, C = 4, 512, 288
NT = NTOK // 128
NK, KC = 3, 96
CR = C - 2 * 128
KCH = [128, 128, 3 * CR]
CX = C + 2 * CR
D0 = 64
NSKEW = D0 * (D0 - 1) // 2
NSQ = 18
TAYLOR = 13
H, D = 16, 18
NL = 3
FF = 4 * C
NF = FF // 128
NE = 4
RAW_W1 = 64
WS = 256.0
EPS = 1e-6


FREE = 1


def free_at_start(eng, *sems):
    for sem in sems:
        eng.sem_inc(sem, FREE)


class Order:

    def __init__(self, eng, sem, start=0):
        self.eng, self.sem, self.n = eng, sem, start

    def __call__(self, ins):
        self.n = self.n + 1
        ins.then_inc(self.sem, 1)
        self.eng.wait_ge(self.sem, self.n)

    def pass_by(self, count):
        self.n = self.n + count


SPLITS = [(0, 0), (1, 0), (0, 1)]
PASSES = [(c, a, w) for c in range(2) for a, w in SPLITS] + [(2, None, None)]


def part_of(pair, c, part, cols):
    return pair[0][:, part, c, cols] if c < 2 else pair[1][:, cols]


def dense(pe, out, lhs, lhs_cols, rhs, rhs_cols, weights_left, sem):
    for n, (c, a, w) in enumerate(PASSES):
        l, r = (w, a) if weights_left else (a, w)
        mm = pe.matmul(out, part_of(lhs, c, l, lhs_cols), part_of(rhs, c, r, rhs_cols), start=(n == 0),
                       stop=(n == len(PASSES) - 1))
    if sem is not None:
        mm.then_inc(sem, 1)
    return mm


def split(pool, src, hi, lo, of, s_hi, n, s_done):
    pool.tensor_scalar(src, src, WS, 1.0, ALU.mult, ALU.mult).then_inc(s_hi, 1)
    pool.wait_ge(s_hi, 3 * n + 1)
    pool.tensor_copy(hi, src).then_inc(s_hi, 1)
    pool.wait_ge(s_hi, 3 * n + 2)
    pool.tensor_tensor(lo, src[of], hi[of], ALU.subtract).then_inc(s_hi, 1)
    pool.wait_ge(s_hi, 3 * n + 3)
    pool.sem_inc(s_done, 1)


ALL, LOW_W, LOW_H = slice(0, 128), slice(2 * CR, 3 * CR), slice(CR, 2 * CR)


def load_rows(sp, to, src, sem):
    sp.dma_start(to[:, 0:2, :], src[0:256].rearrange("(c p) n -> p c n", p=128)).then_inc(sem, 16)
    for j in range(3):
        sp.dma_start(to[j * CR:(j + 1) * CR, 2, :], src[256:C]).then_inc(sem, 16)


def by_chunk(staging):
    return staging[:].rearrange("p (c n) -> p c n", c=3)


def load_w1(sp, io, to, m, sem):
    load_rows(sp, by_chunk(to), io[f"w1_{m}"], sem)


def load_w2(sp, io, to, m, sem):
    sp.dma_start(to[:, 0:NF * C].rearrange("p (f n) -> p f n", f=NF),
                 io[f"w2_{m}"].rearrange("(f p) n -> p f n", p=128)).then_inc(sem, 16)


def load_attention_weights(sp, io, T, l):
    v = by_chunk(T["staging"])
    load_rows(sp, v[:, :, 0:3 * C], io[f"qkv_w{l}"], T["s_raw"])
    load_rows(sp, v[:, :, 3 * C:4 * C], io[f"proj_w{l}"], T["s_raw"])


def split_w1(pool, raw, W1, s_hi, n, s_done):
    v = by_chunk(raw)
    split(pool, v[:, 0:2, :], W1[0][:, 0, :, :], W1[0][:, 1, :, :], ALL, s_hi, n, s_done)
    split(pool, v[0:KCH[2], 2, :], W1[1][:], W1[1][LOW_W, :], LOW_W, s_hi, n + 1, s_done)


def split_w2(pool, raw, W2, s_hi, n, s_done):
    for f in range(NF):
        split(pool, raw[:, f * C:(f + 1) * C], W2[:, 0, f, :], W2[:, 1, f, :], ALL, s_hi, n + f, s_done)


def split_attention_weights(pool, T, s_hi, n, s_done):
    W, view = T["w_att"], by_chunk(T["staging"])

    def columns(k, src, place):
        nonlocal n
        if k < 2:
            split(pool, src, place(W[0][:, 0, k, :]), place(W[0][:, 1, k, :]), ALL, s_hi, n, s_done)
        else:
            split(pool, src, place(W[1][:]), place(W[1][LOW_W, :]), LOW_W, s_hi, n, s_done)
        n += 1

    for k in range(3):
        for side in range(2):
            heads = view[0:KCH[k], k, side * C:(side + 1) * C].rearrange("p (h d) -> p h d", d=D)
            for c in range(NK):
                to = side * C + QK_OFF[c]
                columns(k, heads[:, c::NK, :], lambda w: w[:, to:to + HD_ROWS[c]].rearrange("p (h d) -> p h d", d=D))
        columns(k, view[0:KCH[k], k, 2 * C:], lambda w: w[:, 2 * C:])


def prepare_and_rotate(nc, io, T):
    X, ident, mods = T["x"], T["ident"], T["mods"]
    with nc.cleanup_on_exit(), ExitStack() as ctx:
        def sb(name, shape, dt=F32):
            return ctx.enter_context(nc.sbuf_tensor(name, shape, dt))

        def sem(name):
            return nc.alloc_semaphore(name)

        Aw = sb("qr_work", [KC, NK, D0 + 1])
        Vn = sb("qr_vectors", [KC, NK, D0])
        from_row = sb("from_row", [KC, NK, D0 + 1])
        eye3 = sb("eye3", [KC, NK, D0 + 1])
        am = sb("column_masked", [KC, NK])
        ek = sb("unit_column", [KC, NK])
        vt = sb("minus_v", [KC, NK])
        vc = sb("v_times_c", [KC, NK])
        a_cols = sb("column_products", [KC, D0])
        v_cols = sb("vector_products", [KC, D0])
        n2 = sb("norm2", [KC, 1])
        nrm = sb("norm", [KC, 1])
        root = sb("exponent_half", [KC, 1])
        sgn = sb("minus_sign", [KC, 1])
        beta = sb("beta", [KC, 1])
        vv = sb("half_v_dot_v", [KC, 1])
        cv = sb("c_factor", [KC, 1])
        crow = sb("c_row", [KC, D0])
        cdia = sb("c_diagonal", [D0, D0])
        ccol = sb("c_col", [D0, 1])
        upper = sb("strict_upper", [D0, D0])
        lower = sb("strict_lower", [D0, D0])
        Xn = sb("nilpotent", [D0, 2, 2, D0])
        PT = sb("inverse_transposed", [D0, 2, D0])
        VT = sb("v_transposed", [D0, C])
        Tt = sb("T_transposed", [D0, D0])
        Y = sb("T_v1T", [D0, D0])
        U = sb("u_factor", [KC, NK, D0])
        UT = sb("u_transposed", [D0, C])
        Rm = sb("rotation_T_minus_one", [D0, B, D0])
        F = sb("rotated_minus_same", [D0, B, C])
        cT = sb("cond_T", [KC, NK, B])
        e1 = sb("silu_denominator", [KC, NK, B])
        sT = sb("silu_T", [KC, NK, B])
        Wsk = sb("skew_weights", [KC, NK, NSKEW])
        skb = sb("skew_bias", [B, NSKEW])
        sv = sb("skew_values", [B, NSKEW])
        Up = sb("skew_upper", [D0, B, D0])
        A = sb("skew", [D0, 2, B, D0])
        Ab = sb("skew_abs", [D0, B, D0])
        ones64 = sb("ones64", [D0, D0])
        nrm1 = sb("norm1", [D0, B])
        again = sb("square_again", [D0, NSQ, B])
        halves = sb("halvings", [D0, NSQ, B])
        down = sb("scale_down", [D0, B])
        hor = sb("horner", [D0, 2, B, D0])
        R = sb("rotation", [D0, 2, 2, B, D0])
        dif = sb("squared_minus_same", [D0, 2, B, D0])
        eyeB = sb("eye_batches", [D0, 2, B, D0])
        Wad = sb("ada_weights", [KC, NK, 6 * C])
        bad = sb("ada_bias", [B, 6 * C])
        mrow = sb("mod_rows", [B, 6 * C])
        mrep = sb("mod_rest_repeated", [B, 4, 3, CR])
        xs = sb("x_of_batch", [128, NT, C])
        xT = sb("x_transposed", [KC, NK, B * NTOK])
        inv = sb("inverse_of_step", [D0, TAYLOR])
        n2g, alpha, absa = sb("norm2_guarded", [KC, 1]), sb("alpha", [KC, 1]), sb("alpha_abs", [KC, 1])
        zT = sb("z_transposed", [D0, NTOK])
        bank = [ctx.enter_context(nc.psum_tensor(f"bank{i}", [128, 512], F32)) for i in range(8)]
        psq, psr = bank[0], bank[1]

        s_p, s_x, s_c, s_w, s_b = sem("p_in"), sem("x_in"), sem("cond_in"), sem("skew_w_in"), sem("skew_b_in")
        s_ad, s_adb = sem("ada_w_in"), sem("ada_b_in")
        s_clear, s_mask = sem("masks_cleared"), sem("masks_ready")
        s_dve, s_whi, s_wlo = sem("dve_order"), sem("weights_high"), sem("weights_split")
        s_col, s_prod, s_row, s_sc, s_norm = sem("column_ready"), sem("products_ready"), sem("row_ready"), sem("norm2_ready"), sem("norm_ready")
        s_vt, s_kept, s_half = sem("vector_ready"), sem("vector_kept"), sem("c_factor_ready")
        s_e1, s_sT = sem("silu_exp_ready"), sem("silu_ready")
        s_skp, s_sv, s_up = sem("skew_products"), sem("skew_values_ready"), sem("skew_moved")
        s_upT, s_n1p = sem("upper_transposed"), sem("norm_products")
        s_abs, s_hp, s_h = sem("abs_ready"), sem("horner_product"), sem("horner_ready")
        s_rT, s_sqp, s_R = sem("r_transposed"), sem("square_products"), sem("squared")
        s_gp, s_X, s_PT = sem("gram_products"), sem("nilpotent_ready"), sem("inverse_ready")
        s_vT, s_xp, s_xr = sem("v_transposed_in_psum"), sem("nilpotent_products"), sem("nilpotent_step")
        s_Tt, s_yp, s_Y, s_up2, s_U = sem("t_ready"), sem("y_product"), sem("y_ready"), sem("u_products"), sem("u_ready")
        s_fp, s_F = sem("f_products"), sem("f_ready")
        s_mp, s_mr, s_tp, s_md = sem("mod_products"), sem("mod_rows_ready"), sem("mods_transposed"), sem("mods_ready")
        s_xt, s_xT, s_zp, s_z, s_dp, s_d = (sem("x_transposed_in_psum"), sem("x_transposed_ready"), sem("z_product"),
                                            sem("z_ready"), sem("delta_product"), sem("x_rotated"))
        s_xs, s_inv, s_go = sem("x_of_batch_ready"), sem("inverses_set"), sem("waits_taken")
        block = ctx.enter_context(nc.Block())
        NG, NA = 4, 4
        GW, AW = NSKEW // NG, 6 * C // NA
        MODS, HORNER, SQUARES, XT = NA, TAYLOR - 1, NSQ, B
        WAIT_SKEW = 6
        REST = D0 - NL * MODS - WAIT_SKEW - HORNER - SQUARES - XT
        MR = NA + 2

        @block.sync
        def _(sp):
            sp.dma_start(Aw[:, :, 0:D0], io["P"].rearrange("(c p) d -> p c d", p=KC)).then_inc(s_p, 16)
            sp.dma_start(cT[:], io["condT"]).then_inc(s_c, 16)
            sp.dma_start(Wsk[:], io["skewT"].rearrange("(c p) n -> p c n", p=KC)).then_inc(s_w, 16)
            sp.dma_start(skb[:], io["skew_b"].partition_broadcast(B)).then_inc(s_b, 16)
            sp.dma_start(Wad[:], io["ada_w0"].rearrange("(c p) n -> p c n", p=KC)).then_inc(s_ad, 16)
            sp.dma_start(bad[:], io["ada_b0"].partition_broadcast(B)).then_inc(s_adb, 16)
            for b in range(B):
                sp.dma_start(X[:, b * NT:(b + 1) * NT, :],
                             io["x"][b].rearrange("(t p) c -> p t c", p=128)).then_inc(s_x, 16)
            sp.wait_ge(s_sv, NG)
            sp.wait_ge(s_clear, 5)
            off = 0
            for i in range(D0 - 1):
                n = D0 - 1 - i
                sp.dma_start(Up[i:i + 1, :, i + 1:D0], sv[:, off:off + n],
                             allow_slow_non_contiguous=(n == 1)).then_inc(s_up, 16)
                off += n
            for l in range(NL):
                if l + 1 < NL:
                    sp.wait_ge(s_mp, NA * (l + 1))
                    sp.wait_ge(s_mr, FREE + MR * (l + 1))
                    sp.dma_start(Wad[:], io[f"ada_w{l + 1}"].rearrange("(c p) n -> p c n", p=KC)).then_inc(s_ad, 16)
                    sp.dma_start(bad[:], io[f"ada_b{l + 1}"].partition_broadcast(B)).then_inc(s_adb, 16)
            load_attention_weights(sp, io, T, 0)

        @block.gpsimd
        def _(pool):
            free_at_start(pool, s_kept)
            for m, v in ((ident, 0.0), (from_row, 1.0), (eye3, 0.0), (upper, 1.0), (Up, 0.0), (lower, 1.0), (eyeB, 0.0),
                         (Aw[:, :, D0:D0 + 1], 0.0)):
                pool.memset(m[:], v).then_inc(s_clear, 1)
            pool.memset(ones64[:], 1.0).then_inc(s_clear, 1)
            pool.memset(T["minus_half"][:], -0.5).then_inc(s_clear, 1)
            pool.memset(root[:], 0.5).then_inc(s_clear, 1)
            pool.wait_ge(s_clear, 11)

            def select(m, pattern, op, base, mult, fill):
                pool.affine_select(out=m, in_=m, pattern=pattern, compare_op=op, fill=fill, base=base,
                                   channel_multiplier=mult).then_inc(s_mask, 1)

            select(ident[:], [[-1, 128]], ALU.not_equal, 0, 1, 1.0)
            select(from_row[:, 0, :], [[-1, D0 + 1]], ALU.is_ge, 0, 1, 0.0)
            select(eye3[:, 0, :], [[-1, D0 + 1]], ALU.not_equal, 0, 1, 1.0)
            select(upper[:], [[1, D0]], ALU.is_gt, 0, -1, 0.0)
            select(lower[:], [[-1, D0]], ALU.is_gt, 0, 1, 0.0)
            for i in range(2):
                select(eyeB[:, i, :, :], [[0, B], [-1, D0]], ALU.not_equal, 0, 1, 1.0)
            for n in range(TAYLOR - 1):
                pool.memset(inv[:, n:n + 1], 1.0 / (TAYLOR - 1 - n)).then_inc(s_inv, 1)
                pool.wait_ge(s_inv, n + 1)
            with pool.Fori(0, D0) as k:
                pool.wait_ge(s_sc, k + 1)
                pool.tensor_tensor(nrm[:], n2[:], root[:], ALU.pow).then_inc(s_norm, 1)
                pool.wait_ge(s_vt, k + 1)
                pool.tensor_copy(Vn[:, :, bass.ds(k, 1)], vt[:].unsqueeze(2)).then_inc(s_kept, 1)
                pool.wait_ge(s_half, k + 1)
                pool.tensor_copy(crow[:, bass.ds(k, 1)], cv[:]).then_inc(s_kept, 1)
            pool.wait_ge(T["s_raw"], T["raw_count"])
            split_attention_weights(pool, T, s_whi, 0, s_wlo)

        @block.scalar
        def _(act):
            act.wait_ge(s_c, 16)
            act.activation(e1[:], cT[:], ACT.Exp, scale=-1.0).then_inc(s_e1, 1)

        @block.tensor
        def _(pe):
            free_at_start(pe, s_xt, s_dp)
            pe.wait_ge(s_sT, 1)
            pe.wait_ge(s_w, 16)
            for g in range(NG):
                for c in range(NK):
                    mm = pe.matmul(bank[2 + g][0:B, 0:GW], sT[:, c, :], Wsk[:, c, g * GW:(g + 1) * GW],
                                   start=(c == 0), stop=(c == NK - 1))
                mm.then_inc(s_skp, 1)

            def step(k):
                pe.wait_ge(s_col, k + 1)
                for c in range(NK):
                    mm = pe.matmul(psq[0:KC, 0:D0], am[:, c:c + 1].to_broadcast([KC, KC]), Aw[:, c, 0:D0],
                                   start=(c == 0), stop=(c == NK - 1))
                mm.then_inc(s_prod, 1)
                pe.matmul(psr[0:KC, 0:D0], ek[:, 0:1].to_broadcast([KC, KC]), Aw[:, 0, 0:D0],
                          start=True, stop=True).then_inc(s_row, 1)

            def mods_of(l, k):
                pe.wait_ge(s_ad, 16 * (l + 1))
                with pe.Fori(0, MODS) as g:
                    step(g + k)
                    pe.wait_ge(s_mr, FREE + g + MR * l)
                    for c in range(NK):
                        mm = pe.matmul(bank[2][0:B, 0:AW], sT[:, c, :], Wad[:, c, bass.ds(g * AW, AW)],
                                       start=(c == 0), stop=(c == NK - 1))
                    mm.then_inc(s_mp, 1)
                pe.wait_ge(s_mr, FREE + MR * (l + 1))
                if l:
                    pe.wait_ge(s_md, l)
                for n, v in enumerate((0, 1, 3, 4)):
                    for c in range(3):
                        rows = mrow[:, v * C + c * 128:v * C + (c + 1) * 128] if c < 2 else mrep[:, n, :, :].rearrange("b j r -> b (j r)")
                        to = (3 * n + c) * B
                        pe.transpose(bank[6][0:KCH[c], to:to + B], rows, ident[0:B, 0:B])
                for n, v in enumerate((2, 5)):
                    for c in range(NK):
                        to = (3 * (4 + n) + c) * B
                        mm = pe.transpose(bank[6][0:KC, to:to + B], mrow[:, v * C + c * KC:v * C + (c + 1) * KC], ident[0:B, 0:B])
                mm.then_inc(s_tp, 1)

            pe.wait_ge(s_p, 16)
            pe.wait_ge(s_mask, 7)
            with pe.Fori(0, WAIT_SKEW) as n:
                step(n + 0)
            pe.wait_ge(s_sv, NG)
            mods_of(0, WAIT_SKEW)
            k = WAIT_SKEW + MODS
            pe.wait_ge(s_up, 16 * (D0 - 1))
            for b in range(B):
                mm = pe.transpose(bank[3][0:D0, b * D0:(b + 1) * D0], Up[:, b, :], ident[0:D0, 0:D0])
            mm.then_inc(s_upT, 1)
            pe.wait_ge(s_abs, 1)
            pe.matmul(bank[7][0:D0, 0:B * D0], ones64[:], Ab[:].rearrange("p b j -> p (b j)"),
                      start=True, stop=True).then_inc(s_n1p, 1)
            with pe.Fori(0, HORNER // 2) as m:
                for n in range(2):
                    step(2 * m + (k + n))
                    pe.wait_ge(s_h, 2 * m + (n + 1))
                    pe.sem_inc(s_go, 1)
                    for b in range(B):
                        mm = pe.matmul(bank[4][0:D0, b * D0:(b + 1) * D0], A[:, 1, b, :], hor[:, n, b, :],
                                       start=True, stop=True)
                    mm.then_inc(s_hp, 1)
            k += HORNER
            pe.wait_ge(s_h, TAYLOR)
            for b in range(B):
                mm = pe.transpose(bank[5][0:D0, b * D0:(b + 1) * D0], hor[:, (TAYLOR - 1) % 2, b, :], ident[0:D0, 0:D0])
            mm.then_inc(s_rT, 1)
            with pe.Fori(0, SQUARES // 2) as m:
                for n in range(2):
                    step(2 * m + (k + n))
                    pe.wait_ge(s_R, 2 * m + (n + 1))
                    pe.sem_inc(s_go, 1)
                    for i in range(2):
                        for b in range(B):
                            mm = pe.matmul(bank[4][0:D0, (i * B + b) * D0:(i * B + b + 1) * D0], R[:, n, 1 - i, b, :],
                                           R[:, n, i, b, :], start=True, stop=True)
                    mm.then_inc(s_sqp, 1)
            k += SQUARES
            for l in range(1, NL):
                mods_of(l, k)
                k += MODS
            pe.wait_ge(s_md, NL)
            pe.wait_ge(s_R, NSQ + 1)
            with pe.Fori(0, XT) as b:
                step(b + k)
                pe.wait_ge(s_xs, b + 1)
                for c in range(NK):
                    pe.wait_ge(s_xT, FREE + NK * b + c)
                    for t in range(NT):
                        mm = pe.transpose(bank[4 + c][0:KC, t * 128:(t + 1) * 128], xs[:, t, c * KC:(c + 1) * KC], ident[:])
                    mm.then_inc(s_xt, 1)
            k += XT
            with pe.Fori(0, REST) as n:
                step(n + k)
            pe.wait_ge(s_kept, FREE + 2 * D0)
            pe.wait_ge(s_xT, FREE + NK * B)
            pe.wait_ge(s_md, NL)
            for c in range(NK):
                mm = pe.matmul(bank[2][0:D0, 0:D0], Vn[:, c, :], Vn[:, c, :], start=(c == 0), stop=(c == NK - 1))
            mm.then_inc(s_gp, 1)
            for c in range(NK):
                mm = pe.transpose(bank[3][0:D0, c * KC:(c + 1) * KC], Vn[:, c, :], ident[0:KC, 0:KC])
            mm.then_inc(s_vT, 1)
            for n in range(5):
                pe.wait_ge(s_X, n + 1)
                pe.matmul(bank[4][0:D0, 0:D0], Xn[:, n % 2, 1, :], Xn[:, n % 2, 0, :], start=True, stop=True)
                pe.matmul(bank[4][0:D0, D0:2 * D0], Xn[:, n % 2, 0, :], Xn[:, n % 2, 1, :], start=True, stop=True).then_inc(s_xp, 1)
                pe.wait_ge(s_X, n + 2)
                pe.wait_ge(s_PT, n + 1)
                pe.matmul(bank[5][0:D0, 0:D0], Xn[:, (n + 1) % 2, 0, :], PT[:, n % 2, :], start=True, stop=True).then_inc(s_xr, 1)
            pe.wait_ge(s_Tt, 1)
            pe.matmul(bank[6][0:D0, 0:D0], Tt[:], VT[:, 0:D0], start=True, stop=True).then_inc(s_yp, 1)
            pe.wait_ge(s_Y, 1)
            for c in range(NK):
                mm = pe.matmul(bank[7][0:KC, c * D0:(c + 1) * D0], VT[:, c * KC:(c + 1) * KC], Y[:], start=True, stop=True)
            mm.then_inc(s_up2, 1)
            pe.matmul(bank[2][0:D0, 0:C], Y[:], VT[:], start=True, stop=True).then_inc(s_up2, 1)
            pe.wait_ge(s_U, 2)
            for b in range(B):
                if b >= 2:
                    pe.wait_ge(s_F, b - 1)
                pe.matmul(bank[3 + b % 2][0:D0, 0:C], Rm[:, b, :], UT[:], start=True, stop=True).then_inc(s_fp, 1)
            def z(b):
                pe.wait_ge(s_xT, FREE + NK * B)
                for c in range(NK):
                    mm = pe.matmul(bank[7][0:D0, :], U[:, c, :], xT[:, c, tokens(b, 0, NTOK)], start=(c == 0), stop=(c == NK - 1))
                mm.then_inc(s_zp, 1)

            def delta(b):
                for t in range(NT):
                    pe.wait_ge(s_d, FREE + b * NT)
                    pe.sem_inc(s_go, 1)
                    pe.matmul(bank[t][:, 0:C], zT[:, t * 128:(t + 1) * 128], F[:, one(b), :].squeeze(1),
                              start=True, stop=True).then_inc(s_dp, 1)

            pe.wait_ge(s_F, B)
            z(0)
            with pe.Fori(0, B - 1) as b:
                pe.wait_ge(s_z, b + 1)
                z(b + 1)
                delta(b)
            pe.wait_ge(s_z, B)
            delta(B - 1)

        @block.vector
        def _(dve):
            free_at_start(dve, s_d, s_mr, s_xT)
            link = Order(dve, s_dve)
            dve.wait_ge(s_e1, 1)
            link(dve.tensor_scalar_add(e1[:], e1[:], 1.0))
            link(dve.reciprocal(e1[:], e1[:]))
            dve.wait_ge(s_c, 16)
            dve.tensor_tensor(sT[:], cT[:], e1[:], ALU.mult).then_inc(s_sT, 1)
            dve.wait_ge(s_b, 16)
            for g in range(NG):
                dve.wait_ge(s_skp, g + 1)
                dve.tensor_tensor(sv[:, g * GW:(g + 1) * GW], bank[2 + g][0:B, 0:GW], skb[:, g * GW:(g + 1) * GW],
                                  ALU.add).then_inc(s_sv, 1)
            dve.wait_ge(s_p, 16)
            dve.wait_ge(s_clear, 11)
            dve.wait_ge(s_mask, 7)

            def column(k):
                link(dve.tensor_copy(ek[:].unsqueeze(2), eye3[:, :, k]))
                dve.tensor_tensor(am[:].unsqueeze(2), Aw[:, :, k], from_row[:, :, k], ALU.mult).then_inc(s_col, 1)

            column(slice(0, 1))
            STEP = 13

            def step(link, k):
                at = bass.ds(k, 1)
                dve.wait_ge(s_prod, k + 1)
                dve.wait_ge(s_col, k + 1)
                dve.tensor_copy(n2[:], psq[0:KC, at]).then_inc(s_sc, 1)
                dve.tensor_scalar_add(n2g[:], psq[0:KC, at], 1e-30).then_inc(s_dve, 1)
                dve.tensor_copy(a_cols[:], psq[0:KC, 0:D0]).then_inc(s_dve, 1)
                dve.wait_ge(s_row, k + 1)
                dve.tensor_copy(alpha[:], psr[0:KC, at]).then_inc(s_dve, 1)
                link.pass_by(3)
                dve.wait_ge(s_dve, link.n)
                dve.tensor_scalar(sgn[:], alpha[:], 0.0, -2.0, ALU.is_ge, ALU.mult).then_inc(s_dve, 1)
                dve.scalar_tensor_tensor(absa[:], alpha[:], -1.0, alpha[:], ALU.mult, ALU.max).then_inc(s_dve, 1)
                link.pass_by(2)
                dve.wait_ge(s_dve, link.n)
                dve.wait_ge(s_norm, k + 1)
                dve.scalar_tensor_tensor(beta[:], sgn[:], 1.0, nrm[:], ALU.add, ALU.mult).then_inc(s_dve, 1)
                dve.tensor_scalar(vv[:], nrm[:], absa[:, 0:1], n2g[:, 0:1], ALU.mult, ALU.add).then_inc(s_dve, 1)
                link.pass_by(1)
                dve.wait_ge(s_dve, link.n)
                dve.wait_ge(s_kept, FREE + k * 2)
                dve.scalar_tensor_tensor(vt[:], ek[:], beta[:, 0:1], am[:], ALU.mult, ALU.subtract).then_inc(s_vt, 1)
                dve.scalar_tensor_tensor(v_cols[:], psr[0:KC, 0:D0], beta[:, 0:1], a_cols[:], ALU.mult,
                                         ALU.subtract).then_inc(s_dve, 1)
                link.pass_by(1)
                dve.wait_ge(s_dve, link.n)
                dve.reciprocal(cv[:], vv[:]).then_inc(s_half, 1)
                dve.wait_ge(s_vt, k + 1)
                dve.wait_ge(s_half, k + 1)
                dve.tensor_scalar(vc[:], vt[:], cv[:, 0:1], -1.0, ALU.mult, ALU.mult).then_inc(s_dve, 1)
                nxt = bass.ds(k + 1, 1)
                dve.tensor_copy(ek[:].unsqueeze(2), eye3[:, :, nxt]).then_inc(s_dve, 1)
                link.pass_by(3)
                dve.wait_ge(s_dve, link.n)
                for c in range(NK):
                    dve.scalar_tensor_tensor(Aw[:, c, 0:D0], v_cols[:], vc[:, c:c + 1], Aw[:, c, 0:D0], ALU.mult,
                                             ALU.add).then_inc(s_dve, 1)
                link.pass_by(NK)
                dve.wait_ge(s_dve, link.n)
                dve.tensor_tensor(am[:].unsqueeze(2), Aw[:, :, nxt], from_row[:, :, nxt], ALU.mult).then_inc(s_col, 1)

            def mods_of(l, k, start):
                dve.wait_ge(s_adb, 16 * (l + 1))
                if l:
                    dve.wait_ge(s_tp, l)
                with dve.Fori(0, MODS) as g:
                    step(Order(dve, s_dve, g * STEP + start), g + k)
                    dve.wait_ge(s_mp, g + (NA * l + 1))
                    dve.tensor_tensor(mrow[:, bass.ds(g * AW, AW)], bank[2][0:B, 0:AW], bad[:, bass.ds(g * AW, AW)],
                                      ALU.add).then_inc(s_mr, 1)
                dve.wait_ge(s_mr, FREE + MR * l + NA)
                m6 = mrow[:].rearrange("b (v n) -> b v n", n=C)
                for half in range(2):
                    dve.tensor_copy(mrep[:, 2 * half:2 * half + 2, :, :], m6[:, 3 * half:3 * half + 2, C - CR:C].unsqueeze(2)
                                    .to_broadcast([B, 2, 3, CR])).then_inc(s_mr, 1)
                dve.wait_ge(s_tp, l + 1)
                src = bank[6][:, 0:18 * B].rearrange("p (v c b) -> p v c b", v=6, c=3)
                for n in range(4):
                    for c, rows in ((slice(0, 2), 128), (slice(2, 3), KCH[2])):
                        dve.tensor_scalar(mods[0:rows, l, n, c, :], src[0:rows, n, c, :], float(n % 2), None, ALU.add)
                dve.tensor_copy(T["gates"][:, l, :, :, :], src[0:KC, 4:6, :, :]).then_inc(s_md, 1)

            def steps_alone(count, k, start):
                with dve.Fori(0, count) as n:
                    step(Order(dve, s_dve, n * STEP + start), n + k)

            k, start = 0, link.n
            steps_alone(WAIT_SKEW, k, start)
            k, start = k + WAIT_SKEW, start + WAIT_SKEW * STEP
            mods_of(0, k, start)
            k, start = k + MODS, start + MODS * STEP
            link = Order(dve, s_dve, start)
            dve.wait_ge(s_upT, 1)
            t4 = bank[3][0:D0, 0:B * D0].rearrange("p (b j) -> p b j", b=B)
            link(dve.tensor_tensor(A[:, 1, :, :], t4, Up[:], ALU.subtract))
            link(dve.tensor_scalar(A[:, 0, :, :], A[:, 1, :, :], -1.0, None, ALU.mult))
            dve.tensor_tensor(Ab[:], A[:, 0, :, :], A[:, 1, :, :], ALU.max).then_inc(s_abs, 1)
            dve.wait_ge(s_n1p, 1)
            link(dve.tensor_reduce(nrm1[:], bank[7][0:D0, 0:B * D0].rearrange("p (b j) -> p b j", b=B), AX_X, ALU.max))
            for i in range(NSQ):
                last = dve.tensor_scalar(again[:, i, :], nrm1[:], float(2 ** i), None, ALU.is_gt)
            link(last)
            link(dve.tensor_scalar(halves[:], again[:], -0.5, 1.0, ALU.mult, ALU.add))
            link(dve.tensor_copy(down[:], halves[:, 0, :]))
            for i in range(1, NSQ):
                link(dve.tensor_tensor(down[:], down[:], halves[:, i, :], ALU.mult))
            for i in range(2):
                link(dve.tensor_tensor(A[:, i, :, :], A[:, i, :, :], down[:].unsqueeze(2).to_broadcast([D0, B, D0]), ALU.mult))
            eye4 = eyeB[:, 0, :, :]
            dve.wait_ge(s_mask, 7)
            dve.scalar_tensor_tensor(hor[:, 0, :, :], A[:, 0, :, :], 1.0 / TAYLOR, eye4, ALU.mult, ALU.add).then_inc(s_h, 1)
            dve.wait_ge(s_inv, TAYLOR - 1)
            start = link.n
            with dve.Fori(0, HORNER // 2) as m:
                link = Order(dve, s_dve, m * (2 * STEP) + start)
                for n in range(2):
                    step(link, 2 * m + (k + n))
                    dve.wait_ge(s_hp, 2 * m + (n + 1))
                    dve.wait_ge(s_h, 2 * m + (n + 1))
                    dve.scalar_tensor_tensor(hor[:, 1 - n, :, :], bank[4][0:D0, 0:B * D0].rearrange("p (b j) -> p b j", b=B),
                                             inv[:, one(2 * m + n)], eye4, ALU.mult, ALU.add).then_inc(s_h, 1)
            k, start = k + HORNER, start + HORNER * STEP
            link = Order(dve, s_dve, start)
            dve.wait_ge(s_h, TAYLOR)
            link(dve.tensor_copy(R[:, 0, 0, :, :], hor[:, (TAYLOR - 1) % 2, :, :]))
            dve.wait_ge(s_rT, 1)
            dve.tensor_copy(R[:, 0, 1, :, :], bank[5][0:D0, 0:B * D0].rearrange("p (b j) -> p b j", b=B)).then_inc(s_R, 1)
            start = link.n
            turn = 2 * (STEP + 3)
            with dve.Fori(0, SQUARES // 2) as m:
                link = Order(dve, s_dve, m * turn + start)
                for n in range(2):
                    step(link, 2 * m + (k + n))
                    flat = lambda x: x.rearrange("p i b j -> p (i b) j")
                    dve.wait_ge(s_sqp, 2 * m + (n + 1))
                    dve.wait_ge(s_R, 2 * m + (n + 1))
                    link(dve.tensor_tensor(flat(dif[:]), bank[4][0:D0, :].rearrange("p (n j) -> p n j", j=D0),
                                           flat(R[:, n, :, :, :]), ALU.subtract))
                    for i in range(2):
                        dve.tensor_tensor(dif[:, i, :, :], dif[:, i, :, :],
                                          again[:, bass.ds(2 * m + n, 1), :].squeeze(1).unsqueeze(2).to_broadcast([D0, B, D0]),
                                          ALU.mult).then_inc(s_dve, 1)
                    link.pass_by(2)
                    dve.wait_ge(s_dve, link.n)
                    dve.tensor_tensor(R[:, 1 - n, :, :, :], R[:, n, :, :, :], dif[:], ALU.add).then_inc(s_R, 1)
            k, start = k + SQUARES, start + SQUARES // 2 * turn
            for l in range(1, NL):
                mods_of(l, k, start)
                k, start = k + MODS, start + MODS * STEP
            dve.wait_ge(s_x, 16 * B)
            with dve.Fori(0, XT) as b:
                dve.wait_ge(s_xt, FREE + NK * b)
                dve.tensor_copy(xs[:], X[:, bass.ds(b * NT, NT), :]).then_inc(s_xs, 1)
                step(Order(dve, s_dve, b * STEP + start), b + k)
                for c in range(NK):
                    dve.wait_ge(s_xt, FREE + b * NK + c + 1)
                    dve.tensor_copy(xT[:, c, tokens(b, 0, NTOK)], bank[4 + c][0:KC, :]).then_inc(s_xT, 1)
            k, start = k + XT, start + XT * STEP
            steps_alone(REST, k, start)
            link = Order(dve, s_dve, start + REST * STEP)
            dve.wait_ge(s_R, NSQ + 1)
            link(dve.tensor_tensor(Rm[:], R[:, NSQ % 2, 1, :, :], eye4, ALU.subtract))
            dve.wait_ge(s_kept, FREE + 2 * D0)
            dve.wait_ge(s_mask, 7)
            link(dve.tensor_tensor(cdia[:], crow[0:D0, :], ident[0:D0, 0:D0], ALU.mult))
            link(dve.tensor_reduce(ccol[:], cdia[:], AX_X, ALU.add))
            dve.wait_ge(s_gp, 1)
            gram = bank[2][0:D0, 0:D0]
            link(dve.tensor_tensor(cdia[:], gram, crow[0:D0, :], ALU.mult))
            link(dve.tensor_tensor(Xn[:, 0, 1, :], cdia[:], lower[:], ALU.mult))
            link(dve.tensor_tensor(PT[:, 0, :], ident[0:D0, 0:D0], Xn[:, 0, 1, :], ALU.subtract))
            dve.scalar_tensor_tensor(Xn[:, 0, 0, :], gram, ccol[:, 0:1], upper[:], ALU.mult, ALU.mult).then_inc(s_X, 1)
            dve.wait_ge(s_vT, 1)
            dve.tensor_copy(VT[:], bank[3][0:D0, 0:C]).then_inc(s_PT, 1)
            for n in range(5):
                dve.wait_ge(s_xp, n + 1)
                dve.tensor_copy(Xn[:, (n + 1) % 2, :, :], bank[4][0:D0, 0:2 * D0].rearrange("p (i j) -> p i j", i=2)).then_inc(s_X, 1)
                dve.wait_ge(s_xr, n + 1)
                dve.wait_ge(s_PT, n + 1)
                dve.tensor_tensor(PT[:, (n + 1) % 2, :], bank[5][0:D0, 0:D0], PT[:, n % 2, :], ALU.add).then_inc(s_PT, 1)
            dve.wait_ge(s_PT, 6)
            dve.tensor_scalar(Tt[:], PT[:, 1, :], ccol[:, 0:1], None, ALU.mult).then_inc(s_Tt, 1)
            dve.wait_ge(s_yp, 1)
            dve.tensor_copy(Y[:], bank[6][0:D0, 0:D0]).then_inc(s_Y, 1)
            dve.wait_ge(s_up2, 2)
            dve.tensor_tensor(U[:], eye3[:, :, 0:D0], bank[7][0:KC, 0:NK * D0].rearrange("p (c d) -> p c d", c=NK),
                              ALU.subtract).then_inc(s_U, 1)
            link(dve.tensor_scalar(UT[:], bank[2][0:D0, 0:C], -1.0, None, ALU.mult))
            dve.tensor_tensor(UT[:, 0:D0], UT[:, 0:D0], ident[0:D0, 0:D0], ALU.add).then_inc(s_U, 1)
            for b in range(B):
                dve.wait_ge(s_fp, b + 1)
                dve.tensor_copy(F[:, b, :], bank[3 + b % 2][0:D0, 0:C]).then_inc(s_F, 1)
            with dve.Fori(0, B) as b:
                dve.wait_ge(s_zp, b + 1)
                dve.wait_ge(s_dp, FREE + b * NT)
                dve.tensor_copy(zT[:], bank[7][0:D0, :]).then_inc(s_z, 1)
                for t in range(NT):
                    xt = X[:, one(b * NT + t), :].squeeze(1)
                    dve.wait_ge(s_dp, FREE + b * NT + t + 1)
                    dve.tensor_tensor(xt, xt, bank[t][:, 0:C], ALU.add).then_inc(s_d, 1)


HD_ROWS = [6 * D, 5 * D, 5 * D]
QK_OFF = [0, 6 * D, 11 * D]
NTRI = 6
PRODUCTS = [(0, 0), (0, 1), (0, 2), (1, 0), (1, 1), (2, 0)]
KS_ROWS = len(PRODUCTS) * D
MID = 4
LEAD = 6


class Uses:

    def __init__(self, banks, turns=0, k=0):
        self.banks, self.turns, self.k = banks, turns, k

    @property
    def n(self):
        return self.turns + self.k

    @property
    def bank(self):
        return self.banks[self.k % 2]


def attention_half(nc, io, T, l):
    X, ident, mods = T["x"], T["ident"], T["mods"]
    with nc.cleanup_on_exit(), ExitStack() as ctx:
        def sb(name, shape, dt=F32):
            return ctx.enter_context(nc.sbuf_tensor(f"a{l}_{name}", shape, dt))

        def ps(name, shape=(128, 512)):
            return ctx.enter_context(nc.psum_tensor(f"a{l}_{name}", list(shape), F32))

        def sem(name):
            return nc.alloc_semaphore(f"a{l}_{name}")

        W = T["w_att"]
        qkb = sb("qk_bias", [6 * D, 2, NK])
        bv = sb("v_bias", [128, C])
        bp = sb("proj_bias", [128, C])
        st6 = sb("ln_stats", [128, NT, 6])
        mv = sb("ln_mean_var", [128, NT, 2])
        ve = sb("ln_var_eps", [128, NT])
        rstd = sb("ln_rstd", [128, NT])
        xn = sb("normalized", [128, NT, CX])
        hT = (sb("h_parts", [128, 2, 2, NTOK], F16), sb("h_rest", [KCH[2], NTOK], F16))
        v32 = sb("h_or_qk32", [128, 2, NTOK])
        rest = sb("h_or_qk_rest", [128, NTOK])
        PT3 = sb("qk_parts", [6 * D, 2, NK, 3, NTOK], BF16)
        Vn = sb("v_next", [128, NT, H, D])
        V = sb("v_with_ones", [128, NT, H, 32])
        QS = sb("q_stack", [128, 2, H, NTOK], BF16)
        KS = sb("k_stack", [128, 2, H, NTOK], BF16)
        MX = sb("minus_max", [128, 2, 16])
        MT = sb("minus_max_T", [16, 2, 128], BF16)
        E = sb("exp_scores", [128, 2, 4, NTOK])
        oT = sb("o_T", [128, 4, NTOK])
        rs = sb("sum_inverse", [128, H])
        on = sb("o_normalized", [128, 2, CX])
        oP = [(sb(f"o_parts{t}", [128, 2, 2, 128], F16), sb(f"o_rest{t}", [KCH[2], 128], F16)) for t in range(2)]
        gcol = sb("gate_of_batch", [KC, NK])
        gbc = sb("gate_rows", [128, C])
        st_banks = [ps(f"st{i}") for i in range(2)]
        mx_banks = [ps(f"mx{i}") for i in range(2)]
        dd_banks = [ps(f"dd{i}") for i in range(2)]
        av = [ps(f"av{i}") for i in range(2)]

        s_small, s_w, s_set = sem("biases_in"), sem("w1_split"), sem("constants_set")
        s_dve, s_var, s_rstd, s_xn = sem("dve_order"), sem("var_ready"), sem("rstd_ready"), sem("xn_ready")
        s_h, s_part, s_V, s_go = sem("h_ready"), sem("qk_parts_ready"), sem("v_ready"), sem("waits_taken")
        s_stk = [sem(f"stack{i}_loaded") for i in range(NTRI)]
        s_st, s_str = sem("st_written"), sem("st_read")
        s_mm, s_mmr = sem("mx_written"), sem("mx_read")
        s_dd, s_ddr = sem("dd_written"), sem("dd_read")
        s_mt, s_md, s_av, s_oT = sem("max_T_ready"), sem("max_row_loaded"), sem("av_unit_done"), sem("o_T_ready")
        s_vn, s_y, s_yg, s_x = sem("v_next_ready"), sem("branch_ready"), sem("branch_gated"), sem("x_updated")
        s_g, s_O, s_oh = sem("gate_picked"), sem("o_tokens_ready"), sem("o_parts_ready")
        block = ctx.enter_context(nc.Block())

        QKV_ST, QKV_DD = 8, 5
        ATT_ST, ATT_MM, ATT_DD = 4 * H, 4 * H, 4
        PROJ_MM, PROJ_DD = 2 * NT, 1 + NT
        TURN_ST, TURN_MM, TURN_DD = QKV_ST + ATT_ST, ATT_MM + PROJ_MM, QKV_DD + ATT_DD + PROJ_DD
        FIRST_ST, FIRST_MM, FIRST_DD = QKV_ST, 4 * LEAD, QKV_DD + 1
        BEFORE_ST, BEFORE_MM, BEFORE_DD = FIRST_ST + TURN_ST, FIRST_MM + ATT_MM, FIRST_DD + ATT_DD + QKV_DD

        @block.sync
        def _(sp):
            load_w1(sp, io, T["staging"], T["mlp_of"][l][0], T["s_raw"])
            sp.dma_start(qkb[:], io[f"qk_b{l}"]).then_inc(s_small, 16)
            sp.dma_start(bv[:], io[f"qkv_b{l}"][2 * C:3 * C].partition_broadcast(128)).then_inc(s_small, 16)
            sp.dma_start(bp[:], io[f"proj_b{l}"].partition_broadcast(128)).then_inc(s_small, 16)

            def stacks(i):
                sp.wait_ge(s_part, 6 * i + 6)
                if not isinstance(i, int):
                    sp.wait_ge(s_st, FIRST_ST + TURN_ST * (i - 1))
                for s in range(NTRI):
                    n = min(3, H - 3 * s)
                    for side, S in ((1, KS), (0, QS)):
                        for r, pq in enumerate(PRODUCTS):
                            sp.dma_start(S[r * D:(r + 1) * D, one(i % 2), 3 * s:3 * s + n, :].squeeze(1),
                                         PT3[s * D:(s + 1) * D, side, 0:n, pq[side], :]).then_inc(s_stk[s], 16)

            sp.wait_ge(s_set, 3)
            stacks(0)
            stacks(1)
            with sp.Fori(0, B - 2) as i:
                stacks(i + 2)
            sp.wait_ge(s_w, 2)
            load_w2(sp, io, T["staging"], T["mlp_of"][l][0], T["s_raw"])

        w1_raw = T["raw_count"] + RAW_W1
        T["raw_count"] += RAW_W1 + 16

        @block.gpsimd
        def _(pool):
            def rsqrt(i):
                pool.wait_ge(s_var, i + 1)
                pool.tensor_tensor(rstd[:], ve[:], T["minus_half"][:], ALU.pow).then_inc(s_rstd, 1)
                pool.wait_ge(s_rstd, i + 1)

            rsqrt(0)
            for i in range(2):
                pool.memset(KS[96:KS_ROWS + 1, i, :, :], 1.0).then_inc(s_set, 1)
                pool.wait_ge(s_set, i + 1)
            pool.memset(V[:], 1.0).then_inc(s_set, 1)
            pool.wait_ge(s_set, 3)

            def max_row(i, g):
                pool.wait_ge(s_mt, 4 * i + g + 1)
                pool.sem_inc(s_go, 1)
                pool.dma_start(QS[KS_ROWS:KS_ROWS + 1, one(i % 2), 4 * g:4 * g + 4, :].squeeze(1),
                               MT[:, g % 2, :]).then_inc(s_md, 16)

            def update(i):
                for t in range(NT):
                    yt, xt = xn[:, t, 0:C], X[:, one(i * NT + t), :].squeeze(1)
                    pool.wait_ge(s_y, NT * i + t + 1)
                    pool.tensor_tensor(yt, yt, gbc[:], ALU.mult).then_inc(s_yg, 1)
                    pool.wait_ge(s_yg, NT * i + t + 1)
                    pool.sem_inc(s_go, 1)
                    pool.tensor_tensor(xt, xt, yt, ALU.add).then_inc(s_x, 1)
                    pool.wait_ge(s_x, FREE + NT * i + t + 1)

            free_at_start(pool, s_x)
            max_row(0, 0)
            rsqrt(1)
            for g in (1, 2, 3):
                max_row(0, g)
            max_row(1, 0)
            with pool.Fori(1, B - 1) as i:
                rsqrt(i + 1)
                max_row(i, 1)
                update(i - 1)
                for g in (2, 3):
                    max_row(i, g)
                max_row(i + 1, 0)
            max_row(B - 1, 1)
            update(B - 2)
            for g in (2, 3):
                max_row(B - 1, g)
            update(B - 1)
            pool.wait_ge(s_md, 16 * 4 * B)

        @block.scalar
        def _(act):
            free_at_start(act, s_oT, s_str)

            def h_chunks(i, st):
                for n, c in enumerate((0, 2)):
                    act.wait_ge(s_st, st.n + 1)
                    if not first(i):
                        act.wait_ge(s_part, 6 * i)
                    for to in (part_of(hT, c, 0, slice(0, NTOK)), v32[0:KCH[c], n, :]):
                        a = act.activation(to, st.bank[0:KCH[c], :], ACT.Identity, bias=mods[0:KCH[c], l, 0, c, one(i)],
                                           scale=mods[0:KCH[c], l, 1, c, one(i)])
                    a.then_inc(s_str, 1)
                    st.k += 1

            def qk(i, st):
                act.wait_ge(s_small, 48)
                if not first(i):
                    for s in range(NTRI):
                        act.wait_ge(s_stk[s], 16 * 12 * i)
                for n in range(6):
                    side, c = 1 - n // NK, n % NK
                    M = HD_ROWS[c]
                    act.wait_ge(s_st, st.n + 1)
                    if n < 2:
                        act.wait_ge(s_h, NK * i + 1 + 2 * n)
                    else:
                        act.wait_ge(s_part, 6 * i + n - 1)
                    for to in (PT3[0:M, side, c, 0, :], v32[0:M, n % 2, :]):
                        a = act.activation(to, st.bank[0:M, :], ACT.Identity, bias=qkb[0:M, side, c:c + 1], scale=1.0 / WS)
                    a.then_inc(s_str, 1)
                    st.k += 1

            def attend(i, st, new):
                act.wait_ge(s_vn, i + 1)
                act.wait_ge(s_set, 3)
                act.activation(V[:, :, :, 0:D], Vn[:], ACT.Copy).then_inc(s_V, 1)
                for U in range(16):
                    if U == MID and new is not None:
                        h_chunks(new, st)
                    if U == MID + 1 and new is not None:
                        qk(new, st)
                    for hd in range(4):
                        act.wait_ge(s_av, FREE + 16 * i + max(0, U - 1))
                        act.wait_ge(s_st, st.n + 1)
                        act.activation(E[:, U % 2, hd, :], st.bank[:], ACT.Exp, scale=float(D) ** -0.5).then_inc(s_str, 1)
                        st.k += 1
                    if U % 4 == 1 and U > 1:
                        o_group(i, U // 4 - 1)
                o_group(i, 3)

            def o_group(i, g):
                act.wait_ge(s_av, FREE + 16 * i + 4 * g + 4)
                if not first(i):
                    act.wait_ge(s_O, NT * i)
                act.activation(oT[:, g, :], av[g % 2][:], ACT.Copy).then_inc(s_oT, 1)

            st = Uses(st_banks)
            h_chunks(0, st)
            qk(0, st)
            attend(0, st, 1)
            with act.Fori(1, B - 1) as i:
                attend(i, Uses(st_banks, TURN_ST * (i - 1), BEFORE_ST), i + 1)
            attend(B - 1, Uses(st_banks, 0, BEFORE_ST + (B - 2) * TURN_ST), None)

        @block.tensor
        def _(pe):
            free_at_start(pe, s_av)

            def h_chunk(i, c, use, written, read):
                pe.wait_ge(s_xn, 2 * NT * (i + 1))
                pe.wait_ge(read, FREE + use.n - 1)
                for t in range(NT):
                    mm = pe.transpose(use.bank[0:KCH[c], t * 128:(t + 1) * 128], xn[:, t, c * 128:c * 128 + KCH[c]], ident[:])
                mm.then_inc(written, 1)
                use.k += 1

            def qk_tile(i, n, st):
                pe.wait_ge(s_h, NK * (i + 1))
                pe.wait_ge(s_str, FREE + st.n - 1)
                side, c = 1 - n // NK, n % NK
                to = side * C + QK_OFF[c]
                dense(pe, st.bank[0:HD_ROWS[c], :], W, slice(to, to + HD_ROWS[c]), hT, slice(0, NTOK), True, s_st)
                st.k += 1

            def v_tile(t, dd):
                pe.wait_ge(s_ddr, FREE + dd.n - 1)
                dense(pe, dd.bank[:, 0:C], hT, slice(t * 128, (t + 1) * 128), W, slice(2 * C, 3 * C), False, s_dd)
                dd.k += 1

            def by_token(i, t, mm):
                pe.wait_ge(s_oT, FREE + 4 * (i + 1))
                pe.wait_ge(s_mmr, FREE + mm.n - 1)
                for g in range(4):
                    tr = pe.transpose(mm.bank[:, g * 128:(g + 1) * 128], oT[:, g, t * 128:(t + 1) * 128], ident[:])
                tr.then_inc(s_mm, 1)
                mm.k += 1

            def by_channel(i, t, mm):
                pe.wait_ge(s_O, NT * i + t + 1)
                pe.wait_ge(s_mmr, FREE + mm.n - 1)
                for c in range(NK):
                    tr = pe.transpose(mm.bank[0:KCH[c], c * 128:(c + 1) * 128], on[:, t % 2, c * 128:c * 128 + KCH[c]], ident[:])
                tr.then_inc(s_mm, 1)
                mm.k += 1

            def proj_tile(i, t, dd):
                pe.wait_ge(s_oh, 2 * (NT * i + t + 1))
                pe.wait_ge(s_ddr, FREE + dd.n - 1)
                dense(pe, dd.bank[:, 0:C], oP[t % 2], slice(0, 128), W, slice(3 * C, 4 * C), False, s_dd)
                dd.k += 1

            def scores_for_max(i, h, t, mm):
                if t == 0:
                    pe.wait_ge(s_stk[h // 3], 16 * 12 * (i + 1))
                pe.wait_ge(s_mmr, FREE + mm.n - 1)
                pe.matmul(mm.bank[:], QS[0:KS_ROWS, one(i % 2), h, t * 128:(t + 1) * 128].squeeze(1),
                          KS[0:KS_ROWS, one(i % 2), h, :].squeeze(1), start=True, stop=True).then_inc(s_mm, 1)
                mm.k += 1

            def transpose_maxima(g, taken, dd):
                pe.wait_ge(s_mmr, FREE + taken)
                pe.wait_ge(s_ddr, FREE + dd.n - 1)
                pe.transpose(dd.bank[0:16, 0:128], MX[:, g % 2, :], ident[:]).then_inc(s_dd, 1)
                dd.k += 1

            def gate(i, dd):
                pe.wait_ge(s_g, i + 1)
                pe.wait_ge(s_ddr, FREE + dd.n - 1)
                for c in range(NK):
                    m = pe.matmul(dd.bank[:, c * KC:(c + 1) * KC], gcol[:, c:c + 1].to_broadcast([KC, 128]),
                                  ident[0:KC, 0:KC], start=True, stop=True)
                m.then_inc(s_dd, 1)
                dd.k += 1

            def attend(i, st, mm, dd, done, new):
                last = new is None
                exps = []
                for U in range(17):
                    if U == 1:
                        pe.wait_ge(s_V, i + 1)
                    if U == MID and new is not None:
                        h_chunks(new, st, dd)
                    if U == MID + 1:
                        between(done, new, st, mm, dd)
                    g, j = U // 4, U % 4
                    hm = U + LEAD
                    more = U < 16 and (hm < H or not last)
                    for hd in range(4):
                        h = 4 * g + hd
                        if U < 16:
                            if j == 0 and hd == 0:
                                pe.wait_ge(s_md, 16 * (4 * i + g + 1))
                                pe.wait_ge(s_stk[(h + 3) // 3], 16 * 12 * (i + 1))
                            pe.wait_ge(s_str, FREE + st.n - 1)
                            pe.matmul(st.bank[:], KS[0:KS_ROWS + 1, one(i % 2), h, j * 128:(j + 1) * 128].squeeze(1),
                                      QS[0:KS_ROWS + 1, one(i % 2), h, :].squeeze(1), start=True, stop=True).then_inc(s_st, 1)
                            st.k += 1
                            exps.append(st.n)
                        if more:
                            scores_for_max(i + hm // H, hm % H, hd, mm)
                        if U > 0:
                            g1, j1 = (U - 1) // 4, (U - 1) % 4
                            if j1 == 0 and hd == 0:
                                pe.wait_ge(s_oT, FREE + 4 * i + max(0, g1 - 1))
                            pe.wait_ge(s_str, FREE + exps[4 * (U - 1) + hd])
                            m = pe.matmul(av[g1 % 2][32 * hd:32 * hd + 32, :], V[:, j1, 4 * g1 + hd, :],
                                          E[:, (U - 1) % 2, hd, :], start=(j1 == 0), stop=(j1 == 3))
                        if hd == 2 and U < 16 and (hm - 1) % 4 == 3 and (hm - 1 < H or not last):
                            transpose_maxima((hm - 1) // 4, mm.n - (3 if more else 0), dd)
                    if U > 0:
                        m.then_inc(s_av, 1)

            def h_chunks(new, st, dd):
                h_chunk(new, 0, st, s_st, s_str)
                h_chunk(new, 1, dd, s_dd, s_ddr)
                h_chunk(new, 2, st, s_st, s_str)

            def between(done, new, st, mm, dd):
                if done is not None:
                    by_token(done, 0, mm)
                    gate(done, dd)
                    by_token(done, 1, mm)
                for n in range(6):
                    if new is not None:
                        qk_tile(new, n, st)
                    if done is not None and 2 <= n < 2 + NT:
                        proj_tile(done, n - 2, dd)
                    if done is not None and n < NT:
                        by_channel(done, n, mm)
                        if n < 2:
                            by_token(done, n + 2, mm)
                    if new is not None and n < NT:
                        v_tile(n, dd)

            st, mm, dd = Uses(st_banks), Uses(mx_banks), Uses(dd_banks)
            h_chunks(0, st, dd)
            between(None, 0, st, mm, dd)
            for h in range(LEAD):
                for t in range(4):
                    scores_for_max(0, h, t, mm)
                if h == 4:
                    transpose_maxima(0, 16, dd)
            attend(0, st, mm, dd, None, 1)
            with pe.Fori(1, B - 1) as i:
                st, mm = Uses(st_banks, TURN_ST * (i - 1), BEFORE_ST), Uses(mx_banks, TURN_MM * (i - 1), BEFORE_MM)
                dd = Uses(dd_banks, TURN_DD * (i - 1), BEFORE_DD)
                attend(i, st, mm, dd, i - 1, i + 1)
            st = Uses(st_banks, 0, BEFORE_ST + (B - 2) * TURN_ST)
            mm = Uses(mx_banks, 0, BEFORE_MM + (B - 2) * TURN_MM)
            dd = Uses(dd_banks, 0, BEFORE_DD + (B - 2) * TURN_DD)
            attend(B - 1, st, mm, dd, B - 2, None)
            between(B - 1, None, st, mm, dd)

        @block.vector
        def _(dve):
            free_at_start(dve, s_mmr, s_ddr)

            def norm(link, i, tiles):
                for t in tiles:
                    link(dve.bn_stats(st6[:, t, :], X[:, one(i * NT + t), :].squeeze(1)))
                if tiles[-1] < NT - 1:
                    return
                dve.sem_inc(s_go, 1)
                for t in range(NT):
                    dve.bn_aggr(mv[:, t, :], st6[:, t, :]).then_inc(s_dve, 1)
                link.pass_by(NT)
                dve.wait_ge(s_dve, link.n)
                dve.tensor_scalar_add(ve[:], mv[:, :, 1:2].squeeze(2), EPS).then_inc(s_var, 1)

            def normalize(i, tiles):
                dve.wait_ge(s_rstd, i + 1)
                if not isinstance(i, int):
                    dve.wait_ge(s_x, FREE + NT * (i - 2))
                for t in tiles:
                    normalized_rows(dve, xn[:, t, :], X[:, one(i * NT + t), :].squeeze(1), mv[:, t, 0:1], rstd[:, t:t + 1], s_xn)

            def modulated(link, i, st, dd):
                for n, c in enumerate((0, 1, 2)):
                    src = v32[0:KCH[c], c // 2, :]
                    if c == 1:
                        src = rest[:]
                        dve.wait_ge(s_dd, dd.n + 1)
                        dve.tensor_scalar(src, dd.bank[:], mods[:, l, 1, c, one(i)], mods[:, l, 0, c, one(i)],
                                          ALU.mult, ALU.add).then_inc(s_ddr, 1)
                        dve.wait_ge(s_ddr, FREE + dd.n + 1)
                        dd.k += 1
                    else:
                        dve.wait_ge(s_str, FREE + st.n + 1)
                        st.k += 1
                    if c == 1:
                        link(dve.tensor_copy(part_of(hT, c, 0, slice(0, NTOK)), src))
                    low_chunk(dve, hT, c, slice(0, NTOK), src).then_inc(s_h, 1)

            def qk_split(link, i, n, st):
                side, c = 1 - n // NK, n % NK
                M = HD_ROWS[c]
                src = v32[0:M, n % 2, :]
                P = lambda p: PT3[0:M, side, c, p, :]
                dve.wait_ge(s_str, FREE + st.n + 1)
                st.k += 1
                link(dve.tensor_tensor(rest[0:M, :], src, P(0), ALU.subtract))
                link(dve.tensor_copy(P(1), rest[0:M, :]))
                dve.tensor_tensor(P(2), rest[0:M, :], P(1), ALU.subtract).then_inc(s_part, 1)
                dve.wait_ge(s_part, 6 * i + n + 1)

            def v_rows(i, t, dd):
                if t == 0 and not first(i):
                    dve.wait_ge(s_V, i)
                dve.wait_ge(s_dd, dd.n + 1)
                dve.scalar_tensor_tensor(Vn[:, t, :, :].rearrange("p h d -> p (h d)"), dd.bank[:, 0:C], 1.0 / WS, bv[:],
                                         ALU.mult, ALU.add).then_inc(s_ddr, 1)
                dd.k += 1
                if t == NT - 1:
                    dve.wait_ge(s_ddr, FREE + dd.n)
                    dve.sem_inc(s_vn, 1)

            def take_max(i, h, t, mm):
                dve.wait_ge(s_mm, mm.n + 1)
                at0 = 4 * (h % 4) + t
                dve.tensor_reduce(MX[:, h // 4 % 2, at0:at0 + 1], mm.bank[:], AX_X, ALU.max, negate=True).then_inc(s_mmr, 1)
                mm.k += 1

            def maxima_row(i, g, dd):
                dve.wait_ge(s_dd, dd.n + 1)
                if not first(i):
                    dve.wait_ge(s_md, 16 * (4 * i + max(1, g - 1)))
                dve.tensor_copy(MT[:, g % 2, :], dd.bank[0:16, 0:128]).then_inc(s_mt, 1)
                dve.wait_ge(s_mt, 4 * i + g + 1)
                dve.sem_inc(s_ddr, 1)
                dd.k += 1

            def attend(link, i, st, mm, dd, done, new):
                last = new is None
                for U in range(16):
                    hm = U + LEAD
                    if last and U == H - LEAD + 1:
                        split_next_weights(link)
                    if new is not None and U < 2:
                        norm(link, new, (2 * U, 2 * U + 1))
                    elif new is not None and U < 4:
                        normalize(new, (2 * U - 4, 2 * U - 3))
                    if U == MID and new is not None:
                        modulated(link, new, st, dd)
                        st.k += 4
                    if U == MID + 1:
                        between(link, done, new, st, mm, dd)
                    for hd in range(4):
                        if hm < H or not last:
                            take_max(i + hm // H, hm % H, hd, mm)
                        if hd == 2 and (hm - 1) % 4 == 3 and (hm - 1 < H or not last):
                            maxima_row(i, (hm - 1) // 4, dd)

            def split_next_weights(link):
                src, (whole, low) = by_chunk(T["staging"]), T["w1_parts"]
                dve.wait_ge(T["s_raw"], w1_raw)
                link(dve.tensor_scalar(whole[:, 0, :, :], src[:, 0:2, :], WS, None, ALU.mult))
                link(dve.tensor_scalar(low[:], src[0:KCH[2], 2, :], WS, None, ALU.mult))
                dve.scalar_tensor_tensor(whole[:, 1, :, :], src[:, 0:2, :], WS, whole[:, 0, :, :], ALU.mult,
                                         ALU.subtract).then_inc(s_w, 1)
                dve.scalar_tensor_tensor(low[LOW_W, :], src[LOW_W, 2, :], WS, low[LOW_W, :], ALU.mult,
                                         ALU.subtract).then_inc(s_w, 1)

            def pick_gate(i):
                dve.tensor_copy(gcol[:], T["gates"][:, l, 0, :, one(i)].squeeze(2)).then_inc(s_g, 1)

            def o_rows(link, i, t, mm):
                o = mm.bank[:].rearrange("p (h e) -> p h e", e=32)
                dve.wait_ge(s_mm, mm.n + 1)
                link(dve.reciprocal(rs[:], o[:, :, D:D + 1].squeeze(2)))
                link(dve.tensor_tensor(on[:, t % 2, 0:C].rearrange("p (h d) -> p h d", d=D), o[:, :, 0:D],
                                       rs[:].unsqueeze(2).to_broadcast([128, H, D]), ALU.mult))
                dve.tensor_copy(on[:, t % 2, C:CX].rearrange("p (j r) -> p j r", r=CR),
                                on[:, t % 2, C - CR:C].unsqueeze(1).to_broadcast([128, 2, CR])).then_inc(s_O, 1)
                dve.wait_ge(s_O, NT * i + t + 1)
                dve.sem_inc(s_mmr, 1)
                mm.k += 1

            def o_split(link, i, t, mm):
                dve.wait_ge(s_mm, mm.n + 1)
                whole, low = oP[t % 2]
                src, srcr = mm.bank[:, 0:256].rearrange("p (c n) -> p c n", c=2), mm.bank[0:KCH[2], 256:384]
                dve.tensor_copy(whole[:, 0, :, :], src).then_inc(s_dve, 1)
                dve.tensor_copy(low[:], srcr).then_inc(s_dve, 1)
                link.pass_by(2)
                dve.wait_ge(s_dve, link.n)
                dve.tensor_tensor(whole[:, 1, :, :], src, whole[:, 0, :, :], ALU.subtract).then_inc(s_oh, 1)
                dve.tensor_tensor(low[LOW_H, :], srcr[LOW_H, :], low[LOW_H, :], ALU.subtract).then_inc(s_oh, 1)
                dve.wait_ge(s_oh, 2 * (NT * i + t + 1))
                dve.sem_inc(s_mmr, 1)
                mm.k += 1

            def update(link, i, t, dd):
                y = xn[:, t, 0:C]
                dve.wait_ge(s_dd, dd.n + 1)
                dve.scalar_tensor_tensor(y, dd.bank[:, 0:C], 1.0 / WS, bp[:], ALU.mult, ALU.add).then_inc(s_ddr, 1)
                dve.wait_ge(s_ddr, FREE + dd.n + 1)
                dd.k += 1
                dve.sem_inc(s_y, 1)

            def between(link, done, new, st, mm, dd):
                if done is not None:
                    pick_gate(done)
                if done is not None:
                    o_rows(link, done, 0, mm)
                    dve.wait_ge(s_dd, dd.n + 1)
                    dve.wait_ge(s_x, FREE + NT * done)
                    dve.tensor_copy(gbc[:], dd.bank[:, 0:C]).then_inc(s_ddr, 1)
                    dd.k += 1
                    o_rows(link, done, 1, mm)
                if new is not None and not first(new):
                    for s in range(NTRI):
                        dve.wait_ge(s_stk[s], 16 * 12 * new)
                for n in range(6):
                    if new is not None:
                        qk_split(link, new, n, st)
                    if done is not None and 2 <= n < 2 + NT:
                        update(link, done, n - 2, dd)
                    if done is not None and n < NT:
                        o_split(link, done, n, mm)
                        if n < 2:
                            o_rows(link, done, n + 2, mm)
                    if new is not None and n < NT:
                        v_rows(new, n, dd)

            dve.wait_ge(s_small, 48)
            link = Order(dve, s_dve)
            st, mm, dd = Uses(st_banks), Uses(mx_banks), Uses(dd_banks)
            norm(link, 0, range(NT))
            normalize(0, range(NT))
            modulated(link, 0, st, dd)
            between(link, None, 0, st, mm, dd)
            for h in range(LEAD):
                for t in range(4):
                    take_max(0, h, t, mm)
                if h == 4:
                    maxima_row(0, 0, dd)
            st.k += 4 * MID
            attend(link, 0, st, mm, dd, None, 1)
            before, turn = link.n, 8 + 1 + 12 + NT * (2 + 2)
            with dve.Fori(1, B - 1) as i:
                link = Order(dve, s_dve, (i - 1) * turn + before)
                st, mm = Uses(st_banks, TURN_ST * (i - 1), BEFORE_ST + 4 * MID), Uses(mx_banks, TURN_MM * (i - 1), BEFORE_MM)
                dd = Uses(dd_banks, TURN_DD * (i - 1), BEFORE_DD)
                attend(link, i, st, mm, dd, i - 1, i + 1)
            link = Order(dve, s_dve, before + (B - 2) * turn)
            mm = Uses(mx_banks, 0, BEFORE_MM + (B - 2) * TURN_MM)
            dd = Uses(dd_banks, 0, BEFORE_DD + (B - 2) * TURN_DD)
            attend(link, B - 1, None, mm, dd, B - 2, None)
            between(link, B - 1, None, None, mm, dd)


def one(n):
    return slice(n, n + 1) if isinstance(n, int) else bass.ds(n, 1)


def first(i):
    return isinstance(i, int) and i == 0


def normalized_rows(dve, to, x, mean, rstd, sem):
    dve.tensor_scalar(to[:, 0:C], x, mean, rstd, ALU.subtract, ALU.mult).then_inc(sem, 1)
    dve.tensor_scalar(to[:, C:CX].rearrange("p (j r) -> p j r", r=CR), x[:, C - CR:C].unsqueeze(1).to_broadcast([128, 2, CR]),
                      mean, rstd, ALU.subtract, ALU.mult).then_inc(sem, 1)


def split_chunk(dve, link, pair, c, cols, src):
    link(dve.tensor_copy(part_of(pair, c, 0, cols), src))
    return low_chunk(dve, pair, c, cols, src)


def low_chunk(dve, pair, c, cols, src):
    hi, lo = (part_of(pair, c, 0, cols), part_of(pair, c, 1, cols)) if c < 2 else (pair[1][LOW_H, cols], pair[1][LOW_H, cols])
    return dve.tensor_tensor(lo, src if c < 2 else src[LOW_H], hi, ALU.subtract)


def mlp_half(nc, io, T, l):
    X, ident, mods = T["x"], T["ident"], T["mods"]
    passes = T["mlp_of"][l]
    routed = len(passes) > 1
    with nc.cleanup_on_exit(), ExitStack() as ctx:
        def sb(name, shape, dt=F32):
            return ctx.enter_context(nc.sbuf_tensor(f"m{l}_{name}", shape, dt))

        def ps(name):
            return ctx.enter_context(nc.psum_tensor(f"m{l}_{name}", [128, 512], F32))

        def sem(name):
            return nc.alloc_semaphore(f"m{l}_{name}")

        W1 = [T["w1_parts"]] + ([(sb("w1_odd", [128, 2, 2, FF], F16), sb("w1_odd_rest", [KCH[2], FF], F16))] if routed else [])
        W2 = [sb("w2_even", [128, 2, NF, C], F16)] + ([sb("w2_odd", [128, 2, NF, C], F16)] if routed else [])
        raw1 = T["staging"]
        raw2 = sb("w2_raw", [128, NF * C]) if routed else None
        b1 = sb("b1", [128, len(passes), NF])
        b2 = sb("b2_rows", [128, len(passes), C])
        st6 = sb("ln_stats", [128, NT, 6])
        mv = sb("ln_mean_var", [128, NT, 2])
        ve = sb("ln_var_eps", [128, NT])
        rstd = sb("ln_rstd", [128, NT])
        xn = sb("normalized", [128, NT, CX])
        h32 = sb("h32", [128, NTOK])
        hT = (sb("h_parts", [128, 2, 2, B * NTOK], F16), sb("h_rest", [KCH[2], B * NTOK], F16))
        gcol = sb("gate_of_batch", [KC, NK])
        gbc = sb("gate_rows", [128, B, C])
        g32 = sb("hidden32", [128, 2, NTOK])
        Hs = sb("hidden_parts", [128, 2, 3, NTOK], F16)
        y = sb("branch", [128, NT, C])
        wg = sb("router_w", [128, 3, NE])
        wgs = (sb("router_w_parts", [128, 2, 2, NE], F16), sb("router_w_rest", [KCH[2], NE], F16))
        lg = sb("logits", [128, NT, NE])
        cmp = sb("beaten_by", [128, NT, NE, NE])
        rank = sb("rank", [128, NT, NE])
        sel = sb("selected", [128, NT, NE])
        tot = sb("half_total", [128, NT])
        arg = sb("sigmoid_arg", [128, NT, NE])
        cw = sb("expert_weight", [128, B * NT, NE])
        hb = [ps(f"hidden{i}") for i in range(3)]
        ob = [ps(f"out{t}") for t in range(NT)]
        DD = ps("dd")

        s_small, s_raw2, s_w1, s_w2 = sem("biases_in"), sem("w2_raw_in"), sem("w1_split"), sem("w2_split")
        s_dve, s_var, s_rstd, s_xn, s_h = (sem("dve_order"), sem("var_ready"), sem("rstd_ready"),
                                                   sem("xn_ready"), sem("h_ready"))
        s_dd, s_ddev, s_g, s_th, s_arg, s_cw = (sem("dd_written"), sem("dd_read"), sem("gate_picked"), sem("tanh_ready"),
                                                sem("arg_ready"), sem("weights_ready"))
        s_hb, s_gelu, s_hs, s_out, s_ob, s_x = (sem("hidden_written"), sem("gelu_done"), sem("hidden_split"), sem("out_added"),
                                                sem("out_read"), sem("x_updated"))
        s_hi, s_wlo = sem("weights_high"), sem("attention_weights_split")
        s_wgs, s_clr, s_go = sem("router_w_split"), sem("cleared"), sem("waits_taken")
        block = ctx.enter_context(nc.Block())
        DDL = NK + 1 + (1 if routed else 0)
        UPDATES = (0, 3, 4, 6)
        PE_STEPS, DVE_STEPS = (4, 6, 8), (1, 2, 5, 7, 8)
        base_raw = T["raw_count"]

        @block.sync
        def _(sp):
            for n, m in enumerate(passes):
                sp.dma_start(b1[:, n, :], io[f"b1_{m}"]).then_inc(s_small, 16)
                sp.dma_start(b2[:, n, :], io[f"b2_{m}"].partition_broadcast(128)).then_inc(s_small, 16)
            if routed:
                load_rows(sp, wg[:], io["gate_w"], s_small)
            for n, m in enumerate(passes[1:], 1):
                if n == 1:
                    sp.wait_ge(s_w2, NF)
                else:
                    sp.wait_ge(s_w1, 2 * (n - 1))
                load_w1(sp, io, raw1, m, T["s_raw"])
                if n > 1:
                    sp.wait_ge(s_w2, NF * n)
                load_w2(sp, io, raw2, m, s_raw2)
            if l + 1 < NL:
                if routed:
                    sp.wait_ge(s_w1, 2 * (len(passes) - 1))
                else:
                    sp.wait_ge(s_w2, NF)
                load_attention_weights(sp, io, T, l + 1)

        T["raw_count"] = base_raw + RAW_W1 * (len(passes) - 1) + (2 * RAW_W1 if l + 1 < NL else 0)

        @block.gpsimd
        def _(pool):
            if routed:
                pool.memset(cmp[:], 0.0).then_inc(s_clr, 1)

            def rsqrt(i):
                pool.wait_ge(s_var, i + 1)
                pool.tensor_tensor(rstd[:], ve[:], T["minus_half"][:], ALU.pow).then_inc(s_rstd, 1)

            rsqrt(0)
            pool.wait_ge(T["s_raw"], base_raw)
            split_w2(pool, raw1, W2[0], s_hi, 0, s_w2)
            for i in range(1, B):
                rsqrt(i)
            done = NF
            for n in range(1, len(passes)):
                if n >= 2:
                    pool.wait_ge(s_out, FREE + NF * B * (n - 1))
                pool.wait_ge(T["s_raw"], base_raw + RAW_W1 * n)
                split_w1(pool, raw1, W1[n % 2], s_hi, done, s_w1)
                pool.wait_ge(s_raw2, 16 * n)
                split_w2(pool, raw2, W2[n % 2], s_hi, done + 2, s_w2)
                done += 2 + NF
            if l + 1 < NL:
                pool.wait_ge(T["s_raw"], T["raw_count"])
                split_attention_weights(pool, T, s_hi, done, s_wlo)

        @block.scalar
        def _(act):
            free_at_start(act, s_gelu, s_ob)
            act.wait_ge(s_small, 32 * len(passes) + (RAW_W1 if routed else 0))

            def hidden(n, i):
                k = (n * B + i) * NF
                for f in range(NF):
                    act.wait_ge(s_hb, k + f + 1)
                    act.wait_ge(s_hs, FREE + k + max(0, f - 1))
                    act.wait_ge(s_out, FREE + k + max(0, f - 2))
                    for to in (Hs[:, 0, f % 3, :], g32[:, f % 2, :]):
                        a = act.activation(to, hb[f % 3][:], ACT.Gelu_apprx_tanh, bias=b1[:, n, f:f + 1], scale=1.0 / WS)
                    a.then_inc(s_gelu, 1)
                act.wait_ge(s_out, FREE + k + NF)
                act.wait_ge(s_x, FREE + (n * B + i) * NT)
                for t in range(NT):
                    act.activation(y[:, t, :], ob[t][:, 0:C], ACT.Copy, scale=1.0 / WS).then_inc(s_ob, 1)

            def router(i):
                act.wait_ge(s_arg, i + 1)
                act.activation(arg[:], arg[:], ACT.Tanh).then_inc(s_th, 1)

            if routed:
                router(0)
            with act.Fori(0, B - 1) as i:
                hidden(0, i)
                if routed:
                    router(i + 1)
            hidden(0, B - 1)
            for n in range(1, len(passes)):
                with act.Fori(0, B) as i:
                    hidden(n, i)

        @block.tensor
        def _(pe):
            free_at_start(pe, s_out)
            def chunk(i, c):
                dd = DDL * i
                pe.wait_ge(s_xn, 2 * NT * (i + 1))
                pe.wait_ge(s_ddev, FREE + dd + c)
                for t in range(NT):
                    mm = pe.transpose(DD[0:KCH[c], t * 128:(t + 1) * 128], xn[:, t, c * 128:c * 128 + KCH[c]], ident[:])
                mm.then_inc(s_dd, 1)

            def gate(i):
                pe.wait_ge(s_g, i + 1)
                pe.wait_ge(s_ddev, FREE + DDL * i + NK)
                for c in range(NK):
                    mm = pe.matmul(DD[:, c * KC:(c + 1) * KC], gcol[:, c:c + 1].to_broadcast([KC, 128]),
                                   ident[0:KC, 0:KC], start=True, stop=True)
                mm.then_inc(s_dd, 1)

            def router(i):
                pe.wait_ge(s_wgs, 2)
                pe.wait_ge(s_ddev, FREE + DDL * i + NK + 1)
                pe.wait_ge(s_h, NK * (i + 1))
                for t in range(NT):
                    mm = dense(pe, DD[:, t * NE:(t + 1) * NE], hT, tokens(i, t, 128), wgs, slice(0, NE), False, None)
                mm.then_inc(s_dd, 1)

            def layernorm(i, step):
                if step < NK:
                    chunk(i, step)
                elif step == NK:
                    gate(i)
                elif routed and step == NK + 1:
                    router(i)

            def mlp(n, i, ahead=None):
                k = (n * B + i) * NF
                pe.wait_ge(s_h, NK * (i + 1) if n == 0 else NK * B)

                def out(f):
                    if isinstance(i, int) and i == 0 and n == 0 or not isinstance(i, int):
                        pe.wait_ge(s_w2, NF * n + f + 1)
                    pe.wait_ge(s_hs, FREE + k + f + 1)
                    if f == 0:
                        pe.wait_ge(s_ob, FREE + (n * B + i) * NT)
                    for t in range(NT):
                        for q, (a, w) in enumerate(SPLITS):
                            mm = pe.matmul(ob[t][:, 0:C], Hs[:, a, f % 3, t * 128:(t + 1) * 128], W2[n % 2][:, w, f, :],
                                           start=(f == 0 and q == 0), stop=(f == NF - 1 and q == 2))
                    mm.then_inc(s_out, 1)

                if n:
                    pe.wait_ge(s_w1, 2 * n)
                for f in range(NF):
                    pe.wait_ge(s_gelu, FREE + k + max(0, f - 2))
                    dense(pe, hb[f % 3][:], W1[n % 2], slice(f * 128, (f + 1) * 128), hT, tokens(i, 0, NTOK), True, s_hb)
                    if f >= 2:
                        out(f - 2)
                    if ahead is not None and f in PE_STEPS:
                        chunk(ahead, PE_STEPS.index(f))
                out(NF - 2)
                out(NF - 1)
                if ahead is not None:
                    gate(ahead)
                if ahead is not None and routed:
                    router(ahead)

            for step in range(NK + 2):
                layernorm(0, step)
            with pe.Fori(0, B - 1) as i:
                mlp(0, i, i + 1)
            mlp(0, B - 1)
            for n in range(1, len(passes)):
                with pe.Fori(0, B) as i:
                    mlp(n, i)

        @block.vector
        def _(dve):
            free_at_start(dve, s_hs, s_x, s_ddev)
            def layernorm(link, i, step):
                dd = DDL * i
                if step == 0:
                    for t in range(NT):
                        link(dve.bn_stats(st6[:, t, :], X[:, one(i * NT + t), :].squeeze(1)))
                    dve.sem_inc(s_go, 1)
                    for t in range(NT):
                        dve.bn_aggr(mv[:, t, :], st6[:, t, :]).then_inc(s_dve, 1)
                    link.pass_by(NT)
                    dve.wait_ge(s_dve, link.n)
                    dve.tensor_scalar_add(ve[:], mv[:, :, 1:2].squeeze(2), EPS).then_inc(s_var, 1)
                    dve.tensor_copy(gcol[:], T["gates"][:, l, 1, :, one(i)].squeeze(2)).then_inc(s_g, 1)
                elif step == 1:
                    dve.wait_ge(s_rstd, i + 1)
                    for t in range(NT):
                        normalized_rows(dve, xn[:, t, :], X[:, one(i * NT + t), :].squeeze(1), mv[:, t, 0:1],
                                        rstd[:, t:t + 1], s_xn)
                elif 2 <= step < 2 + NK:
                    c = step - 2
                    dve.wait_ge(s_dd, dd + c + 1)
                    rows = KCH[c]
                    dve.tensor_scalar(h32[0:rows], DD[0:rows, :], mods[0:rows, l, 3, c, one(i)], mods[0:rows, l, 2, c, one(i)],
                                      ALU.mult, ALU.add).then_inc(s_ddev, 1)
                    dve.wait_ge(s_ddev, FREE + dd + c + 1)
                    split_chunk(dve, link, hT, c, tokens(i, 0, NTOK), h32[0:rows, :]).then_inc(s_h, 1)
                    dve.wait_ge(s_h, NK * i + c + 1)
                elif step == 2 + NK:
                    dve.wait_ge(s_dd, dd + NK + 1)
                    dve.tensor_copy(gbc[:, one(i), :].squeeze(1), DD[:, 0:C]).then_inc(s_ddev, 1)
                elif routed and step == 3 + NK:
                    router(link, i, dd)

            def router(link, i, dd):
                dve.wait_ge(s_dd, dd + NK + 2)
                dve.tensor_scalar(lg[:], DD[:, 0:NT * NE].rearrange("p (t e) -> p t e", e=NE), 1.0 / WS, None,
                                  ALU.mult).then_inc(s_ddev, 1)
                dve.wait_ge(s_ddev, FREE + dd + NK + 2)
                for e in range(NE):
                    for lo, hi, op in ((0, e, ALU.is_ge), (e + 1, NE, ALU.is_gt)):
                        if lo < hi:
                            last = dve.tensor_tensor(cmp[:, :, e, lo:hi], lg[:, :, lo:hi],
                                                     lg[:, :, e:e + 1].to_broadcast([128, NT, hi - lo]), op)
                            link(last)
                link(dve.tensor_reduce(rank[:], cmp[:], AX_X, ALU.add))
                link(dve.tensor_scalar(sel[:], rank[:], 2.0, None, ALU.is_lt))
                link(dve.tensor_tensor(rank[:], lg[:], sel[:], ALU.mult))
                link(dve.tensor_reduce(tot[:], rank[:], AX_X, ALU.add))
                dve.scalar_tensor_tensor(arg[:], tot[:].unsqueeze(2).to_broadcast([128, NT, NE]), -0.5, lg[:], ALU.mult,
                                         ALU.add).then_inc(s_arg, 1)

            def expert_weights(link, i):
                dve.wait_ge(s_th, i + 1)
                link(dve.tensor_scalar(arg[:], arg[:], 0.5, 0.5, ALU.mult, ALU.add))
                dve.tensor_tensor(cw[:, tokens(i, 0, NT, NT), :], arg[:], sel[:], ALU.mult).then_inc(s_cw, 1)

            def update(link, n, i, t):
                xt, yt, g = X[:, one(i * NT + t), :].squeeze(1), y[:, t, :], gbc[:, one(i), :].squeeze(1)
                dve.wait_ge(s_ob, FREE + (n * B + i) * NT + t + 1)
                link(dve.tensor_tensor(yt, yt, b2[:, n, :], ALU.add))
                if routed:
                    link(dve.scalar_tensor_tensor(yt, yt, cw[:, one(i * NT + t), n:n + 1].squeeze(1), g, ALU.mult, ALU.mult))
                else:
                    link(dve.tensor_tensor(yt, yt, g, ALU.mult))
                dve.tensor_tensor(xt, xt, yt, ALU.add).then_inc(s_x, 1)

            def mlp(link, n, i, ahead=None, before=None):
                k = (n * B + i) * NF
                for f in range(NF):
                    if before is not None and f in UPDATES:
                        update(link, *before, UPDATES.index(f))
                    dve.wait_ge(s_gelu, FREE + k + f + 1)
                    dve.wait_ge(s_out, FREE + k + max(0, f - 2))
                    dve.tensor_tensor(Hs[:, 1, f % 3, :], g32[:, f % 2, :], Hs[:, 0, f % 3, :], ALU.subtract).then_inc(s_hs, 1)
                    if ahead is not None:
                        if f in DVE_STEPS:
                            layernorm(link, ahead, DVE_STEPS.index(f))
                if ahead is not None:
                    layernorm(link, ahead, 2 + NK)
                if ahead is not None and routed:
                    layernorm(link, ahead, 3 + NK)
                if ahead is not None and routed:
                    expert_weights(link, ahead)

            dve.wait_ge(s_small, 32 * len(passes) + (RAW_W1 if routed else 0))
            link = Order(dve, s_dve)
            if routed:
                dve.wait_ge(s_clr, 1)
                whole, low = wg[:, 0:2, :], wg[0:KCH[2], 2, :]
                for v in (whole, low):
                    link(dve.tensor_scalar(v, v, WS, None, ALU.mult))
                link(dve.tensor_copy(wgs[0][:, 0, :, :], whole))
                link(dve.tensor_copy(wgs[1][:], low))
                dve.tensor_tensor(wgs[0][:, 1, :, :], whole, wgs[0][:, 0, :, :], ALU.subtract).then_inc(s_wgs, 1)
                dve.tensor_tensor(wgs[1][LOW_W, :], low[LOW_W], wgs[1][LOW_W, :], ALU.subtract).then_inc(s_wgs, 1)
            for step in range(4 + NK):
                layernorm(link, 0, step)
            if routed:
                expert_weights(link, 0)
            mlp(link, 0, 0, 1)
            start, LN, MLP = link.n, 2 * NT + NK + (6 + 4 + 1 if routed else 0), 2 * NT
            with dve.Fori(1, B - 1) as i:
                mlp(Order(dve, s_dve, (i - 1) * (LN + MLP) + start), 0, i, i + 1, (0, i - 1))
            link = Order(dve, s_dve, start + (B - 2) * (LN + MLP))
            mlp(link, 0, B - 1, None, (0, B - 2))
            for n in range(1, len(passes)):
                mlp(link, n, 0, None, (n - 1, B - 1))
                start = link.n
                with dve.Fori(1, B) as i:
                    mlp(Order(dve, s_dve, (i - 1) * MLP + start), n, i, None, (n, i - 1))
                link = Order(dve, s_dve, start + (B - 1) * MLP)
            for t in range(NT):
                update(link, len(passes) - 1, B - 1, t)


def tokens(i, t, n, per=NTOK):
    at0 = i * per + t * 128
    return slice(at0, at0 + n) if isinstance(i, int) else bass.ds(at0, n)


def build(nc, io, out):
    with ExitStack() as ctx:
        def sb(name, shape, dt=F32):
            return ctx.enter_context(nc.sbuf_tensor(name, shape, dt))

        T = {
            "x": sb("x_tokens", [128, B * NT, C]),
            "ident": sb("identity", [128, 128]),
            "minus_half": sb("minus_half", [128, NT]),
            "mods": sb("mods", [128, NL, 4, 3, B]),
            "gates": sb("gates", [KC, NL, 2, NK, B]),
            "staging": sb("raw_weights", [128, NK * FF]),
            "w_att": (sb("w_att_parts", [128, 2, 2, 4 * C], F16), sb("w_att_rest", [KCH[2], 4 * C], F16)),
            "w1_parts": (sb("w1_parts", [128, 2, 2, FF], F16), sb("w1_rest", [KCH[2], FF], F16)),
            "s_raw": nc.alloc_semaphore("raw_weights_in"),
            "raw_count": 2 * RAW_W1,
            "mlp_of": [[0], [1, 2, 3, 4], [5]],
        }
        prepare_and_rotate(nc, io, T)
        for l in range(NL):
            attention_half(nc, io, T, l)
            mlp_half(nc, io, T, l)
        store(nc, T, out)


def store(nc, T, out):
    with ExitStack() as ctx:
        s_out = nc.alloc_semaphore("out_written")
        block = ctx.enter_context(nc.Block())

        @block.sync
        def _(sp):
            for b in range(B):
                sp.dma_start(out[b].rearrange("(t p) c -> p t c", p=128), T["x"][:, b * NT:(b + 1) * NT, :]).then_inc(s_out, 16)
            sp.wait_ge(s_out, 16 * B)


def layouts(inputs):
    import numpy as np

    a = {k: np.asarray(v) for k, v in inputs.items()}
    L = {1: "L1_cond_", 2: "L2_cond_", 3: "L3_cond_"}
    ada_w = [a["L1_cond_W_ada"], a["L2_cond_w_adaln"], a["L3_cond_ada_w"]]
    ada_b = [a["L1_cond_b_ada"], a["L2_cond_b_adaln"], a["L3_cond_ada_b"]]
    per_layer = {
        "qkv_w": [a["L1_cond_W_qkv"], a["L2_cond_w_qkv"], a["L3_cond_qkv_w"]],
        "qkv_b": [a["L1_cond_b_qkv"], a["L2_cond_b_qkv"], a["L3_cond_qkv_b"]],
        "proj_w": [a["L1_cond_W_proj"], a["L2_cond_w_proj"], a["L3_cond_out_w"]],
        "proj_b": [a["L1_cond_b_proj"], a["L2_cond_b_proj"], a["L3_cond_out_b"]],
    }
    put = {"x": a["x"], "P": a["L0_cond_P"], "skewT": a["L0_cond_W"].T, "skew_b": a["L0_cond_b"],
           "condT": a["cond_1152"].T.reshape(NK, KC, B).transpose(1, 0, 2), "gate_w": a["L2_cond_w_gate"]}
    for l in range(NL):
        put[f"ada_w{l}"], put[f"ada_b{l}"] = ada_w[l], ada_b[l]
        for k, v in per_layer.items():
            put[f"{k}{l}"] = v[l]
        qk = np.pad(per_layer["qkv_b"][l][:2 * C].reshape(2, H, D), ((0, 0), (0, 2), (0, 0)))
        put[f"qk_b{l}"] = qk.reshape(2, 6, NK, D).transpose(1, 3, 0, 2).reshape(6 * D, 2, NK)
    mlp = [("L1_cond_W_fc1", "L1_cond_b_fc1", "L1_cond_W_fc2", "L1_cond_b_fc2", None)]
    mlp += [("L2_cond_w1", "L2_cond_b1", "L2_cond_w2", "L2_cond_b2", e) for e in range(NE)]
    mlp += [("L3_cond_w1", "L3_cond_b1", "L3_cond_w2", "L3_cond_b2", None)]
    for m, (w1, b1, w2, b2, e) in enumerate(mlp):
        get = lambda n: a[n] if e is None else a[n][e]
        put[f"w1_{m}"], put[f"w2_{m}"], put[f"b2_{m}"] = get(w1), get(w2), get(b2)
        put[f"b1_{m}"] = get(b1).reshape(NF, 128).T
    return {k: np.ascontiguousarray(v) for k, v in put.items()}


def kernel(**inputs):
    import concourse.bacc as bacc
    from concourse.bass_utils import run_bass_kernel_spmd as run

    nc = bacc.Bacc("TRN2", target_bir_lowering=False, num_devices=1)
    arrays = layouts(inputs)
    io = {k: nc.dram_tensor(f"in_{k}", v.shape, mybir.dt.from_np(v.dtype), kind="ExternalInput").ap()
          for k, v in arrays.items()}
    out = nc.dram_tensor("out_x", (B, NTOK, C), F32, kind="ExternalOutput").ap()
    build(nc, io, out)
    r = run(nc, [{f"in_{k}": v for k, v in arrays.items()}], core_ids=[0])
    return r.results[0]["out_x"]
```
